# Optimizing a Trainium2 kernel written in Bass

```python
import numpy as np
import jax
import jax.numpy as jnp

def _softmax(x, axis=-1):
    return jax.nn.softmax(x, axis=axis)

def _gelu(x):
    return jax.nn.gelu(x, approximate=True)

def _silu(x):
    return jax.nn.silu(x)

def _sigmoid(x):
    return jax.nn.sigmoid(x)

def _layernorm(x, axis=-1, eps=1e-05):
    m = jnp.mean(x, axis=axis, keepdims=True)
    v = jnp.var(x, axis=axis, keepdims=True)
    return (x - m) / jnp.sqrt(v + eps)

def _scatter_add(tgt, idx, src, axis=0):
    return tgt.at[idx].add(src)

def _segment_sum(src, seg, n):
    return jax.ops.segment_sum(src, seg, n)
kernel_name = 'mk_adj_resnorm_d2_adj_r2_a75b9e'

def setup_inputs(seed: int=0):
    np.random.seed(seed)
    _w = jnp.asarray

    def _rec_inputs():
        import jax
        import jax.numpy as jnp
        _gk = jax.random.key(seed)
        x = -0.0002928 + 1 * jax.random.normal(jax.random.fold_in(_gk, 1), (2048, 512), jnp.float32)
        _w = (1.0 + jnp.arange(2048, dtype=jnp.float32)) ** (-0.5)
        _w = _w / _w.mean()
        _pij = jnp.clip(0.0078125 * _w[:, None] * _w[None, :], 0.0, 1.0)
        _a = jax.random.uniform(jax.random.fold_in(_gk, 2), (2048, 2048)) < _pij
        _a = jnp.logical_or(_a, jnp.eye(2048, dtype=bool))
        _af = _a.astype(jnp.float32)
        adj = _af
        return (x, adj)
    x, adj = _rec_inputs()

    def _L0_gnn_setup():
        import jax, jax.numpy as jnp
        import numpy as np
        ALPHA = 0.2
        NEG = -9000000000000000.0
        N, NFEAT, NHID, NHEADS = (2048, 512, 64, 8)
        EMB = NHID * NHEADS
        key = jax.random.key(seed)
        ks = jax.random.split(key, 16)
        x = jax.random.normal(ks[0], (N, NFEAT), dtype=jnp.float32)
        adj = (jax.random.uniform(ks[1], (N, N)) < 0.01).astype(jnp.float32)
        adj = jnp.maximum(adj, jnp.eye(N, dtype=jnp.float32))
        s = 0.05
        W = jax.random.normal(ks[2], (NHEADS, NFEAT, NHID), dtype=jnp.float32) * s
        a1 = jax.random.normal(ks[3], (NHEADS, NHID), dtype=jnp.float32) * s
        a2 = jax.random.normal(ks[4], (NHEADS, NHID), dtype=jnp.float32) * s
        W1 = jax.random.normal(ks[5], (EMB // 2, EMB), dtype=jnp.float32) * s
        b1 = jnp.zeros((EMB // 2,), dtype=jnp.float32)
        W2 = jax.random.normal(ks[6], (NFEAT // 4, EMB // 2), dtype=jnp.float32) * s
        b2 = jnp.zeros((NFEAT // 4,), dtype=jnp.float32)
        W3 = jax.random.normal(ks[7], (NFEAT // 2, NFEAT // 4), dtype=jnp.float32) * s
        b3 = jnp.zeros((NFEAT // 2,), dtype=jnp.float32)
        W4 = jax.random.normal(ks[8], (NFEAT, NFEAT // 2), dtype=jnp.float32) * s
        b4 = jnp.zeros((NFEAT,), dtype=jnp.float32)
        return {'x': x, 'adj': adj, 'W': W, 'a1': a1, 'a2': a2, 'W1': W1, 'b1': b1, 'W2': W2, 'b2': b2, 'W3': W3, 'b3': b3, 'W4': W4, 'b4': b4}
    _L0_gnn_all = _L0_gnn_setup()
    _L0_gnn_in = {k: v for k, v in _L0_gnn_all.items() if k in ('W', 'a1', 'a2', 'W1', 'b1', 'W2', 'b2', 'W3', 'b3', 'W4', 'b4')}
    del _L0_gnn_all

    def _L1_gnn_setup():
        import jax, jax.numpy as jnp
        import numpy as np
        N, H, E, HEADS = (1500, 512, 10000, 8)
        DK = H // HEADS
        key = jax.random.key(seed)
        k1, k2, k3, k4 = jax.random.split(key, 4)
        inst_feature = jax.random.normal(k1, (N, H), dtype=jnp.float32)
        rel_pair_index = jax.random.randint(k2, (E, 2), 0, N, dtype=jnp.int64)
        agg = jnp.zeros((N, N), dtype=jnp.float32)
        agg = agg.at[rel_pair_index[:, 0], rel_pair_index[:, 1]].set(1.0)
        agg = agg.at[jnp.arange(N), jnp.arange(N)].set(1.0)
        std = float(np.sqrt(2.0 / (H + DK)))
        Wq = jax.random.normal(k3, (H, H), dtype=jnp.float32) * std
        Wk = jax.random.normal(k4, (H, H), dtype=jnp.float32) * std
        bq = jnp.zeros((H,), dtype=jnp.float32)
        bk = jnp.zeros((H,), dtype=jnp.float32)
        return {'inst_feature': inst_feature, 'aggregator_matrix': agg, 'rel_pair_index': rel_pair_index, 'Wq': Wq, 'bq': bq, 'Wk': Wk, 'bk': bk}
    _L1_gnn_all = _L1_gnn_setup()
    _L1_gnn_in = {k: v for k, v in _L1_gnn_all.items() if k in ('rel_pair_index', 'Wq', 'bq', 'Wk', 'bk')}
    del _L1_gnn_all
    return {'x': x, 'adj': adj, 'L0_gnn_W': _L0_gnn_in['W'], 'L0_gnn_a1': _L0_gnn_in['a1'], 'L0_gnn_a2': _L0_gnn_in['a2'], 'L0_gnn_W1': _L0_gnn_in['W1'], 'L0_gnn_b1': _L0_gnn_in['b1'], 'L0_gnn_W2': _L0_gnn_in['W2'], 'L0_gnn_b2': _L0_gnn_in['b2'], 'L0_gnn_W3': _L0_gnn_in['W3'], 'L0_gnn_b3': _L0_gnn_in['b3'], 'L0_gnn_W4': _L0_gnn_in['W4'], 'L0_gnn_b4': _L0_gnn_in['b4'], 'L1_gnn_rel_pair_index': _L1_gnn_in['rel_pair_index'], 'L1_gnn_Wq': _L1_gnn_in['Wq'], 'L1_gnn_bq': _L1_gnn_in['bq'], 'L1_gnn_Wk': _L1_gnn_in['Wk'], 'L1_gnn_bk': _L1_gnn_in['bk']}

def reference(x, adj, L0_gnn_W, L0_gnn_a1, L0_gnn_a2, L0_gnn_W1, L0_gnn_b1, L0_gnn_W2, L0_gnn_b2, L0_gnn_W3, L0_gnn_b3, L0_gnn_W4, L0_gnn_b4, L1_gnn_rel_pair_index, L1_gnn_Wq, L1_gnn_bq, L1_gnn_Wk, L1_gnn_bk):
    import jax
    import jax.numpy as jnp

    def _L0_gnn_ref(x, adj, W, a1, a2, W1, b1, W2, b2, W3, b3, W4, b4):
        import jax, jax.numpy as jnp
        import numpy as np
        ALPHA = 0.2
        NEG = -9000000000000000.0
        N, NFEAT, NHID, NHEADS = (2048, 512, 64, 8)
        EMB = NHID * NHEADS
        Wh = jnp.einsum('nf,hfd->hnd', x, W)
        e_src = jnp.einsum('hnd,hd->hn', Wh, a1)
        e_dst = jnp.einsum('hnd,hd->hn', Wh, a2)
        e = jax.nn.leaky_relu(e_src[:, :, None] + e_dst[:, None, :], ALPHA)
        e = jnp.where(adj[None] > 0, e, NEG)
        att = jax.nn.softmax(e, axis=-1)
        h = jnp.einsum('hnm,hmd->hnd', att, Wh)
        h = jax.nn.elu(h)
        enc = jnp.transpose(h, (1, 0, 2)).reshape(x.shape[0], -1)
        out = jax.nn.relu(enc @ W1.T + b1)
        out = jax.nn.relu(out @ W2.T + b2)
        out = jax.nn.relu(out @ W3.T + b3)
        out = out @ W4.T + b4
        return out

    def _L1_gnn_ref(inst_feature, aggregator_matrix, rel_pair_index, Wq, bq, Wk, bk):
        import jax, jax.numpy as jnp
        import numpy as np
        N, H, E, HEADS = (1500, 512, 10000, 8)
        DK = H // HEADS
        n = inst_feature.shape[0]
        sub = rel_pair_index[:, 0]
        obj = rel_pair_index[:, 1]
        q = (inst_feature[sub] @ Wq.T + bq).reshape(-1, HEADS, DK)
        k = (inst_feature[obj] @ Wk.T + bk).reshape(-1, HEADS, DK)
        att = ((q * k).sum(-1) / np.sqrt(DK)).T.astype(inst_feature.dtype)
        scores = jnp.zeros((HEADS, n, n), dtype=inst_feature.dtype)
        scores = scores.at[:, sub, obj].set(att)
        mask = (1.0 - aggregator_matrix).astype(bool)
        scores = jnp.where(mask[None], -jnp.inf, scores)
        di = jnp.arange(n)
        scores = scores.at[:, di, di].set(1e-07)
        attn = jax.nn.softmax(scores, axis=2)
        aggregator_factor = attn.sum(axis=0) / HEADS
        return aggregator_factor @ inst_feature
    x = _layernorm(x + _L0_gnn_ref(x, adj, L0_gnn_W, L0_gnn_a1, L0_gnn_a2, L0_gnn_W1, L0_gnn_b1, L0_gnn_W2, L0_gnn_b2, L0_gnn_W3, L0_gnn_b3, L0_gnn_W4, L0_gnn_b4), axis=-1)
    x = _layernorm(x + _L1_gnn_ref(x, adj, L1_gnn_rel_pair_index, L1_gnn_Wq, L1_gnn_bq, L1_gnn_Wk, L1_gnn_bk), axis=-1)
    return x

_drawn_inputs = setup_inputs


def setup_inputs(seed=0):
    import zlib

    import numpy as np

    out = dict(_drawn_inputs(seed))
    spreads = {'L0_gnn_b1': (0.0, 0.408),
     'L0_gnn_b2': (0.0, 0.1),
     'L0_gnn_b3': (0.0, 0.1),
     'L0_gnn_b4': (0.0, 0.1),
     'L1_gnn_bq': (0.0, 2.0),
     'L1_gnn_bk': (0.0, 2.0)}
    factors = {'L0_gnn_a1': 23.299, 'L0_gnn_a2': 4.097, 'L1_gnn_Wq': 4.556, 'L1_gnn_Wk': 4.393}
    for name, (base, spread) in spreads.items():
        noise = np.random.default_rng([zlib.crc32(name.encode()), seed]).standard_normal(out[name].shape)
        drawn = base * np.exp(spread * noise) if base else spread * noise
        out[name] = jnp.asarray(drawn.astype(out[name].dtype))
    for name, factor in factors.items():
        out[name] = (out[name] * factor).astype(out[name].dtype)
    return out
```

```python
import concourse.bass as bass
from concourse import mybir
from contextlib import ExitStack

F32 = mybir.dt.float32
BF16 = mybir.dt.bfloat16
I32 = mybir.dt.int32
ALU = mybir.AluOpType
ACT = mybir.ActivationFunctionType
AX = mybir.AxisListType

P = 128
N, F, H, DH = 2048, 512, 8, 64
NT = N // P
KT = F // P
BLK = 512
NB = N // BLK
TI = BLK // P
DA = DH + 1
E1, E2, E3 = 256, 128, 256
EDGES = 10000
ET = 80
EP = EDGES // ET
TRASH = N * N
CH = 8
SPAN = 78.0
LOW = -44.0
EPS = 1e-5
DIAG = 1e-7
NP_BUF = 4
RING = 8


def build(nc, a):
    ds = bass.ds
    with ExitStack() as ctx:
        def sb(name, shape, dt=F32):
            return ctx.enter_context(nc.sbuf_tensor(name, shape, dt))

        def sem(name):
            return ctx.enter_context(nc.semaphore(name))

        def dram(name, shape, dt=F32):
            return nc.dram_tensor(name, shape, dt).ap()

        r_dram = dram("r_dram", (NB * H, BLK))
        f_dram = dram("f_dram", (ET, P))
        q_dram = dram("q_dram", (N, F))
        k_dram = dram("k_dram", (N, F))
        c_dram = dram("c_dram", (NT, P))
        t_dram = dram("t_dram", (N * N + P * ET, 1), I32)
        d_dram = dram("d_dram", (N * N + P * ET, 1))

        adjT = sb("adjT", [P, NT, N], BF16)
        xs = sb("xs", [P, NT, F])
        U = sb("U", [P, NT, H, DA])
        WT = sb("WT", [P, 52, P])
        arena = sb("arena", [P, 10372])
        q_col = sb("q_col", [P, NT, H])
        bqk = sb("bqk", [P, 2, F])
        bqk_f = bqk[:, :, :].rearrange("p w n -> p (w n)")
        tri = bqk_f[:, 0:128]
        junk0 = bqk_f[:, 128:256]
        e_col = bqk_f[:, 256:512].rearrange("p (t h) -> p t h", t=NT)
        Wa = bqk_f[:, 512:576].rearrange("p (k h) -> p k h", k=KT)
        bcol = sb("bcol", [P, 5])
        zero = sb("zero", [P, 144])
        ident = sb("ident", [P, P])
        identb = sb("identb", [P, P], BF16)
        biota = sb("biota", [P, P])
        ones = sb("ones", [8, P])
        cst = sb("cst", [P, 4])
        adj_sum = sb("adj_sum", [P, NT])
        adj_diag = sb("adj_diag", [P, NT])
        pairs = sb("pairs", [P, 2 * ET], I32)
        eid = sb("eid", [P, ET], I32)
        sub_i = sb("sub_i", [P, ET], I32)
        obj_i = sb("obj_i", [P, ET], I32)
        fn_i = sb("fn_i", [P, ET], I32)
        tidx = sb("tidx", [P, ET], I32)
        didx = sb("didx", [P, ET], I32)
        t_got = sb("t_got", [P, ET], I32)
        ef = sb("ef", [P, 8, ET])
        sub_f, obj_f, fn_f, ft_f, trash_f, ok_f, live, adj_got = (ef[:, k, :] for k in range(8))
        stats = sb("stats", [P, TI, 6])
        var = sb("var", [P, TI, 2])
        rstd = sb("rstd", [P, TI])
        carrier = sb("carrier", [P, 1])

        adj_raw = [arena[:, 2048 * u:2048 * u + 2048] for u in range(2)]
        adj_b = [arena[:, 4096 + 1024 * u:5120 + 1024 * u].bitcast(BF16) for u in range(2)]
        x_in = [arena[:, 6144 + 512 * u:6656 + 512 * u] for u in range(2)]
        xT = [arena[:, 7168 + 512 * u:7680 + 512 * u] for u in range(2)]
        W_in = arena[:, 8192:10240].rearrange("p (k n) -> p k n", k=KT)
        s_row = arena[0:H, 6144:8192]
        d_row = arena[0:H, 8192:10240]
        d_lim = sb("d_lim", [H, 4])
        d_diag = sb("d_diag", [H, H])
        b4_in = adjT[:, 15, 0:1024].bitcast(F32)
        f_row = arena[0:ET, 10240:10368]
        pair_rows = adjT[:, 0:10, :].rearrange("p a n -> p (a n)").bitcast(F32)
        raw = U[:, :, :, :].rearrange("p j h d -> p (j h d)")
        w_raw = raw[:, 0:6656]
        W1r = w_raw[:, 0:1024].rearrange("p (o n) -> p o n", o=2)
        W2r = w_raw[:, 1024:1280]
        W3r = w_raw[:, 1280:1536].rearrange("p (o n) -> p o n", o=2)
        W4r = w_raw[:, 1536:2560].rearrange("p (o n) -> p o n", o=4)
        Wqr = w_raw[:, 2560:4608].rearrange("p (o n) -> p o n", o=4)
        Wkr = w_raw[:, 4608:6656].rearrange("p (o n) -> p o n", o=4)
        a_in = [raw[:, 6656 + 512 * u:7168 + 512 * u] for u in range(2)]
        wa_tmp = raw[:, 7680:8192]
        chunks = ([(W1r[:, o, k * P:(k + 1) * P]) for k in range(4) for o in range(2)]
                  + [W2r[:, k * P:(k + 1) * P] for k in range(2)]
                  + [W3r[:, o, :] for o in range(2)]
                  + [W4r[:, o, k * P:(k + 1) * P] for k in range(2) for o in range(4)]
                  + [Wqr[:, o, k * P:(k + 1) * P] for k in range(4) for o in range(4)]
                  + [Wkr[:, o, k * P:(k + 1) * P] for k in range(4) for o in range(4)])
        W1T = [WT[:, 2 * k:2 * k + 2, :].rearrange("p o n -> p (o n)") for k in range(4)]
        W2T = [WT[:, 8 + k, :] for k in range(2)]
        W3T = WT[:, 10:12, :].rearrange("p o n -> p (o n)")
        W4T = [WT[:, 12 + 4 * k:16 + 4 * k, :].rearrange("p o n -> p (o n)") for k in range(2)]
        WqT = [WT[:, 20 + 4 * k:24 + 4 * k, :].rearrange("p o n -> p (o n)") for k in range(4)]
        WkT = [WT[:, 36 + 4 * k:40 + 4 * k, :].rearrange("p o n -> p (o n)") for k in range(4)]

        att_raw = arena[:, 0:2080].rearrange("p (h t d) -> p h t d", h=H, t=TI)
        enc = arena[:, 2080:4128].rearrange("p (t n) -> p t n", t=TI)
        encT = enc
        ebuf = arena[:, 4128:5152].rearrange("p (t n) -> p t n", t=2)
        z1T = ebuf
        z3T = ebuf
        x1T = [arena[:, 5152 + 512 * u:5664 + 512 * u] for u in range(2)]
        z2T = x1T[0]
        qk_out = [arena[:, 6176 + 512 * u:6688 + 512 * u] for u in range(2)]
        Pw = [arena[:, 7200 + 512 * u:7712 + 512 * u] for u in range(NP_BUF)]
        r_b = [arena[:, 9248 + 512 * u:9760 + 512 * u] for u in range(2)]
        y = [arena[:, 512 * t:512 * t + 512] for t in range(TI)]
        rden = sb("rden", [P, H, TI])

        k_rows = [raw[:, 512 * u:512 * u + 512] for u in range(RING)]
        q_rows = [raw[:, 4096 + 512 * u:4608 + 512 * u] for u in range(RING)]
        att = arena[:, 0:640].rearrange("p (t h) -> p t h", h=H)
        att_f = arena[:, 0:640]
        e1 = arena[:, 640:1280]
        m_e = arena[:, 1280:1920]
        p9 = arena[:, 1920:2640].rearrange("p (t h) -> p t h", h=9)
        Oa = arena[:, 2640:3920].rearrange("p (t k) -> p t k", k=NT)
        a_f = arena[:, 3920:4000]
        b_f = arena[:, 4000:4080]
        v_e = arena[:, 4080:4160]
        prod = [arena[:, 4160 + 512 * u:4672 + 512 * u] for u in range(2)]
        Ob = [arena[:, 4160 + 1024 * u:5184 + 1024 * u].rearrange("p (t b) -> p t b", t=CH) for u in range(2)]
        Wc = [arena[:, 6208 + 1152 * u:7360 + 1152 * u] for u in range(2)]
        m_tmp = arena[:, 8512:9024]
        v_part = arena[:, 9168:9176]
        ObT = WT[:, 0:40, :].rearrange("p t n -> p (t n)").bitcast(BF16).rearrange("p (t e) -> p t e", t=ET)
        tab = WT[:, 40:52, :].rearrange("p t n -> p (t n)")
        m_b = tab[:, 0:64].bitcast(BF16)
        base = tab[:, 64:192]
        dterm = tab[:, 192:320]
        seg = tab[:, 320:464].rearrange("p (t h) -> p t h", h=9)
        Z = tab[:, 464:592]
        T9 = tab[:, 592:736].rearrange("p (t h) -> p t h", h=9)
        T9f = tab[:, 592:736]
        Tb = [tab[:, 736 + 72 * u:808 + 72 * u].bitcast(BF16) for u in range(3)]
        c_col = tab[:, 952:968]
        cd_col = tab[:, 968:984]
        n_col = tab[:, 984:1000]
        dcoef = tab[:, 1000:1016]
        c_row = tab[0:NT, 1016:1144]
        glob = tab[:, 1144:1156]
        T_tmp = tab[:, 1156:1300]
        d_in = [raw[:, 512 * u:512 * u + 512] for u in range(4)]
        A = [raw[:, 2048 + 512 * u:2560 + 512 * u] for u in range(4)]
        c_b = raw[:, 4096:6144]
        o_buf = [raw[:, 6144 + 512 * u:6656 + 512 * u] for u in range(TI)]

        ps = ctx.enter_context(nc.psum_tensor("ps", [P, 8, 512], F32))
        psb = ps[:, :, :].rearrange("p b n -> p (b n)").bitcast(BF16).rearrange("p (b n) -> p b n", b=8)

        consts = sem("consts")
        pairs_in = sem("pairs_in")
        w_in = sem("w_in")
        wh_in = sem("wh_in")
        small_in = sem("small_in")
        b4_in_s = sem("b4_in_s")
        bqk_in = sem("bqk_in")
        x_res_in = sem("x_res_in")
        dve_own = sem("dve_own")
        fn_ready = sem("fn_ready")
        fn_ps = sem("fn_ps")
        f_row_ready = sem("f_row_ready")
        f_out = sem("f_out")
        f_in = sem("f_in")
        idx_ready = sem("idx_ready")
        wa_ready = sem("wa_ready")
        wt_ps = sem("wt_ps")
        wt_sb = sem("wt_sb")
        x_in_s = [sem(f"x_in_s{u}") for u in range(2)]
        xT_ps = sem("xT_ps")
        xT_sb = sem("xT_sb")
        wh_ps = sem("wh_ps")
        wh_sb = sem("wh_sb")
        e_sb = sem("e_sb")
        rows_ps = sem("rows_ps")
        rows_sb = sem("rows_sb")
        d_ready = sem("d_ready")
        d_ps = sem("d_ps")
        shift_ready = sem("shift_ready")
        r_arg = sem("r_arg")
        r_ready = sem("r_ready")
        ed_ready = sem("ed_ready")
        u_ready = sem("u_ready")
        adj_in = [sem(f"adj_in{u}") for u in range(2)]
        adj_cast = sem("adj_cast")
        dve_loop = sem("dve_loop")
        adj_dg = sem("adj_dg")
        adj_ps = sem("adj_ps")
        adj_sb = sem("adj_sb")
        r_out = sem("r_out")
        r_in = [sem(f"r_in{u}") for u in range(2)]
        P_ready = sem("P_ready")
        P_free = sem("P_free")
        att_ev = sem("att_ev")
        rden_ready = sem("rden_ready")
        hn_ready = sem("hn_ready")
        min_ready = sem("min_ready")
        exp_ready = sem("exp_ready")
        enc_ready = sem("enc_ready")
        encT_ps = sem("encT_ps")
        encT_a = sem("encT_a")
        encT_d = sem("encT_d")
        z1_ps, z1_sb = sem("z1_ps"), sem("z1_sb")
        z2_ps, z2_sb = sem("z2_ps"), sem("z2_sb")
        z3_ps, z3_sb = sem("z3_ps"), sem("z3_sb")
        z4_ps = sem("z4_ps")
        y_ready = sem("y_ready")
        st_ready = sem("st_ready")
        var_ready = sem("var_ready")
        ln_ready = sem("ln_ready")
        rstd_ready = sem("rstd_ready")
        x1_ready = sem("x1_ready")
        x1_kept = sem("x1_kept")
        x1T_ps, x1T_sb = sem("x1T_ps"), sem("x1T_sb")
        qk_ps = sem("qk_ps")
        qk_sb = sem("qk_sb")
        qk_dma = [sem(f"qk_dma{w}") for w in range(2)]
        t_out = sem("t_out")
        t_in = sem("t_in")
        aj_in = sem("aj_in")
        zeroed = sem("zeroed")
        k_in = [sem(f"k_in{u}") for u in range(RING)]
        q_in = [sem(f"q_in{u}") for u in range(RING)]
        prod_ready = sem("prod_ready")
        rows_used = sem("rows_used")
        didx_ready = sem("didx_ready")
        gm_ready, gm_ps, g1_ready, g_all = sem("gm_ready"), sem("gm_ps"), sem("g1_ready"), sem("g_all")
        beta_ready, e1_ready = sem("beta_ready"), sem("e1_ready")
        oh_ready = sem("oh_ready")
        oh_used = sem("oh_used")
        obT_sb = sem("obT_sb")
        lse_arg, lse_ready = sem("lse_arg"), sem("lse_ready")
        m_ready = sem("m_ready")
        tabs_ready = sem("tabs_ready")
        mg_ps, mg_sb = sem("mg_ps"), sem("mg_sb")
        p_arg, p_exp, p_ready = sem("p_arg"), sem("p_exp"), sem("p_ready")
        c_ready, c_ps, c_row_ready = sem("c_ready"), sem("c_ps"), sem("c_row_ready")
        c_out, c_in = sem("c_out"), sem("c_in")
        t9_ready = sem("t9_ready")
        w_ready = sem("w_ready")
        g9_ps = sem("g9_ps")
        v_sum = sem("v_sum")
        v_ready = sem("v_ready")
        d_out = sem("d_out")
        d_slot = [sem(f"d_slot{u}") for u in range(4)]
        A_tmp = sem("A_tmp")
        A_ready = sem("A_ready")
        A_free = sem("A_free")
        o_ev = sem("o_ev")
        o_st, o_var, o_ln, o_rstd, o_norm = sem("o_st"), sem("o_var"), sem("o_ln"), sem("o_rstd"), sem("o_norm")
        out_dma = [sem(f"out_dma{t}") for t in range(TI)]

        credits = ([(s, 2) for s in (wt_sb, xT_sb, wh_ps, wh_sb, e_sb, att_ev, enc_ready, oh_used, obT_sb,
                                     mg_sb, v_ready)]
                   + [(adj_sb, 3), (adj_dg, 1), (P_free, NP_BUF), (A_ready, 4), (A_free, 4), (o_ev, 8)]
                   + [(s, 16) for s in qk_dma + out_dma])
        CHUNKS = ET // CH

        block = ctx.enter_context(nc.Block())

        @block.sync
        def _(sp):
            sp.wait_ge(consts, 1)
            sp.dma_start(pairs[0:EP, :], a["pairs"].rearrange("(p t) c -> p (t c)", t=ET)).then_inc(pairs_in, 16)
            for k in range(KT):
                sp.dma_start(W_in[:, k, :].rearrange("p (h d) -> p h d", h=H),
                             a["W"][:, k * P:(k + 1) * P, :].rearrange("h p d -> p h d")).then_inc(wh_in, 16)
            for u, name in enumerate(("a1", "a2")):
                sp.dma_start(a_in[u], a[name].rearrange("h d -> (h d)").partition_broadcast(P)).then_inc(wh_in, 16)
            sp.dma_start(W1r, a["W1"].rearrange("(o p) n -> p o n", p=P)).then_inc(w_in, 16)
            sp.dma_start(W2r, a["W2"]).then_inc(w_in, 16)
            sp.dma_start(W3r, a["W3"].rearrange("(o p) n -> p o n", p=P)).then_inc(w_in, 16)
            sp.dma_start(W4r, a["W4"].rearrange("(o p) n -> p o n", p=P)).then_inc(w_in, 16)
            sp.dma_start(Wqr, a["Wq"].rearrange("(o p) n -> p o n", p=P)).then_inc(w_in, 16)
            sp.dma_start(Wkr, a["Wk"].rearrange("(o p) n -> p o n", p=P)).then_inc(w_in, 16)
            for u in range(2):
                sp.dma_start(x_in[u], a["x"][u * P:(u + 1) * P, :]).then_inc(x_in_s[u], 16)
            for c, name, n in ((0, "b1", 2), (2, "b2", 1), (3, "b3", 2)):
                for o in range(n):
                    sp.dma_start(bcol[:, c + o:c + o + 1],
                                 a[name][o * P:(o + 1) * P].unsqueeze(1)).then_inc(small_in, 16)
            sp.dma_start(b4_in, a["b4"].partition_broadcast(P)).then_inc(b4_in_s, 16)
            for u in range(2):
                sp.dma_start(adj_raw[u], a["adj"][u * P:(u + 1) * P, :]).then_inc(adj_in[u], 16)
            sp.wait_ge(f_row_ready, 1)
            sp.dma_start(f_dram, f_row).then_inc(f_out, 16)
            sp.wait_ge(f_out, 16)
            sp.dma_start(pair_rows, f_dram.rearrange("t e -> (t e)").partition_broadcast(P)).then_inc(f_in, 16)
            with sp.Fori(1, (NT) // 2) as i_:
                i = i_ * 2
                for u in range(2):
                    sp.wait_ge(xT_ps, i + (u - 1))
                    sp.dma_start(x_in[u], a["x"][ds((i + u) * P, P), :]).then_inc(x_in_s[u], 16)
            sp.dma_start(xs[:, :, :], a["x"].rearrange("(t p) n -> p t n", p=P)).then_inc(x_res_in, 16)
            with sp.Fori(1, (NT) // 2) as i_:
                i = i_ * 2
                for u in range(2):
                    sp.wait_ge(adj_cast, i + (u - 1))
                    sp.dma_start(adj_raw[u], a["adj"][ds((i + u) * P, P), :]).then_inc(adj_in[u], 16)
            sp.wait_ge(r_ready, 1)
            sp.dma_start(r_dram.rearrange("(b h) n -> h b n", h=H),
                         s_row.rearrange("p (b n) -> p b n", b=NB)).then_inc(r_out, 16)
            sp.wait_ge(r_out, 16)
            sp.wait_ge(u_ready, NT)
            sp.wait_ge(adj_ps, 2 * NT)
            for w, name in enumerate(("bq", "bk")):
                sp.dma_start(bqk[:, w, :], a[name].partition_broadcast(P)).then_inc(bqk_in, 16)
            for u in range(2):
                sp.dma_start(r_b[u], r_dram[u, :].partition_broadcast(P)).then_inc(r_in[u], 16)
            for k in range(4):
                sp.dma_start(d_dram[(60 + k) * P * BLK:(61 + k) * P * BLK, :].rearrange("(p m n) o -> p m (n o)", m=4, n=P),
                             zero[:, 0:P].unsqueeze(1).broadcast_to([P, 4, P])).then_inc(zeroed, 16)
            with sp.Fori(0, (NB * H - 2) // 2) as g_:
                g = g_ * 2
                for u in range(2):
                    sp.wait_ge(P_ready, (g + (u + 1)) * NT)
                    sp.dma_start(r_b[u], r_dram[ds(g + (u + 2), 1), :].rearrange("o n -> (o n)").partition_broadcast(P)
                                 ).then_inc(r_in[u], 16)
                for k in range(4):
                    sp.dma_start(d_dram[ds((g * 2 + k) * (P * BLK), P * BLK), :].rearrange("(p m n) o -> p m (n o)", m=4, n=P),
                                 zero[:, 0:P].unsqueeze(1).broadcast_to([P, 4, P])).then_inc(zeroed, 16)
            sp.wait_ge(c_row_ready, 1)
            sp.dma_start(c_dram, c_row).then_inc(c_out, 16)
            sp.wait_ge(c_out, 16)
            sp.dma_start(c_b, c_dram.rearrange("t p -> (t p)").partition_broadcast(P)).then_inc(c_in, 16)
            sp.wait_ge(d_out, 16 * ET)
            dj = d_dram[0:N * N, :].rearrange("(j i) o -> j (i o)", i=N)
            with sp.Fori(0, NB) as b:
                with sp.Fori(0, NT // 4) as jq:
                    for u in range(4):
                        sp.wait_ge(A_ready, b * NT + jq * 4 + (u + 1))
                        sp.dma_start(d_in[u], dj[ds((jq * 4 + u) * P, P), ds(b * BLK, BLK)]).then_inc(d_slot[u], 16)
            for w in range(2):
                sp.wait_ge(qk_dma[w], 16 * (NT + 1))
            for t in range(TI):
                sp.wait_ge(out_dma[t], 16 * (NB + 1))

        @block.gpsimd
        def _(pool):
            nc.gpsimd.memset(pairs[:, :], 0).then_inc(consts, 1)
            nc.gpsimd.memset(zero[:, :], 0.0).then_inc(consts, 1)
            nc.gpsimd.memset(ones[:, :], 1.0).then_inc(consts, 1)
            nc.gpsimd.memset(cst[:, 0:1], EPS).then_inc(consts, 1)
            nc.gpsimd.memset(cst[:, 1:2], LOW).then_inc(consts, 1)
            nc.gpsimd.memset(cst[:, 2:3], DIAG).then_inc(consts, 1)
            nc.gpsimd.memset(ident[:, :], 0.0).then_inc(consts, 1)
            nc.gpsimd.memset(tri, 1.0).then_inc(consts, 1)
            pool.wait_ge(consts, 8)
            nc.gpsimd.affine_select(ident[:, :], ident[:, :], [[-1, P]], ALU.not_equal, 1.0,
                                    base=0, channel_multiplier=1).then_inc(consts, 1)
            nc.gpsimd.affine_select(tri, tri, [[-1, P]], ALU.is_gt, 0.0,
                                    base=0, channel_multiplier=1).then_inc(consts, 1)
            nc.gpsimd.iota(biota[:, :], [[1, P]], 0, 0, allow_small_or_imprecise_dtypes=True).then_inc(consts, 1)
            nc.gpsimd.iota(eid[:, :], [[1, ET]], 0, ET).then_inc(consts, 1)
            pool.wait_ge(consts, 12)
            nc.gpsimd.tensor_copy(identb[:, :], ident[:, :]).then_inc(consts, 1)
            for s, n in credits:
                pool.sem_inc(s, n)
            pool.wait_ge(idx_ready, 1)
            pool.wait_ge(consts, 13)
            for t in range(ET):
                if t:
                    pool.wait_ge(t_out, 16 * t)
                nc.gpsimd.indirect_dma_start(
                    out=t_dram, out_offset=bass.IndirectOffsetOnAxis(ap=tidx[:, t:t + 1], axis=0),
                    in_=eid[:, t:t + 1], in_offset=None).then_inc(t_out, 16)
            pool.wait_ge(t_out, 16 * ET)
            adj_flat = a["adj"].rearrange("i (j o) -> (i j) o", o=1)
            for t in range(ET):
                nc.gpsimd.indirect_dma_start(
                    out=t_got[:, t:t + 1], out_offset=None, in_=t_dram,
                    in_offset=bass.IndirectOffsetOnAxis(ap=tidx[:, t:t + 1], axis=0)).then_inc(t_in, 16)
                nc.gpsimd.indirect_dma_start(
                    out=adj_got[:, t:t + 1], out_offset=None, in_=adj_flat,
                    in_offset=bass.IndirectOffsetOnAxis(ap=fn_i[:, t:t + 1], axis=0)).then_inc(aj_in, 16)
            for w in range(2):
                pool.wait_ge(qk_dma[w], 16 * (NT + 1))
            pool.wait_ge(P_free, NP_BUF + NB * H * NT)
            for t in range(ET):
                if t >= RING:
                    pool.wait_ge(rows_used, t - RING + 1)
                nc.gpsimd.indirect_dma_start(
                    out=k_rows[t % RING], out_offset=None, in_=k_dram,
                    in_offset=bass.IndirectOffsetOnAxis(ap=obj_i[:, t:t + 1], axis=0)).then_inc(k_in[t % RING], 16)
                nc.gpsimd.indirect_dma_start(
                    out=q_rows[t % RING], out_offset=None, in_=q_dram,
                    in_offset=bass.IndirectOffsetOnAxis(ap=sub_i[:, t:t + 1], axis=0)).then_inc(q_in[t % RING], 16)
            pool.wait_ge(didx_ready, 1)
            pool.wait_ge(zeroed, 16 * 64)
            for t in range(ET):
                if t % CH == 0:
                    pool.wait_ge(v_ready, 2 + t // CH + 1)
                nc.gpsimd.indirect_dma_start(
                    out=d_dram, out_offset=bass.IndirectOffsetOnAxis(ap=didx[:, t:t + 1], axis=0),
                    in_=v_e[:, t:t + 1], in_offset=None).then_inc(d_out, 16)

        @block.tensor
        def _(pe):
            mm, tr = nc.tensor.matmul, nc.tensor.transpose
            pe.wait_ge(consts, 13)
            pe.wait_ge(fn_ready, 1)
            tr(ps[0:ET, 7, 0:P], fn_f, ident[:, :]).then_inc(fn_ps, 1)
            pe.wait_ge(w_in, 16 * 6)
            for g in range(13):
                pe.wait_ge(wt_sb, g + 1)
                for k in range(4):
                    last = tr(ps[:, g % 2, k * P:(k + 1) * P], chunks[4 * g + k], ident[:, :])
                last.then_inc(wt_ps, 1)
            pe.wait_ge(wa_ready, 2 * KT)
            pe.wait_ge(wh_in, 16 * 6)
            pe.wait_ge(f_row_ready, 1)
            with pe.Fori(0, (NT) // 2) as i_:
                i = i_ * 2
                for u in range(2):
                    pe.wait_ge(x_in_s[u], i * 8 + 16)
                    pe.wait_ge(xT_sb, i + (u + 1))
                    for k in range(KT):
                        last = tr(ps[:, 2 + u, k * P:(k + 1) * P], x_in[u][:, k * P:(k + 1) * P], ident[:, :])
                    last.then_inc(xT_ps, 1)
                for u in range(2):
                    pe.wait_ge(xT_sb, i + (u + 3))
                    pe.wait_ge(wh_sb, i + (u + 1))
                    pe.wait_ge(e_sb, i + (u + 1))
                    for k in range(KT):
                        mm(ps[:, 4 + u, :], xT[u][:, k * P:(k + 1) * P], W_in[:, k, :], start=(k == 0), stop=(k == KT - 1))
                    for k in range(KT):
                        last = mm(ps[:, 6 + u, 0:2 * H], xT[u][:, k * P:(k + 1) * P], Wa[:, k, :],
                                  start=(k == 0), stop=(k == KT - 1))
                    last.then_inc(wh_ps, 1)
            pe.wait_ge(e_sb, 2 + NT)
            pe.wait_ge(wt_sb, 2 + 13)
            for g in range(4):
                if g >= 2:
                    pe.wait_ge(rows_sb, 2 * (g - 1))
                for w in range(2):
                    for k in range(4):
                        last = tr(ps[0:H, 2 * (g % 2) + w, k * P:(k + 1) * P],
                                  e_col[:, 4 * g + k, w * H:(w + 1) * H], ident[:, :])
                last.then_inc(rows_ps, 1)
            pe.wait_ge(d_ready, 1)
            pe.wait_ge(wh_sb, 2 + NT)
            mm(ps[:, 4, 0:H], ones[:, :], d_diag[:, :], start=True, stop=True).then_inc(d_ps, 1)
            with pe.Fori(0, (NT) // 2) as i_:
                i = i_ * 2
                for u in range(2):
                    pe.wait_ge(adj_cast, i + (u + 1))
                    for half in range(2):
                        pe.wait_ge(adj_sb, (i + u) * 2 + (half + 2))
                        for k in range(8):
                            j = half * 8 + k
                            last = tr(psb[:, 6 + half, k * P:(k + 1) * P], adj_b[u][:, j * P:(j + 1) * P], identb[:, :])
                        last.then_inc(adj_ps, 1)
            pe.wait_ge(u_ready, NT)
            pe.wait_ge(rows_sb, 8)
            with pe.Fori(0, NB) as b:
                with pe.Fori(0, H // 2) as hp:
                    for u in range(2):
                        g = b * H + hp * 2 + u
                        pe.wait_ge(att_ev, g + 1)
                        for j in range(NT):
                            pe.wait_ge(P_ready, g * NT + (j + 1))
                            for t in range(TI):
                                last = mm(ps[:, u, t * DA:(t + 1) * DA], Pw[j % NP_BUF][:, t * P:(t + 1) * P],
                                          U[:, j, ds(hp * 2 + u, 1), :], start=(j == 0 and t == 0),
                                          stop=(j == NT - 1), skip_group_check=True)
                            last.then_inc(P_free, 1)
                pe.wait_ge(enc_ready, 2 + b * 4 + 4)
                for k in range(KT):
                    for t in range(TI):
                        last = tr(ps[:, 2 + k, t * P:(t + 1) * P], enc[:, t, k * P:(k + 1) * P], ident[:, :])
                last.then_inc(encT_ps, 1)
                pe.wait_ge(encT_a, b * 2 + 2)
                pe.wait_ge(encT_d, b * 2 + 2)
                for o in range(2):
                    for k in range(KT):
                        last = mm(ps[:, 6 + o, :], W1T[k][:, o * P:(o + 1) * P], encT[:, k, :],
                                  start=(k == 0), stop=(k == KT - 1))
                    last.then_inc(z1_ps, 1)
                pe.wait_ge(z1_sb, b * 2 + 2)
                for k in range(2):
                    last = mm(ps[:, 2, :], W2T[k], z1T[:, k, :], start=(k == 0), stop=(k == 1))
                last.then_inc(z2_ps, 1)
                pe.wait_ge(z2_sb, b + 1)
                for o in range(2):
                    mm(ps[:, 3 + o, :], W3T[:, o * P:(o + 1) * P], z2T, start=True, stop=True).then_inc(z3_ps, 1)
                pe.wait_ge(z3_sb, b * 2 + 2)
                for t in range(TI):
                    if t >= 2:
                        pe.wait_ge(y_ready, b * 4 + (t - 1))
                    for k in range(2):
                        last = mm(ps[:, 6 + t % 2, :], z3T[:, k, t * P:(t + 1) * P], W4T[k], start=(k == 0), stop=(k == 1))
                    last.then_inc(z4_ps, 1)
                for t in range(TI):
                    pe.wait_ge(x1_ready, b * 4 + (t + 1))
                    for k in range(KT):
                        last = tr(ps[:, 2 + t % 2, k * P:(k + 1) * P], y[t][:, k * P:(k + 1) * P], ident[:, :])
                    last.then_inc(x1T_ps, 1)
                    pe.wait_ge(x1T_sb, b * 4 + (t + 1))
                    for w, wT in enumerate((WqT, WkT)):
                        if t:
                            pe.wait_ge(qk_sb, b * 8 + (2 * t - 1 + w))
                        for k in range(KT):
                            last = mm(ps[:, 4 + w, :], x1T[t % 2][:, k * P:(k + 1) * P], wT[k],
                                      start=(k == 0), stop=(k == KT - 1))
                        last.then_inc(qk_ps, 1)
            pe.wait_ge(gm_ready, 1)
            tr(ps[0:1, 2, 0:P], glob[:, 0:1], ident[:, :]).then_inc(gm_ps, 1)
            pe.wait_ge(g1_ready, 1)
            mm(ps[:, 3, 0:1], ones[0:1, :], glob[0:1, 1:2], start=True, stop=True).then_inc(g_all, 1)
            pe.wait_ge(beta_ready, 1)
            mm(ps[:, 0, 0:P], zero[:, 0:P], zero[:, 0:P], start=True, stop=False, skip_group_check=True)
            with pe.Fori(0, (CHUNKS) // 2) as c_:
                c = c_ * 2
                for u in range(2):
                    pe.wait_ge(oh_ready, (c + u) * 2 + 2)
                    pe.wait_ge(obT_sb, c + (u + 1))
                    for k in range(CH):
                        mm(ps[:, 0, 0:P], Ob[u][:, k, :], Wc[u][:, k * P:(k + 1) * P], start=False, stop=False,
                           skip_group_check=True)
                        last = tr(ps[:, 2 + 2 * u + k // 4, (k % 4) * P:(k % 4 + 1) * P], Ob[u][:, k, :], ident[:, :])
                    last.then_inc(oh_used, 1)
            pe.wait_ge(m_ready, 1)
            pe.wait_ge(obT_sb, 2 + CHUNKS)
            with pe.Fori(0, (CHUNKS) // 2) as c_:
                c = c_ * 2
                for u in range(2):
                    pe.wait_ge(mg_sb, c + (u + 1))
                    for k in range(CH):
                        last = mm(ps[:, 2 + 2 * u + k // 4, (k % 4) * P:(k % 4 + 1) * P],
                                  ObT[:, ds((c + u) * CH + k, 1), :].rearrange("p o e -> p (o e)"), m_b,
                                  start=(k % 4 == 0), stop=True, skip_group_check=True)
                    last.then_inc(mg_ps, 1)
            mm(ps[:, 1, 0:144], zero[:, 0:P], zero[:, 0:144], start=True, stop=False, skip_group_check=True)
            with pe.Fori(0, (CHUNKS) // 2) as c_:
                c = c_ * 2
                for u in range(2):
                    pe.wait_ge(oh_ready, 2 * CHUNKS + (c + u) * 2 + 2)
                    for k in range(CH):
                        last = mm(ps[:, 1, 0:144], Ob[u][:, k, :], Wc[u][:, k * 144:(k + 1) * 144], start=False,
                                  stop=False, skip_group_check=True)
                    last.then_inc(oh_used, 1)
            pe.wait_ge(c_ready, 1)
            tr(ps[0:NT, 0, 0:P], c_col, ident[:, :]).then_inc(c_ps, 1)
            pe.wait_ge(t9_ready, 1)
            pe.wait_ge(mg_sb, 2 + CHUNKS)
            with pe.Fori(0, (CHUNKS) // 2) as c_:
                c = c_ * 2
                for u in range(2):
                    pe.wait_ge(v_ready, c + (u + 1))
                    for k in range(CH):
                        for part in range(3):
                            last = mm(ps[:, 2 + 3 * u + k // 3, (k % 3) * 144:(k % 3 + 1) * 144],
                                      ObT[:, ds((c + u) * CH + k, 1), :].rearrange("p o e -> p (o e)"), Tb[part],
                                      start=(k % 3 == 0 and part == 0), stop=(part == 2), skip_group_check=True)
                    last.then_inc(g9_ps, 1)
            pe.wait_ge(x1_kept, NT)
            pe.wait_ge(v_ready, 2 + CHUNKS)
            pe.wait_ge(c_row_ready, 1)
            with pe.Fori(0, (NB) // 2) as b_:
                b = b_ * 2
                for v in range(2):
                    pe.wait_ge(o_ev, (b + v) * 4 + 4)
                    for j in range(NT):
                        pe.wait_ge(A_ready, (b + v) * NT + (4 + j + 1))
                        for t in range(TI):
                            last = mm(ps[:, 4 * v + t, :], A[j % 4][:, t * P:(t + 1) * P], xs[:, j, :],
                                      start=(j == 0), stop=(j == NT - 1))
                        last.then_inc(A_free, 1)

        @block.scalar
        def _(act):
            fn = nc.scalar.activation
            act.wait_ge(fn_ps, 1)
            nc.scalar.copy(f_row, ps[0:ET, 7, 0:P]).then_inc(f_row_ready, 1)
            for g in range(13):
                act.wait_ge(wt_ps, g + 1)
                nc.scalar.copy(WT[:, 4 * g:4 * g + 4, :].rearrange("p t n -> p (t n)"), ps[:, g % 2, :]).then_inc(wt_sb, 1)
            with act.Fori(0, (NT) // 2) as i_:
                i = i_ * 2
                for u in range(2):
                    act.wait_ge(xT_ps, i + (u + 1))
                    act.wait_ge(wh_ps, i + (u + 1))
                    nc.scalar.copy(xT[u], ps[:, 2 + u, :]).then_inc(xT_sb, 1)
                for u in range(2):
                    act.wait_ge(wh_ps, i + (u + 3))
                    nc.scalar.copy(e_col[:, ds(i + u, 1), :], ps[:, 6 + u, 0:2 * H]).then_inc(e_sb, 1)
            for g in range(4):
                act.wait_ge(rows_ps, g + 1)
                nc.scalar.copy(s_row[:, g * BLK:(g + 1) * BLK], ps[0:H, 2 * (g % 2), :]).then_inc(rows_sb, 1)
                nc.scalar.copy(d_row[:, g * BLK:(g + 1) * BLK], ps[0:H, 2 * (g % 2) + 1, :]).then_inc(rows_sb, 1)
            with act.Fori(0, (NT) // 2) as i_:
                i = i_ * 2
                for u in range(2):
                    act.wait_ge(adj_in[u], i * 8 + 16)
                    act.wait_ge(adj_sb, (i + u) * 2 + 1)
                    fn(adj_b[u], adj_raw[u], ACT.Copy, accum_out=adj_sum[:, ds(i + u, 1)]).then_inc(adj_cast, 1)
            act.wait_ge(r_arg, 1)
            fn(s_row, s_row, ACT.Exp, scale=0.8).then_inc(r_ready, 1)
            act.wait_ge(shift_ready, 1)
            fn(q_col[:, :, :], e_col[:, :, H:2 * H], ACT.Exp, scale=-0.8).then_inc(ed_ready, 1)
            fn(U[:, :, :, DH], e_col[:, :, H:2 * H], ACT.Exp).then_inc(ed_ready, 1)
            act.wait_ge(small_in, 16 * 5)
            with act.Fori(0, NB) as b:
                with act.Fori(0, H // 2) as hp:
                    for u in range(2):
                        g = b * H + hp * 2 + u
                        act.wait_ge(P_free, (g + 1) * NT + NP_BUF)
                        nc.scalar.copy(att_raw[:, ds(hp * 2 + u, 1), :, :].rearrange("p h t d -> p (h t d)"),
                                       ps[:, u, 0:TI * DA]).then_inc(att_ev, 1)
                for t in range(TI):
                    act.wait_ge(min_ready, b * 4 + (t + 1))
                    fn(ebuf[:, t % 2, :], ebuf[:, t % 2, :], ACT.Exp).then_inc(exp_ready, 1)
                act.wait_ge(encT_ps, b + 1)
                for k in range(2):
                    nc.scalar.copy(encT[:, k, :], ps[:, 2 + k, :]).then_inc(encT_a, 1)
                for o in range(2):
                    act.wait_ge(z1_ps, b * 2 + (o + 1))
                    fn(z1T[:, o, :], ps[:, 6 + o, :], ACT.Relu, bias=bcol[:, o:o + 1]).then_inc(z1_sb, 1)
                act.wait_ge(z2_ps, b + 1)
                fn(z2T, ps[:, 2, :], ACT.Relu, bias=bcol[:, 2:3]).then_inc(z2_sb, 1)
                for o in range(2):
                    act.wait_ge(z3_ps, b * 2 + (o + 1))
                    fn(z3T[:, o, :], ps[:, 3 + o, :], ACT.Relu, bias=bcol[:, 3 + o:4 + o]).then_inc(z3_sb, 1)
                for t in range(TI):
                    act.wait_ge(var_ready, b * 4 + (t + 1))
                    fn(rstd[:, t:t + 1], var[:, t, 1:2], ACT.Ln, bias=cst[:, 0:1]).then_inc(ln_ready, 1)
                    act.wait_ge(ln_ready, b * 4 + (t + 1))
                    fn(rstd[:, t:t + 1], rstd[:, t:t + 1], ACT.Exp, scale=-0.5).then_inc(rstd_ready, 1)
                for t in range(TI):
                    act.wait_ge(x1T_ps, b * 4 + (t + 1))
                    nc.scalar.copy(x1T[t % 2], ps[:, 2 + t % 2, :]).then_inc(x1T_sb, 1)
                    nc.scalar.copy(xs[:, ds(b * 4 + t, 1), :], y[t]).then_inc(x1_kept, 1)
                    for w, dst in enumerate((q_dram, k_dram)):
                        act.wait_ge(qk_sb, b * 8 + (2 * t + w + 1))
                        act.dma_start(dst[ds((b * 4 + t) * P, P), :], qk_out[w]).then_inc(qk_dma[w], 16)
            act.wait_ge(beta_ready, 1)
            fn(e1, e1, ACT.Exp, scale=glob[:, 3:4], bias=cst[:, 1:2]).then_inc(e1_ready, 1)
            with act.Fori(0, (CHUNKS) // 2) as c_:
                c = c_ * 2
                for u in range(2):
                    act.wait_ge(oh_used, c + (u + 3))
                    nc.scalar.copy(ObT[:, ds((c + u) * CH, CH), :].rearrange("p t e -> p (t e)"),
                                   ps[:, 2 + 2 * u:4 + 2 * u, :].rearrange("p b n -> p (b n)")).then_inc(obT_sb, 1)
            act.wait_ge(lse_arg, 1)
            fn(base, base, ACT.Ln).then_inc(lse_ready, 1)
            act.wait_ge(m_ready, 1)
            fn(dterm, Z, ACT.Exp, scale=-1.0, bias=cst[:, 2:3]).then_inc(tabs_ready, 1)
            fn(base, Z, ACT.Exp, scale=-1.0).then_inc(tabs_ready, 1)
            act.wait_ge(p_arg, 1)
            fn(m_e, m_e, ACT.Exp).then_inc(p_exp, 1)
            act.wait_ge(c_ps, 1)
            nc.scalar.copy(c_row, ps[0:NT, 0, 0:P]).then_inc(c_row_ready, 1)
            with act.Fori(0, NB) as b:
                for t in range(TI):
                    act.wait_ge(o_var, b * 4 + (t + 1))
                    fn(rstd[:, t:t + 1], var[:, t, 1:2], ACT.Ln, bias=cst[:, 0:1]).then_inc(o_ln, 1)
                    act.wait_ge(o_ln, b * 4 + (t + 1))
                    fn(rstd[:, t:t + 1], rstd[:, t:t + 1], ACT.Exp, scale=-0.5).then_inc(o_rstd, 1)
                for t in range(TI):
                    act.wait_ge(o_norm, b * 4 + (t + 1))
                    act.dma_start(a["out"][ds((b * 4 + t) * P, P), :], o_buf[t]).then_inc(out_dma[t], 16)

        @block.vector
        def _(dve):
            v = nc.vector
            own = [0]

            def own_step(ins):
                own[0] += 1
                ins.then_inc(dve_own, 1)
                dve.wait_ge(dve_own, own[0])

            dve.wait_ge(pairs_in, 16)
            dve.wait_ge(consts, 13)
            pv = pairs[:, :].rearrange("p (t c) -> p t c", c=2)
            v.tensor_copy(sub_i[:, :], pv[:, :, 0]).then_inc(dve_own, 1)
            v.tensor_copy(obj_i[:, :], pv[:, :, 1]).then_inc(dve_own, 1)
            v.tensor_copy(trash_f, eid[:, :]).then_inc(dve_own, 1)
            v.tensor_copy(sub_f, pv[:, :, 0]).then_inc(dve_own, 1)
            own[0] = 4
            own_step(v.tensor_copy(obj_f, pv[:, :, 1]))
            v.tensor_scalar(ok_f, trash_f, float(EDGES), None, ALU.is_lt).then_inc(dve_own, 1)
            own[0] += 1
            own_step(v.tensor_scalar(ft_f, obj_f, float(N), None, ALU.mult))
            own_step(v.tensor_tensor(ft_f, ft_f, sub_f, ALU.add))
            own_step(v.tensor_scalar(fn_f, sub_f, float(N), None, ALU.mult))
            v.tensor_tensor(fn_f, fn_f, obj_f, ALU.add).then_inc(fn_ready, 1)
            dve.wait_ge(fn_ready, 1)
            own_step(v.tensor_copy(fn_i[:, :], fn_f))
            own_step(v.tensor_scalar(trash_f, trash_f, float(TRASH), None, ALU.add))
            dve.wait_ge(wh_in, 16 * 6)
            for k in range(KT):
                for w in range(2):
                    own_step(v.tensor_tensor(wa_tmp, W_in[:, k, :], a_in[w], ALU.mult))
                    v.tensor_reduce(Wa[:, k, w * H:(w + 1) * H], wa_tmp.rearrange("p (h d) -> p h d", h=H),
                                    AX.X, ALU.add).then_inc(wa_ready, 1)
                    dve.wait_ge(wa_ready, 2 * k + w + 1)
            dve.wait_ge(f_in, 16)
            for t in range(ET):
                own_step(v.scalar_tensor_tensor(out=junk0, in0=pair_rows[:, t * P:(t + 1) * P],
                                                scalar=fn_f[:, t:t + 1], in1=tri, op0=ALU.is_equal, op1=ALU.mult,
                                                accum_out=live[:, t:t + 1]))
            own_step(v.tensor_scalar(live, live, 0.5, None, ALU.is_lt))
            own_step(v.tensor_tensor(ok_f, ok_f, live, ALU.mult))
            own_step(v.tensor_tensor(live, fn_f, trash_f, ALU.subtract))
            own_step(v.tensor_tensor(live, live, ok_f, ALU.mult))
            own_step(v.tensor_tensor(live, live, trash_f, ALU.add))
            v.tensor_copy(tidx[:, :], live).then_inc(idx_ready, 1)
            dve.wait_ge(wt_sb, 2 + 13)
            with dve.Fori(0, (NT) // 2) as i_:
                i = i_ * 2
                for u in range(2):
                    dve.wait_ge(wh_ps, i + (u + 3))
                    v.tensor_copy(U[:, ds(i + u, 1), :, 0:DH].rearrange("p o h d -> p (o h) d"),
                                  ps[:, 4 + u, :].rearrange("p (h d) -> p h d", h=H)).then_inc(wh_sb, 1)
            dve.wait_ge(b4_in_s, 16)
            dve.wait_ge(x_res_in, 16)
            own_step(v.tensor_tensor(xs[:, :, :], xs[:, :, :], b4_in.unsqueeze(1).broadcast_to([P, NT, F]), ALU.add))
            dve.wait_ge(rows_sb, 8)
            own_step(v.tensor_reduce(d_lim[:, 0:1], d_row, AX.X, ALU.max))
            own_step(v.tensor_reduce(d_lim[:, 1:2], d_row, AX.X, ALU.min))
            own_step(v.tensor_tensor(d_lim[:, 2:3], d_lim[:, 0:1], d_lim[:, 1:2], ALU.subtract))
            v.tensor_scalar(d_diag[:, :], ident[0:H, 0:H], d_lim[:, 0:1], None, ALU.mult).then_inc(d_ready, 1)
            own_step(v.tensor_scalar(s_row, s_row, d_lim[:, 0:1], 0.0, ALU.add, ALU.max))
            v.tensor_scalar(s_row, s_row, d_lim[:, 2:3], None, ALU.min).then_inc(r_arg, 1)
            dve.wait_ge(d_ps, 1)
            v.tensor_tensor(e_col[:, :, H:2 * H], e_col[:, :, H:2 * H],
                            ps[:, 4, 0:H].unsqueeze(1).broadcast_to([P, NT, H]), ALU.subtract).then_inc(shift_ready, 1)
            with dve.Fori(0, (NT) // 2) as i_:
                i = i_ * 2
                for u in range(2):
                    dve.wait_ge(adj_cast, i + (u + 1))
                    dve.wait_ge(adj_dg, i + (u + 1))
                    v.scalar_tensor_tensor(out=junk0, in0=adj_b[u].rearrange("p (j n) -> p j n", n=P)[:, ds(i + u, 1), :]
                                           .rearrange("p o n -> p (o n)"), scalar=1.0, in1=identb[:, :], op0=ALU.mult,
                                           op1=ALU.mult, accum_out=adj_diag[:, ds(i + u, 1)]).then_inc(adj_dg, 1)
                    for half in range(2):
                        dve.wait_ge(adj_ps, (i + u) * 2 + (half + 1))
                        v.tensor_copy(adjT[:, half * 8:half * 8 + 8, ds((i + u) * P, P)],
                                      psb[:, 6 + half, :].rearrange("p (j n) -> p j n", n=P)).then_inc(adj_sb, 1)
            dve.wait_ge(ed_ready, 2)
            for j in range(NT):
                v.tensor_tensor(U[:, j, :, 0:DH], U[:, j, :, 0:DH],
                                U[:, j, :, DH:DA].broadcast_to([P, H, DH]), ALU.mult).then_inc(u_ready, 1)
            dve.wait_ge(bqk_in, 32)
            with dve.Fori(0, NB) as b:
                with dve.Fori(0, H // 2) as hp:
                    for u in range(2):
                        g = b * H + hp * 2 + u
                        dve.wait_ge(r_in[u], b * 64 + hp * 16 + 16)
                        for j in range(NT):
                            dve.wait_ge(P_free, g * NT + (j + 1))
                            v.scalar_tensor_tensor(out=Pw[j % NP_BUF], in0=r_b[u], scalar=q_col[:, j, ds(hp * 2 + u, 1)],
                                                   in1=adjT[:, j, ds(b * BLK, BLK)], op0=ALU.max,
                                                   op1=ALU.mult).then_inc(P_ready, 1)
                dve.wait_ge(att_ev, b * 8 + 10)
                v.reciprocal(rden[:, :, :], att_raw[:, :, :, DH]).then_inc(rden_ready, 1)
                dve.wait_ge(rden_ready, b + 1)
                for t in range(TI):
                    v.tensor_tensor(enc[:, t, :].rearrange("p (h d) -> p h d", h=H), att_raw[:, :, t, 0:DH],
                                    rden[:, :, t:t + 1].broadcast_to([P, H, DH]), ALU.mult).then_inc(hn_ready, 1)
                for t in range(TI):
                    dve.wait_ge(hn_ready, b * 4 + (t + 1))
                    dve.wait_ge(enc_ready, b * 4 + (t + 1))
                    v.tensor_scalar(ebuf[:, t % 2, :], enc[:, t, :], 0.0, None, ALU.min).then_inc(min_ready, 1)
                    if t % 2:
                        for s in (t - 1, t):
                            dve.wait_ge(exp_ready, b * 4 + (s + 1))
                            v.scalar_tensor_tensor(out=enc[:, s, :], in0=ebuf[:, s % 2, :], scalar=-1.0,
                                                   in1=enc[:, s, :], op0=ALU.add, op1=ALU.max).then_inc(enc_ready, 1)
                dve.wait_ge(encT_ps, b + 1)
                for k in range(2, 4):
                    v.tensor_copy(encT[:, k, :], ps[:, 2 + k, :]).then_inc(encT_d, 1)
                for t in range(TI):
                    dve.wait_ge(z4_ps, b * 4 + (t + 1))
                    v.tensor_tensor(y[t], ps[:, 6 + t % 2, :], xs[:, ds(b * 4 + t, 1), :].rearrange("p o n -> p (o n)"),
                                    ALU.add).then_inc(y_ready, 1)
                    dve.wait_ge(y_ready, b * 4 + (t + 1))
                    v.bn_stats(stats[:, t, :], y[t]).then_inc(st_ready, 1)
                dve.wait_ge(st_ready, b * 4 + 4)
                v.memset(carrier[:, :], 0.0)
                for t in range(TI):
                    v.bn_aggr(var[:, t, :], stats[:, t, :]).then_inc(var_ready, 1)
                for t in range(TI):
                    dve.wait_ge(rstd_ready, b * 4 + (t + 1))
                    v.tensor_scalar(y[t], y[t], var[:, t, 0:1], rstd[:, t:t + 1], ALU.subtract,
                                    ALU.mult).then_inc(x1_ready, 1)
                for t in range(TI):
                    for w in range(2):
                        dve.wait_ge(qk_ps, b * 8 + (2 * t + w + 1))
                        dve.wait_ge(qk_dma[w], b * 64 + (16 * t + 16))
                        v.tensor_tensor(qk_out[w], ps[:, 4 + w, :], bqk[:, w, :], ALU.add).then_inc(qk_sb, 1)

            dve.wait_ge(t_in, 16 * ET)
            dve.wait_ge(aj_in, 16 * ET)
            dve.wait_ge(x1_kept, NT)
            own_step(v.tensor_tensor(live, t_got[:, :], eid[:, :], ALU.is_equal))
            own_step(v.tensor_tensor(live, live, ok_f, ALU.mult))
            own_step(v.tensor_tensor(ok_f, sub_f, obj_f, ALU.not_equal))
            own_step(v.tensor_tensor(live, live, ok_f, ALU.mult))
            own_step(v.tensor_scalar(ok_f, adj_got, 1.0, None, ALU.is_equal))
            own_step(v.tensor_tensor(live, live, ok_f, ALU.mult))
            own_step(v.tensor_tensor(ft_f, ft_f, trash_f, ALU.subtract))
            own_step(v.tensor_tensor(ft_f, ft_f, live, ALU.mult))
            own_step(v.tensor_tensor(ft_f, ft_f, trash_f, ALU.add))
            v.tensor_copy(didx[:, :], ft_f).then_inc(didx_ready, 1)
            own_step(v.tensor_scalar(t_got[:, :], sub_i[:, :], 7, None, ALU.logical_shift_right))
            own_step(v.tensor_copy(a_f, t_got[:, :]))
            own_step(v.scalar_tensor_tensor(out=b_f, in0=a_f, scalar=-float(P), in1=sub_f, op0=ALU.mult, op1=ALU.add))
            own_step(v.tensor_tensor(Oa, biota[:, 0:NT].unsqueeze(1).broadcast_to([P, ET, NT]),
                                     a_f.unsqueeze(2).broadcast_to([P, ET, NT]), ALU.is_equal))
            with dve.Fori(0, (ET) // RING) as t8_:
                t8 = t8_ * RING
                for u in range(RING):
                    dve.wait_ge(k_in[u], t8 * 2 + 16)
                    dve.wait_ge(q_in[u], t8 * 2 + 16)
                    v.tensor_tensor(prod[u % 2], k_rows[u], q_rows[u], ALU.mult).then_inc(prod_ready, 1)
                    dve.wait_ge(prod_ready, t8 + (u + 1))
                    v.tensor_reduce(att[:, ds(t8 + u, 1), :].rearrange("p o h -> p (o h)"),
                                    prod[u % 2].rearrange("p (h d) -> p h d", h=H), AX.X, ALU.add).then_inc(rows_used, 1)
            dve.wait_ge(rows_used, ET)
            own_step(v.scalar_tensor_tensor(out=att, in0=att, scalar=1.0 / float(DH) ** 0.5,
                                            in1=live.unsqueeze(2).broadcast_to([P, ET, H]), op0=ALU.mult, op1=ALU.mult))
            v.tensor_reduce(glob[:, 0:1], att_f, AX.X, ALU.max).then_inc(gm_ready, 1)
            own_step(v.tensor_scalar(e1, att_f, 0.0, None, ALU.max))
            dve.wait_ge(gm_ps, 1)
            own_step(v.tensor_reduce(glob[0:1, 2:3], ps[0:1, 2, 0:P], AX.X, ALU.max))
            v.tensor_scalar(glob[0:1, 1:2], glob[0:1, 2:3], 1.0, None, ALU.max).then_inc(g1_ready, 1)
            dve.wait_ge(g_all, 1)
            own_step(v.tensor_scalar(glob[:, 4:5], ps[:, 3, 0:1], 1.0 / SPAN, None, ALU.mult))
            v.reciprocal(glob[:, 3:4], glob[:, 4:5]).then_inc(beta_ready, 1)
            dve.wait_ge(e1_ready, 1)
            e1v = e1.rearrange("p (t h) -> p t h", h=H)

            def one_hot(c, u, vals, nh):
                v.tensor_tensor(Ob[u], biota[:, :].unsqueeze(1).broadcast_to([P, CH, P]),
                                b_f[:, ds(c * CH, CH)].unsqueeze(2).broadcast_to([P, CH, P]),
                                ALU.is_equal).then_inc(oh_ready, 1)
                weighted(c, u, vals, nh).then_inc(oh_ready, 1)

            def weighted(c, u, vals, nh):
                return v.tensor_tensor(Wc[u][:, 0:CH * NT * nh].rearrange("p (t k h) -> p t k h", t=CH, k=NT),
                                       vals[:, ds(c * CH, CH), :].unsqueeze(2).broadcast_to([P, CH, NT, nh]),
                                       Oa[:, ds(c * CH, CH), :].unsqueeze(3).broadcast_to([P, CH, NT, nh]), ALU.mult)

            with dve.Fori(0, (CHUNKS) // 2) as c_:
                c = c_ * 2
                for u in range(2):
                    dve.wait_ge(oh_used, c + (u + 1))
                    one_hot(c + u, u, e1v, H)
            dve.wait_ge(oh_used, 2 + CHUNKS)
            v.tensor_scalar(base, ps[:, 0, 0:P], float(2.718281828459045 ** LOW), None, ALU.add).then_inc(lse_arg, 1)
            dve.wait_ge(lse_ready, 1)
            own_step(v.tensor_scalar(Z, base, -LOW, glob[:, 4:5], ALU.add, ALU.mult))
            own_step(v.tensor_copy(m_b, Z))
            v.tensor_copy(Z, m_b).then_inc(m_ready, 1)
            with dve.Fori(0, (CHUNKS) // 2) as c_:
                c = c_ * 2
                for u in range(2):
                    dve.wait_ge(mg_ps, c + (u + 1))
                    m_prod = Wc[u][:, 0:CH * P]
                    v.tensor_tensor(m_prod.rearrange("p (t k h) -> p t k h", t=CH, k=NT),
                                    ps[:, 2 + 2 * u:4 + 2 * u, :].rearrange("p b n -> p (b n)").rearrange(
                                        "p (t k h) -> p t k h", t=CH, k=NT),
                                    Oa[:, ds((c + u) * CH, CH), :].unsqueeze(3).broadcast_to([P, CH, NT, H]),
                                    ALU.mult).then_inc(mg_sb, 1)
                    dve.wait_ge(mg_sb, c + (u + 3))
                    v.tensor_reduce(m_e.rearrange("p (t h) -> p t h", h=H)[:, ds((c + u) * CH, CH), :],
                                    m_prod.rearrange("p (t k h) -> p t h k", t=CH, k=NT), AX.X, ALU.add).then_inc(dve_loop, 1)
            dve.wait_ge(dve_loop, CHUNKS)
            v.tensor_tensor(m_e, att_f, m_e, ALU.subtract).then_inc(p_arg, 1)
            dve.wait_ge(p_exp, 1)
            own_step(v.tensor_tensor(p9[:, :, 0:H], m_e.rearrange("p (t h) -> p t h", h=H),
                                     live.unsqueeze(2).broadcast_to([P, ET, H]), ALU.mult))
            own_step(v.tensor_copy(p9[:, :, H], live))
            with dve.Fori(0, (CHUNKS) // 2) as c_:
                c = c_ * 2
                for u in range(2):
                    dve.wait_ge(oh_used, CHUNKS + (c + u) + 1)
                    one_hot(c + u, u, p9, 9)
            dve.wait_ge(oh_used, 2 + 2 * CHUNKS)
            dve.wait_ge(tabs_ready, 2)
            own_step(v.tensor_copy(seg, ps[:, 1, 0:144].rearrange("p (t h) -> p t h", h=9)))
            own_step(v.tensor_tensor(n_col, adj_sum[:, :], adj_diag[:, :], ALU.subtract))
            own_step(v.tensor_tensor(n_col, n_col, seg[:, :, H], ALU.subtract))
            b3, d3, z3 = (w.rearrange("p (t h) -> p t h", h=H) for w in (base, dterm, Z))
            own_step(v.tensor_tensor(z3, b3, n_col.unsqueeze(2).broadcast_to([P, NT, H]), ALU.mult))
            own_step(v.tensor_tensor(z3, z3, seg[:, :, 0:H], ALU.add))
            own_step(v.tensor_tensor(z3, z3, d3, ALU.add))
            own_step(v.reciprocal(Z, Z))
            own_step(v.tensor_scalar(T9[:, :, 0:H], z3, 1.0 / H, None, ALU.mult))
            own_step(v.tensor_tensor(b3, b3, T9[:, :, 0:H], ALU.mult))
            own_step(v.tensor_tensor(d3, d3, T9[:, :, 0:H], ALU.mult))
            v.tensor_reduce(c_col, b3, AX.X, ALU.add).then_inc(c_ready, 1)
            own_step(v.tensor_reduce(cd_col, d3, AX.X, ALU.add))
            dve.wait_ge(c_ready, 1)
            own_step(v.tensor_scalar(T9[:, :, H], c_col, -1.0, None, ALU.mult))
            own_step(v.tensor_tensor(n_col, c_col, adj_diag[:, :], ALU.mult))
            own_step(v.tensor_tensor(cd_col, cd_col, n_col, ALU.subtract))
            own_step(v.tensor_scalar(dcoef, cd_col, 1.0, None, ALU.add))
            own_step(v.tensor_copy(Tb[0], T9f))
            own_step(v.tensor_tensor(T_tmp, T9f, Tb[0], ALU.subtract))
            own_step(v.tensor_copy(Tb[1], T_tmp))
            own_step(v.tensor_tensor(T_tmp, T_tmp, Tb[1], ALU.subtract))
            v.tensor_copy(Tb[2], T_tmp).then_inc(t9_ready, 1)
            with dve.Fori(0, (CHUNKS) // 2) as c_:
                c = c_ * 2
                for u in range(2):
                    weighted(c + u, u, p9, 9).then_inc(w_ready, 1)
                    dve.wait_ge(w_ready, c + (u + 1))
                    dve.wait_ge(g9_ps, c + (u + 1))
                    for k in range(CH):
                        last = v.tensor_tensor_reduce(Wc[u][:, k * 144:(k + 1) * 144], ps[:, 2 + 3 * u + k // 3, (k % 3) * 144:(k % 3 + 1) * 144],
                                                      Wc[u][:, k * 144:(k + 1) * 144], 1.0, 0.0, ALU.mult, ALU.add,
                                                      v_part[:, k:k + 1])
                        last.then_inc(v_sum, 1)
                    dve.wait_ge(v_sum, (c + u) * CH + CH)
                    v.tensor_copy(v_e[:, ds((c + u) * CH, CH)], v_part).then_inc(v_ready, 1)
            dve.wait_ge(c_in, 16)
            with dve.Fori(0, (NB) // 2) as b_:
                b = b_ * 2
                for w in range(2):
                    with dve.Fori(0, NT // 4) as jq:
                        for u in range(4):
                            n = (b + w) * NT + jq * 4 + u
                            dve.wait_ge(A_free, n + 1)
                            v.tensor_tensor(A[u], adjT[:, ds(jq * 4 + u, 1), ds((b + w) * BLK, BLK)].rearrange("p o n -> p (o n)"),
                                            c_b[:, ds((b + w) * BLK, BLK)], ALU.mult).then_inc(A_tmp, 1)
                            dve.wait_ge(A_tmp, n + 1)
                            dve.wait_ge(d_slot[u], (b + w) * 64 + jq * 16 + 16)
                            v.tensor_tensor(A[u], A[u], d_in[u], ALU.add).then_inc(A_ready, 1)
                    dve.wait_ge(A_free, (b + w) * NT + (NT + 4))
                    for t in range(TI):
                        dve.wait_ge(out_dma[t], (b + w) * 16 + 16)
                        v.scalar_tensor_tensor(out=o_buf[t], in0=xs[:, ds((b + w) * 4 + t, 1), :].rearrange("p o n -> p (o n)"),
                                               scalar=dcoef[:, ds((b + w) * 4 + t, 1)], in1=ps[:, 4 * w + t, :],
                                               op0=ALU.mult, op1=ALU.add).then_inc(o_ev, 1)
                        dve.wait_ge(o_ev, (b + w) * 4 + (t + 9))
                        v.bn_stats(stats[:, t, :], o_buf[t]).then_inc(o_st, 1)
                    dve.wait_ge(o_st, (b + w) * 4 + 4)
                    v.memset(carrier[:, :], 0.0)
                    for t in range(TI):
                        v.bn_aggr(var[:, t, :], stats[:, t, :]).then_inc(o_var, 1)
                    for t in range(TI):
                        dve.wait_ge(o_rstd, (b + w) * 4 + (t + 1))
                        v.tensor_scalar(o_buf[t], o_buf[t], var[:, t, 0:1], rstd[:, t:t + 1], ALU.subtract,
                                        ALU.mult).then_inc(o_norm, 1)


_INS = {"x": "x", "adj": "adj", "W": "L0_gnn_W", "a1": "L0_gnn_a1", "a2": "L0_gnn_a2",
        "W1": "L0_gnn_W1", "b1": "L0_gnn_b1", "W2": "L0_gnn_W2", "b2": "L0_gnn_b2", "W3": "L0_gnn_W3",
        "b3": "L0_gnn_b3", "W4": "L0_gnn_W4", "b4": "L0_gnn_b4", "pairs": "L1_gnn_rel_pair_index",
        "Wq": "L1_gnn_Wq", "bq": "L1_gnn_bq", "Wk": "L1_gnn_Wk", "bk": "L1_gnn_bk"}


def kernel(**inputs):
    import numpy as _np
    import concourse.bacc as _bacc
    from concourse import mybir as _mybir
    from concourse.bass_utils import run_bass_kernel_spmd as _run

    nc = _bacc.Bacc("TRN2", target_bir_lowering=False, num_devices=1)
    arrays, args = {}, {}
    for short, name in _INS.items():
        arr = _np.ascontiguousarray(inputs[name])
        arrays[f"in_{short}"] = arr
        args[short] = nc.dram_tensor(f"in_{short}", arr.shape, _mybir.dt.from_np(arr.dtype), kind="ExternalInput").ap()
    args["out"] = nc.dram_tensor("out_0", (N, F), F32, kind="ExternalOutput").ap()
    build(nc, args)
    r = _run(nc, [arrays], core_ids=[0])
    return r.results[0]["out_0"]
```

```python
import concourse.bass as bass
from concourse import mybir
from contextlib import ExitStack

F32 = mybir.dt.float32
BF16 = mybir.dt.bfloat16
I32 = mybir.dt.int32
ALU = mybir.AluOpType
ACT = mybir.ActivationFunctionType
AX = mybir.AxisListType

P = 128
N, F, H, DH = 2048, 512, 8, 64
NT = N // P
KT = F // P
BLK = 512
NB = N // BLK
TI = BLK // P
E1, E2, E3 = 256, 128, 256
EDGES = 10000
ET = 80
EP = EDGES // ET
TRASH = N * N
CH = 8
SPAN = 78.0
LOW = -44.0
EPS = 1e-5
DIAG = 1e-7
NP_BUF = 4
RING = 8


def build(nc, a):
    ds = bass.ds
    with ExitStack() as ctx:
        def sb(name, shape, dt=F32):
            return ctx.enter_context(nc.sbuf_tensor(name, shape, dt))

        def sem(name):
            return ctx.enter_context(nc.semaphore(name))

        def dram(name, shape, dt=F32):
            return nc.dram_tensor(name, shape, dt).ap()

        r_dram = dram("r_dram", (NB * H, BLK))
        f_dram = dram("f_dram", (ET, P))
        q_dram = dram("q_dram", (N, F))
        k_dram = dram("k_dram", (N, F))
        c_dram = dram("c_dram", (NT, P))
        t_dram = dram("t_dram", (N * N + P * ET, 1), I32)
        d_dram = dram("d_dram", (N * N + P * ET, 1))

        adjT = sb("adjT", [P, NT, N], BF16)
        U = sb("U", [P, NT, H, DH])
        xs = U[:, :, :, :].rearrange("p j h d -> p j (h d)")
        WT = sb("WT", [P, 52, P])
        arena = sb("arena", [P, 15872])
        ED = sb("ED", [P, NT, H])
        q_col = sb("q_col", [P, NT, H])
        bqk = sb("bqk", [P, 2, F])
        b4_row = sb("b4_row", [P, F])
        tri = sb("tri", [P, P])[:, :]
        junk0 = sb("junk0", [P, P])[:, :]
        e_col = sb("e_col", [P, NT, 2 * H])
        Wa = sb("Wa", [P, KT, 2 * H])
        bcol = sb("bcol", [P, 5])
        zero = sb("zero", [P, 144])
        ident = sb("ident", [P, P])
        identb = sb("identb", [P, P], BF16)
        biota = sb("biota", [P, P])
        ones = sb("ones", [8, P])
        cst = sb("cst", [P, 4])
        adj_sum = sb("adj_sum", [P, NT])
        adj_diag = sb("adj_diag", [P, NT])
        pairs = sb("pairs", [P, 2 * ET], I32)
        eid = sb("eid", [P, ET], I32)
        sub_i = sb("sub_i", [P, ET], I32)
        obj_i = sb("obj_i", [P, ET], I32)
        fn_i = sb("fn_i", [P, ET], I32)
        tidx = sb("tidx", [P, ET], I32)
        didx = sb("didx", [P, ET], I32)
        t_got = sb("t_got", [P, ET], I32)
        ef = sb("ef", [P, 8, ET])
        sub_f, obj_f, fn_f, ft_f, trash_f, ok_f, live, adj_got = (ef[:, k, :] for k in range(8))
        stats = sb("stats", [P, NT, 6])
        var = sb("var", [P, NT, 2])
        rstd = sb("rstd", [P, NT])
        carrier = sb("carrier", [P, 1])

        adj_raw = [arena[:, 2048 * u:2048 * u + 2048] for u in range(2)]
        adj_b = [arena[:, 4096 + 1024 * u:5120 + 1024 * u].bitcast(BF16) for u in range(2)]
        x_in = [arena[:, 6144 + 512 * u:6656 + 512 * u] for u in range(2)]
        xT = [arena[:, 7168 + 512 * u:7680 + 512 * u] for u in range(2)]
        W_in = arena[:, 8704:10752].rearrange("p (k n) -> p k n", k=KT)
        a_in = [arena[:, 10752 + 512 * u:11264 + 512 * u] for u in range(2)]
        wa_tmp = arena[:, 11776:12288]
        s_row = arena[0:H, 8704:10752]
        d_row = arena[0:H, 10752:12800]
        d_lim = sb("d_lim", [H, 4])
        d_diag = sb("d_diag", [H, H])
        f_row = arena[0:ET, 12800:12928]
        pair_rows = adjT[:, 0:10, :].rearrange("p a n -> p (a n)").bitcast(F32)
        raw = U[:, :, :, :].rearrange("p j h d -> p (j h d)")
        w_raw = raw[:, 0:6656]
        W1r = w_raw[:, 0:1024].rearrange("p (o n) -> p o n", o=2)
        W2r = w_raw[:, 1024:1280]
        W3r = w_raw[:, 1280:1536].rearrange("p (o n) -> p o n", o=2)
        W4r = w_raw[:, 1536:2560].rearrange("p (o n) -> p o n", o=4)
        Wqr = w_raw[:, 2560:4608].rearrange("p (o n) -> p o n", o=4)
        Wkr = w_raw[:, 4608:6656].rearrange("p (o n) -> p o n", o=4)
        chunks = ([(W1r[:, o, k * P:(k + 1) * P]) for k in range(4) for o in range(2)]
                  + [W2r[:, k * P:(k + 1) * P] for k in range(2)]
                  + [W3r[:, o, :] for o in range(2)]
                  + [W4r[:, o, k * P:(k + 1) * P] for k in range(2) for o in range(4)]
                  + [Wqr[:, o, k * P:(k + 1) * P] for k in range(4) for o in range(4)]
                  + [Wkr[:, o, k * P:(k + 1) * P] for k in range(4) for o in range(4)])
        W1T = [WT[:, 2 * k:2 * k + 2, :].rearrange("p o n -> p (o n)") for k in range(4)]
        W2T = [WT[:, 8 + k, :] for k in range(2)]
        W3T = WT[:, 10:12, :].rearrange("p o n -> p (o n)")
        W4T = [WT[:, 12 + 4 * k:16 + 4 * k, :].rearrange("p o n -> p (o n)") for k in range(2)]
        WqT = [WT[:, 20 + 4 * k:24 + 4 * k, :].rearrange("p o n -> p (o n)") for k in range(4)]
        WkT = [WT[:, 36 + 4 * k:40 + 4 * k, :].rearrange("p o n -> p (o n)") for k in range(4)]

        enc_all = arena[:, 0:8704]
        encT = enc_all[:, 512:8704].rearrange("p (k n) -> p k n", k=KT)
        Us = [arena[:, 8704 + 2048 * u:10752 + 2048 * u].rearrange("p (j n) -> p j n", j=NT) for u in range(2)]
        Pw = [arena[:, 12800 + 512 * u:13312 + 512 * u] for u in range(NP_BUF)]
        r_b = [arena[:, 14848 + 512 * u:15360 + 512 * u] for u in range(2)]
        rden = sb("rden", [DH, BLK])
        ebuf = arena[:, 14848:15872].rearrange("p (t n) -> p t n", t=2)
        z1T = arena[:, 8704:12800].rearrange("p (o n) -> p o n", o=2)
        z2T = arena[:, 12800:14848]
        z3T = arena[:, 8704:12800].rearrange("p (o n) -> p o n", o=2)
        y = [arena[:, 512 * u:512 * u + 512] for u in range(2)]
        x1T = [arena[:, 1024 + 512 * u:1536 + 512 * u] for u in range(2)]
        qk_out = [arena[:, 2048 + 512 * u:2560 + 512 * u] for u in range(2)]

        k_rows = [arena[:, 512 * u:512 * u + 512] for u in range(RING)]
        q_rows = [arena[:, 4096 + 512 * u:4608 + 512 * u] for u in range(RING)]
        o = 8704
        att = arena[:, o:o + 640].rearrange("p (t h) -> p t h", h=H)
        att_f = arena[:, o:o + 640]
        e1 = arena[:, o + 640:o + 1280]
        m_e = arena[:, o + 1280:o + 1920]
        p9 = arena[:, o + 1920:o + 2640].rearrange("p (t h) -> p t h", h=9)
        Oa = arena[:, o + 2640:o + 3920].rearrange("p (t k) -> p t k", k=NT)
        a_f = arena[:, o + 3920:o + 4000]
        b_f = arena[:, o + 4000:o + 4080]
        v_e = arena[:, o + 4080:o + 4160]
        v_part = arena[:, o + 4160:o + 4168]
        prod = [arena[:, o + 4176 + 512 * u:o + 4688 + 512 * u] for u in range(2)]
        Ob = [arena[:, 1024 * u:1024 * u + 1024].rearrange("p (t b) -> p t b", t=CH) for u in range(2)]
        Wc = [arena[:, 2048 + 1152 * u:3200 + 1152 * u] for u in range(2)]
        ObT = WT[:, 0:40, :].rearrange("p t n -> p (t n)").bitcast(BF16).rearrange("p (t e) -> p t e", t=ET)
        tab = WT[:, 40:52, :].rearrange("p t n -> p (t n)")
        m_b = tab[:, 0:64].bitcast(BF16)
        base = tab[:, 64:192]
        dterm = tab[:, 192:320]
        seg = tab[:, 320:464].rearrange("p (t h) -> p t h", h=9)
        Z = tab[:, 464:592]
        T9 = tab[:, 592:736].rearrange("p (t h) -> p t h", h=9)
        T9f = tab[:, 592:736]
        Tb = [tab[:, 736 + 72 * u:808 + 72 * u].bitcast(BF16) for u in range(3)]
        c_col = tab[:, 952:968]
        cd_col = tab[:, 968:984]
        n_col = tab[:, 984:1000]
        dcoef = tab[:, 1000:1016]
        c_row = tab[0:NT, 1016:1144]
        glob = tab[:, 1144:1156]
        T_tmp = tab[:, 1156:1300]
        A = [arena[:, 512 * u:512 * u + 512] for u in range(4)]
        o_buf = [arena[:, 2048 + 512 * u:2560 + 512 * u] for u in range(TI)]
        c_b = arena[:, 4352:6400]
        d_in = [arena[:, 6400 + 512 * u:6912 + 512 * u] for u in range(4)]

        ps = ctx.enter_context(nc.psum_tensor("ps", [P, 8, 512], F32))
        psb = ps[:, :, :].rearrange("p b n -> p (b n)").bitcast(BF16).rearrange("p (b n) -> p b n", b=8)

        consts = sem("consts")
        pairs_in = sem("pairs_in")
        w_in = sem("w_in")
        wh_in = sem("wh_in")
        small_in = sem("small_in")
        b4_in_s = sem("b4_in_s")
        bqk_in = sem("bqk_in")
        x_res_in = sem("x_res_in")
        dve_own = sem("dve_own")
        fn_ready = sem("fn_ready")
        fn_ps = sem("fn_ps")
        f_row_ready = sem("f_row_ready")
        f_out = sem("f_out")
        f_in = sem("f_in")
        idx_ready = sem("idx_ready")
        wa_ready = sem("wa_ready")
        wt_ps = sem("wt_ps")
        wt_sb = sem("wt_sb")
        x_in_s = [sem(f"x_in_s{u}") for u in range(2)]
        xT_ps = sem("xT_ps")
        xT_sb = sem("xT_sb")
        wh_ps = sem("wh_ps")
        wh_sb = sem("wh_sb")
        e_sb = sem("e_sb")
        rows_ps = sem("rows_ps")
        rows_sb = sem("rows_sb")
        d_ready = sem("d_ready")
        d_ps = sem("d_ps")
        shift_ready = sem("shift_ready")
        r_arg = sem("r_arg")
        r_ready = sem("r_ready")
        ed_ready = sem("ed_ready")
        u_ready = sem("u_ready")
        adj_in = [sem(f"adj_in{u}") for u in range(2)]
        adj_cast = sem("adj_cast")
        dve_loop = sem("dve_loop")
        adj_dg = sem("adj_dg")
        adj_ps = sem("adj_ps")
        adj_sb = sem("adj_sb")
        r_out = sem("r_out")
        r_in = [sem(f"r_in{u}") for u in range(2)]
        P_ready = sem("P_ready")
        P_free = sem("P_free")
        us_ready = sem("us_ready")
        bank_set = sem("bank_set")
        rden_ready = sem("rden_ready")
        att_ev = sem("att_ev")
        b4_added = sem("b4_added")
        min_ready = sem("min_ready")
        exp_ready = sem("exp_ready")
        enc_ready = sem("enc_ready")
        z1_ps, z1_sb = sem("z1_ps"), sem("z1_sb")
        z2_ps, z2_sb = sem("z2_ps"), sem("z2_sb")
        z3_ps, z3_sb = sem("z3_ps"), sem("z3_sb")
        z4_ps = sem("z4_ps")
        y_ready = sem("y_ready")
        st_ready = sem("st_ready")
        var_ready = sem("var_ready")
        ln_ready = sem("ln_ready")
        rstd_ready = sem("rstd_ready")
        x1_ready = sem("x1_ready")
        x1_kept = sem("x1_kept")
        x1T_ps, x1T_sb = sem("x1T_ps"), sem("x1T_sb")
        qk_ps = sem("qk_ps")
        qk_sb = sem("qk_sb")
        qk_dma = [sem(f"qk_dma{w}") for w in range(2)]
        t_out = sem("t_out")
        t_in = sem("t_in")
        aj_in = sem("aj_in")
        zeroed = sem("zeroed")
        k_in = [sem(f"k_in{u}") for u in range(RING)]
        q_in = [sem(f"q_in{u}") for u in range(RING)]
        prod_ready = sem("prod_ready")
        rows_used = sem("rows_used")
        didx_ready = sem("didx_ready")
        gm_ready, gm_ps, g1_ready, g_all = sem("gm_ready"), sem("gm_ps"), sem("g1_ready"), sem("g_all")
        beta_ready, e1_ready = sem("beta_ready"), sem("e1_ready")
        oh_ready = sem("oh_ready")
        oh_used = sem("oh_used")
        obT_sb = sem("obT_sb")
        lse_arg, lse_ready = sem("lse_arg"), sem("lse_ready")
        m_ready = sem("m_ready")
        tabs_ready = sem("tabs_ready")
        mg_ps, mg_sb = sem("mg_ps"), sem("mg_sb")
        p_arg, p_exp, p_ready = sem("p_arg"), sem("p_exp"), sem("p_ready")
        c_ready, c_ps, c_row_ready = sem("c_ready"), sem("c_ps"), sem("c_row_ready")
        c_out, c_in = sem("c_out"), sem("c_in")
        t9_ready = sem("t9_ready")
        w_ready = sem("w_ready")
        g9_ps = sem("g9_ps")
        v_sum = sem("v_sum")
        v_ready = sem("v_ready")
        d_out = sem("d_out")
        d_slot = [sem(f"d_slot{u}") for u in range(4)]
        A_tmp = sem("A_tmp")
        A_ready = sem("A_ready")
        A_free = sem("A_free")
        o_ev = sem("o_ev")
        o_st, o_var, o_ln, o_rstd, o_norm = sem("o_st"), sem("o_var"), sem("o_ln"), sem("o_rstd"), sem("o_norm")
        out_dma = [sem(f"out_dma{t}") for t in range(TI)]

        credits = ([(s, 2) for s in (wt_sb, xT_sb, wh_ps, wh_sb, e_sb, enc_ready, oh_used, obT_sb,
                                     mg_sb, v_ready)]
                   + [(adj_sb, 3), (adj_dg, 1), (att_ev, 1), (z1_sb, 4), (qk_sb, 2), (x1_ready, 2), (x1T_sb, 2), (x1_kept, 2), (P_free, NP_BUF), (A_ready, 4), (A_free, 4), (o_ev, 8)]
                   + [(s, 16) for s in qk_dma + out_dma])
        CHUNKS = ET // CH

        block = ctx.enter_context(nc.Block())

        @block.sync
        def _(sp):
            sp.wait_ge(consts, 1)
            sp.dma_start(pairs[0:EP, :], a["pairs"].rearrange("(p t) c -> p (t c)", t=ET)).then_inc(pairs_in, 16)
            for k in range(KT):
                sp.dma_start(W_in[:, k, :].rearrange("p (h d) -> p h d", h=H),
                             a["W"][:, k * P:(k + 1) * P, :].rearrange("h p d -> p h d")).then_inc(wh_in, 16)
            for u, name in enumerate(("a1", "a2")):
                sp.dma_start(a_in[u], a[name].rearrange("h d -> (h d)").partition_broadcast(P)).then_inc(wh_in, 16)
            sp.dma_start(W1r, a["W1"].rearrange("(o p) n -> p o n", p=P)).then_inc(w_in, 16)
            sp.dma_start(W2r, a["W2"]).then_inc(w_in, 16)
            sp.dma_start(W3r, a["W3"].rearrange("(o p) n -> p o n", p=P)).then_inc(w_in, 16)
            sp.dma_start(W4r, a["W4"].rearrange("(o p) n -> p o n", p=P)).then_inc(w_in, 16)
            sp.dma_start(Wqr, a["Wq"].rearrange("(o p) n -> p o n", p=P)).then_inc(w_in, 16)
            sp.dma_start(Wkr, a["Wk"].rearrange("(o p) n -> p o n", p=P)).then_inc(w_in, 16)
            for u in range(2):
                sp.dma_start(x_in[u], a["x"][u * P:(u + 1) * P, :]).then_inc(x_in_s[u], 16)
            for c, name, n in ((0, "b1", 2), (2, "b2", 1), (3, "b3", 2)):
                for o in range(n):
                    sp.dma_start(bcol[:, c + o:c + o + 1],
                                 a[name][o * P:(o + 1) * P].unsqueeze(1)).then_inc(small_in, 16)
            sp.dma_start(b4_row[:, :], a["b4"].partition_broadcast(P)).then_inc(b4_in_s, 16)
            for w, name in enumerate(("bq", "bk")):
                sp.dma_start(bqk[:, w, :], a[name].partition_broadcast(P)).then_inc(bqk_in, 16)
            for u in range(2):
                sp.dma_start(adj_raw[u], a["adj"][u * P:(u + 1) * P, :]).then_inc(adj_in[u], 16)
            sp.wait_ge(f_row_ready, 1)
            sp.dma_start(f_dram, f_row).then_inc(f_out, 16)
            sp.wait_ge(f_out, 16)
            sp.dma_start(pair_rows, f_dram.rearrange("t e -> (t e)").partition_broadcast(P)).then_inc(f_in, 16)
            with sp.Fori(1, (NT) // 2) as i_:
                i = i_ * 2
                for u in range(2):
                    sp.wait_ge(xT_ps, i + (u - 1))
                    sp.dma_start(x_in[u], a["x"][ds((i + u) * P, P), :]).then_inc(x_in_s[u], 16)
            with sp.Fori(1, (NT) // 2) as i_:
                i = i_ * 2
                for u in range(2):
                    sp.wait_ge(adj_cast, i + (u - 1))
                    sp.dma_start(adj_raw[u], a["adj"][ds((i + u) * P, P), :]).then_inc(adj_in[u], 16)
            sp.wait_ge(r_ready, 1)
            r_view = r_dram.rearrange("(g b u) n -> g u b n", b=NB, u=2)
            for h in range(H):
                sp.dma_start(r_view[h // 2, h % 2].unsqueeze(0),
                             s_row[h:h + 1, :].rearrange("p (b n) -> p b n", b=NB)).then_inc(r_out, 16)
            sp.wait_ge(r_out, 16 * H)
            for u in range(2):
                sp.dma_start(r_b[u], r_dram[u, :].partition_broadcast(P)).then_inc(r_in[u], 16)
            for k in range(4):
                sp.dma_start(d_dram[(60 + k) * P * BLK:(61 + k) * P * BLK, :].rearrange("(p m n) o -> p m (n o)", m=4, n=P),
                             zero[:, 0:P].unsqueeze(1).broadcast_to([P, 4, P])).then_inc(zeroed, 16)
            with sp.Fori(0, (NB * H - 2) // 2) as g_:
                g = g_ * 2
                for u in range(2):
                    sp.wait_ge(P_ready, (g + (u + 1)) * NT)
                    sp.dma_start(r_b[u], r_dram[ds(g + (u + 2), 1), :].rearrange("o n -> (o n)").partition_broadcast(P)
                                 ).then_inc(r_in[u], 16)
                for k in range(4):
                    sp.dma_start(d_dram[ds((g * 2 + k) * (P * BLK), P * BLK), :].rearrange("(p m n) o -> p m (n o)", m=4, n=P),
                                 zero[:, 0:P].unsqueeze(1).broadcast_to([P, 4, P])).then_inc(zeroed, 16)
            sp.wait_ge(us_ready, 2 * H)
            sp.dma_start(xs, a["x"].rearrange("(t p) n -> p t n", p=P)).then_inc(x_res_in, 16)
            sp.wait_ge(c_row_ready, 1)
            sp.dma_start(c_dram, c_row).then_inc(c_out, 16)
            sp.wait_ge(c_out, 16)
            sp.dma_start(c_b, c_dram.rearrange("t p -> (t p)").partition_broadcast(P)).then_inc(c_in, 16)
            sp.wait_ge(d_out, 16 * ET)
            dj = d_dram[0:N * N, :].rearrange("(j i) o -> j (i o)", i=N)
            with sp.Fori(0, NB) as b:
                with sp.Fori(0, NT // 4) as jq:
                    for u in range(4):
                        sp.wait_ge(A_ready, b * NT + jq * 4 + (u + 1))
                        sp.dma_start(d_in[u], dj[ds((jq * 4 + u) * P, P), ds(b * BLK, BLK)]).then_inc(d_slot[u], 16)
            for w in range(2):
                sp.wait_ge(qk_dma[w], 16 * (NT + 1))
            for t in range(TI):
                sp.wait_ge(out_dma[t], 16 * (NB + 1))

        @block.gpsimd
        def _(pool):
            nc.gpsimd.memset(pairs[:, :], 0).then_inc(consts, 1)
            nc.gpsimd.memset(zero[:, :], 0.0).then_inc(consts, 1)
            nc.gpsimd.memset(ones[:, :], 1.0).then_inc(consts, 1)
            nc.gpsimd.memset(cst[:, 0:1], EPS).then_inc(consts, 1)
            nc.gpsimd.memset(cst[:, 1:2], LOW).then_inc(consts, 1)
            nc.gpsimd.memset(cst[:, 2:3], DIAG).then_inc(consts, 1)
            nc.gpsimd.memset(ident[:, :], 0.0).then_inc(consts, 1)
            nc.gpsimd.memset(tri, 1.0).then_inc(consts, 1)
            pool.wait_ge(consts, 8)
            nc.gpsimd.affine_select(ident[:, :], ident[:, :], [[-1, P]], ALU.not_equal, 1.0,
                                    base=0, channel_multiplier=1).then_inc(consts, 1)
            nc.gpsimd.affine_select(tri, tri, [[-1, P]], ALU.is_gt, 0.0,
                                    base=0, channel_multiplier=1).then_inc(consts, 1)
            nc.gpsimd.iota(biota[:, :], [[1, P]], 0, 0, allow_small_or_imprecise_dtypes=True).then_inc(consts, 1)
            nc.gpsimd.iota(eid[:, :], [[1, ET]], 0, ET).then_inc(consts, 1)
            pool.wait_ge(consts, 12)
            nc.gpsimd.tensor_copy(identb[:, :], ident[:, :]).then_inc(consts, 1)
            for s, n in credits:
                pool.sem_inc(s, n)
            pool.wait_ge(idx_ready, 1)
            pool.wait_ge(consts, 13)
            for t in range(ET):
                if t:
                    pool.wait_ge(t_out, 16 * t)
                nc.gpsimd.indirect_dma_start(
                    out=t_dram, out_offset=bass.IndirectOffsetOnAxis(ap=tidx[:, t:t + 1], axis=0),
                    in_=eid[:, t:t + 1], in_offset=None).then_inc(t_out, 16)
            pool.wait_ge(t_out, 16 * ET)
            adj_flat = a["adj"].rearrange("i (j o) -> (i j) o", o=1)
            for t in range(ET):
                nc.gpsimd.indirect_dma_start(
                    out=t_got[:, t:t + 1], out_offset=None, in_=t_dram,
                    in_offset=bass.IndirectOffsetOnAxis(ap=tidx[:, t:t + 1], axis=0)).then_inc(t_in, 16)
                nc.gpsimd.indirect_dma_start(
                    out=adj_got[:, t:t + 1], out_offset=None, in_=adj_flat,
                    in_offset=bass.IndirectOffsetOnAxis(ap=fn_i[:, t:t + 1], axis=0)).then_inc(aj_in, 16)
            for w in range(2):
                pool.wait_ge(qk_dma[w], 16 * (NT + 1))
            pool.wait_ge(x1_kept, NT + 2)
            for t in range(ET):
                if t >= RING:
                    pool.wait_ge(rows_used, t - RING + 1)
                nc.gpsimd.indirect_dma_start(
                    out=k_rows[t % RING], out_offset=None, in_=k_dram,
                    in_offset=bass.IndirectOffsetOnAxis(ap=obj_i[:, t:t + 1], axis=0)).then_inc(k_in[t % RING], 16)
                nc.gpsimd.indirect_dma_start(
                    out=q_rows[t % RING], out_offset=None, in_=q_dram,
                    in_offset=bass.IndirectOffsetOnAxis(ap=sub_i[:, t:t + 1], axis=0)).then_inc(q_in[t % RING], 16)
            pool.wait_ge(didx_ready, 1)
            pool.wait_ge(zeroed, 16 * 64)
            for t in range(ET):
                if t % CH == 0:
                    pool.wait_ge(v_ready, 2 + t // CH + 1)
                nc.gpsimd.indirect_dma_start(
                    out=d_dram, out_offset=bass.IndirectOffsetOnAxis(ap=didx[:, t:t + 1], axis=0),
                    in_=v_e[:, t:t + 1], in_offset=None).then_inc(d_out, 16)

        @block.tensor
        def _(pe):
            mm, tr = nc.tensor.matmul, nc.tensor.transpose
            pe.wait_ge(consts, 13)
            pe.wait_ge(fn_ready, 1)
            tr(ps[0:ET, 7, 0:P], fn_f, ident[:, :]).then_inc(fn_ps, 1)
            pe.wait_ge(w_in, 16 * 6)
            for g in range(13):
                pe.wait_ge(wt_sb, g + 1)
                for k in range(4):
                    last = tr(ps[:, g % 2, k * P:(k + 1) * P], chunks[4 * g + k], ident[:, :])
                last.then_inc(wt_ps, 1)
            pe.wait_ge(wa_ready, 2 * KT)
            pe.wait_ge(wh_in, 16 * 6)
            pe.wait_ge(f_row_ready, 1)
            with pe.Fori(0, (NT) // 2) as i_:
                i = i_ * 2
                for u in range(2):
                    pe.wait_ge(x_in_s[u], i * 8 + 16)
                    pe.wait_ge(xT_sb, i + (u + 1))
                    for k in range(KT):
                        last = tr(ps[:, 2 + u, k * P:(k + 1) * P], x_in[u][:, k * P:(k + 1) * P], ident[:, :])
                    last.then_inc(xT_ps, 1)
                for u in range(2):
                    pe.wait_ge(xT_sb, i + (u + 3))
                    pe.wait_ge(wh_sb, i + (u + 1))
                    pe.wait_ge(e_sb, i + (u + 1))
                    for k in range(KT):
                        mm(ps[:, 4 + u, :], xT[u][:, k * P:(k + 1) * P], W_in[:, k, :], start=(k == 0), stop=(k == KT - 1))
                    for k in range(KT):
                        last = mm(ps[:, 6 + u, 0:2 * H], xT[u][:, k * P:(k + 1) * P], Wa[:, k, :],
                                  start=(k == 0), stop=(k == KT - 1))
                    last.then_inc(wh_ps, 1)
            pe.wait_ge(e_sb, 2 + NT)
            pe.wait_ge(wt_sb, 2 + 13)
            for g in range(4):
                if g >= 2:
                    pe.wait_ge(rows_sb, 2 * (g - 1))
                for w in range(2):
                    for k in range(4):
                        last = tr(ps[0:H, 2 * (g % 2) + w, k * P:(k + 1) * P],
                                  e_col[:, 4 * g + k, w * H:(w + 1) * H], ident[:, :])
                last.then_inc(rows_ps, 1)
            pe.wait_ge(d_ready, 1)
            pe.wait_ge(wh_sb, 2 + NT)
            mm(ps[:, 4, 0:H], ones[:, :], d_diag[:, :], start=True, stop=True).then_inc(d_ps, 1)
            with pe.Fori(0, (NT) // 2) as i_:
                i = i_ * 2
                for u in range(2):
                    pe.wait_ge(adj_cast, i + (u + 1))
                    for half in range(2):
                        pe.wait_ge(adj_sb, (i + u) * 2 + (half + 2))
                        for k in range(8):
                            j = half * 8 + k
                            last = tr(psb[:, 6 + half, k * P:(k + 1) * P], adj_b[u][:, j * P:(j + 1) * P], identb[:, :])
                        last.then_inc(adj_ps, 1)
            pe.wait_ge(rows_sb, 8)
            for k in range(4):
                last = mm(ps[:, 1, k * P:(k + 1) * P], ones[:, :], ones[:, :], start=True, stop=True)
            last.then_inc(bank_set, 1)
            with pe.Fori(0, H // 2) as hp:
                with pe.Fori(0, NB) as b:
                    for u in range(2):
                        g = (hp * NB + b) * 2 + u
                        pe.wait_ge(att_ev, g + 1)
                        pe.wait_ge(us_ready, hp * 4 + (2 * u + 2))
                        for j in range(NT):
                            pe.wait_ge(P_ready, g * NT + (j + 1))
                            mm(ps[:, u, :], Us[u][:, j, :], Pw[j % NP_BUF], start=(j == 0),
                               stop=(j == NT - 1)).then_inc(P_free, 1)
            pe.wait_ge(wt_sb, 2 + 13)
            with pe.Fori(0, NB // 2) as b2:
                for v in range(2):
                    b = b2 * 2 + v
                    pe.wait_ge(enc_ready, b * 4 + 6)
                    for o in range(2):
                        pe.wait_ge(z1_sb, b * 2 + (o + 1))
                        for k in range(KT):
                            last = mm(ps[:, 2 + 2 * v + o, :], W1T[k][:, o * P:(o + 1) * P],
                                      encT[:, k, ds(b * BLK, BLK)], start=(k == 0), stop=(k == KT - 1))
                        last.then_inc(z1_ps, 1)
            for b in range(NB):
                pe.wait_ge(z1_sb, 4 + 2 * b + 2)
                for k in range(2):
                    last = mm(ps[:, 6 + b % 2, :], W2T[k], z1T[:, k, b * BLK:(b + 1) * BLK], start=(k == 0), stop=(k == 1))
                last.then_inc(z2_ps, 1)
                if b >= 1:
                    pe.wait_ge(z2_sb, b)
            pe.wait_ge(z1_sb, 4 + 2 * NB)
            for b in range(NB):
                pe.wait_ge(z2_sb, b + 1)
                if b == 0:
                    pe.wait_ge(z2_sb, NB)
                if b >= 2:
                    pe.wait_ge(z3_sb, 2 * (b - 1))
                for o in range(2):
                    mm(ps[:, 2 + 2 * (b % 2) + o, :], W3T[:, o * P:(o + 1) * P], z2T[:, b * BLK:(b + 1) * BLK],
                       start=True, stop=True).then_inc(z3_ps, 1)
            for t in range(NT):
                if t % TI == 0:
                    pe.wait_ge(z3_sb, 2 * (t // TI) + 2)
                if t >= 2:
                    pe.wait_ge(y_ready, t - 1)
                for k in range(2):
                    last = mm(ps[:, 6 + t % 2, :], z3T[:, k, t * P:(t + 1) * P], W4T[k], start=(k == 0), stop=(k == 1))
                last.then_inc(z4_ps, 1)
            pe.wait_ge(y_ready, NT)
            pe.wait_ge(z3_sb, 8)
            with pe.Fori(0, NT // 2) as t2:
                for u in range(2):
                    t = t2 * 2 + u
                    pe.wait_ge(x1_ready, t + 3)
                    pe.wait_ge(x1T_sb, t + 1)
                    for k in range(KT):
                        last = tr(ps[:, 2 + u, k * P:(k + 1) * P], y[u][:, k * P:(k + 1) * P], ident[:, :])
                    last.then_inc(x1T_ps, 1)
                    pe.wait_ge(x1T_sb, t + 3)
                    for w, wT in enumerate((WqT, WkT)):
                        pe.wait_ge(qk_sb, t * 2 + (w + 1))
                        for k in range(KT):
                            last = mm(ps[:, 4 + w, :], x1T[u][:, k * P:(k + 1) * P], wT[k],
                                      start=(k == 0), stop=(k == KT - 1))
                        last.then_inc(qk_ps, 1)
            pe.wait_ge(gm_ready, 1)
            tr(ps[0:1, 2, 0:P], glob[:, 0:1], ident[:, :]).then_inc(gm_ps, 1)
            pe.wait_ge(g1_ready, 1)
            mm(ps[:, 3, 0:1], ones[0:1, :], glob[0:1, 1:2], start=True, stop=True).then_inc(g_all, 1)
            pe.wait_ge(beta_ready, 1)
            mm(ps[:, 0, 0:P], zero[:, 0:P], zero[:, 0:P], start=True, stop=False, skip_group_check=True)
            with pe.Fori(0, (CHUNKS) // 2) as c_:
                c = c_ * 2
                for u in range(2):
                    pe.wait_ge(oh_ready, (c + u) * 2 + 2)
                    pe.wait_ge(obT_sb, c + (u + 1))
                    for k in range(CH):
                        mm(ps[:, 0, 0:P], Ob[u][:, k, :], Wc[u][:, k * P:(k + 1) * P], start=False, stop=False,
                           skip_group_check=True)
                        last = tr(ps[:, 2 + 2 * u + k // 4, (k % 4) * P:(k % 4 + 1) * P], Ob[u][:, k, :], ident[:, :])
                    last.then_inc(oh_used, 1)
            pe.wait_ge(m_ready, 1)
            pe.wait_ge(obT_sb, 2 + CHUNKS)
            with pe.Fori(0, (CHUNKS) // 2) as c_:
                c = c_ * 2
                for u in range(2):
                    pe.wait_ge(mg_sb, c + (u + 1))
                    for k in range(CH):
                        last = mm(ps[:, 2 + 2 * u + k // 4, (k % 4) * P:(k % 4 + 1) * P],
                                  ObT[:, ds((c + u) * CH + k, 1), :].rearrange("p o e -> p (o e)"), m_b,
                                  start=(k % 4 == 0), stop=True, skip_group_check=True)
                    last.then_inc(mg_ps, 1)
            mm(ps[:, 1, 0:144], zero[:, 0:P], zero[:, 0:144], start=True, stop=False, skip_group_check=True)
            with pe.Fori(0, (CHUNKS) // 2) as c_:
                c = c_ * 2
                for u in range(2):
                    pe.wait_ge(oh_ready, 2 * CHUNKS + (c + u) * 2 + 2)
                    for k in range(CH):
                        last = mm(ps[:, 1, 0:144], Ob[u][:, k, :], Wc[u][:, k * 144:(k + 1) * 144], start=False,
                                  stop=False, skip_group_check=True)
                    last.then_inc(oh_used, 1)
            pe.wait_ge(c_ready, 1)
            tr(ps[0:NT, 0, 0:P], c_col, ident[:, :]).then_inc(c_ps, 1)
            pe.wait_ge(t9_ready, 1)
            pe.wait_ge(mg_sb, 2 + CHUNKS)
            with pe.Fori(0, (CHUNKS) // 2) as c_:
                c = c_ * 2
                for u in range(2):
                    pe.wait_ge(v_ready, c + (u + 1))
                    for k in range(CH):
                        for part in range(3):
                            last = mm(ps[:, 2 + 3 * u + k // 3, (k % 3) * 144:(k % 3 + 1) * 144],
                                      ObT[:, ds((c + u) * CH + k, 1), :].rearrange("p o e -> p (o e)"), Tb[part],
                                      start=(k % 3 == 0 and part == 0), stop=(part == 2), skip_group_check=True)
                    last.then_inc(g9_ps, 1)
            pe.wait_ge(x1_kept, NT + 2)
            pe.wait_ge(v_ready, 2 + CHUNKS)
            pe.wait_ge(c_row_ready, 1)
            with pe.Fori(0, (NB) // 2) as b_:
                b = b_ * 2
                for v in range(2):
                    pe.wait_ge(o_ev, (b + v) * 4 + 4)
                    for j in range(NT):
                        pe.wait_ge(A_ready, (b + v) * NT + (4 + j + 1))
                        for t in range(TI):
                            last = mm(ps[:, 4 * v + t, :], A[j % 4][:, t * P:(t + 1) * P], xs[:, j, :],
                                      start=(j == 0), stop=(j == NT - 1))
                        last.then_inc(A_free, 1)

        @block.scalar
        def _(act):
            fn = nc.scalar.activation
            act.wait_ge(fn_ps, 1)
            nc.scalar.copy(f_row, ps[0:ET, 7, 0:P]).then_inc(f_row_ready, 1)
            for g in range(13):
                act.wait_ge(wt_ps, g + 1)
                nc.scalar.copy(WT[:, 4 * g:4 * g + 4, :].rearrange("p t n -> p (t n)"), ps[:, g % 2, :]).then_inc(wt_sb, 1)
            with act.Fori(0, (NT) // 2) as i_:
                i = i_ * 2
                for u in range(2):
                    act.wait_ge(xT_ps, i + (u + 1))
                    act.wait_ge(wh_ps, i + (u + 1))
                    nc.scalar.copy(xT[u], ps[:, 2 + u, :]).then_inc(xT_sb, 1)
                for u in range(2):
                    act.wait_ge(wh_ps, i + (u + 3))
                    nc.scalar.copy(e_col[:, ds(i + u, 1), :], ps[:, 6 + u, 0:2 * H]).then_inc(e_sb, 1)
            for g in range(4):
                act.wait_ge(rows_ps, g + 1)
                nc.scalar.copy(s_row[:, g * BLK:(g + 1) * BLK], ps[0:H, 2 * (g % 2), :]).then_inc(rows_sb, 1)
                nc.scalar.copy(d_row[:, g * BLK:(g + 1) * BLK], ps[0:H, 2 * (g % 2) + 1, :]).then_inc(rows_sb, 1)
            with act.Fori(0, (NT) // 2) as i_:
                i = i_ * 2
                for u in range(2):
                    act.wait_ge(adj_in[u], i * 8 + 16)
                    act.wait_ge(adj_sb, (i + u) * 2 + 1)
                    fn(adj_b[u], adj_raw[u], ACT.Copy, accum_out=adj_sum[:, ds(i + u, 1)]).then_inc(adj_cast, 1)
            act.wait_ge(r_arg, 1)
            fn(s_row, s_row, ACT.Exp, scale=0.8).then_inc(r_ready, 1)
            act.wait_ge(shift_ready, 1)
            fn(q_col[:, :, :], e_col[:, :, H:2 * H], ACT.Exp, scale=-0.8).then_inc(ed_ready, 1)
            fn(ED[:, :, :], e_col[:, :, H:2 * H], ACT.Exp).then_inc(ed_ready, 1)
            act.wait_ge(u_ready, NT)
            act.wait_ge(r_out, 16 * H)

            def sources(hp, u):
                h = hp * 2 + u
                nc.scalar.copy(Us[u][:, :, 0:DH], U[:, :, ds(h, 1), :].rearrange("p j o d -> p (j o) d")).then_inc(us_ready, 1)
                nc.scalar.copy(Us[u][:, :, DH:P], ED[:, :, ds(h, 1)].broadcast_to([P, NT, DH])).then_inc(us_ready, 1)

            for u in range(2):
                sources(0, u)
            with act.Fori(1, H // 2) as hp:
                for u in range(2):
                    act.wait_ge(P_free, hp * (NB * 2 * NT) + (NP_BUF + (u - 1) * NT))
                    sources(hp, u)
            act.wait_ge(small_in, 16 * 5)
            with act.Fori(0, NB) as b:
                for k in range(KT):
                    act.wait_ge(min_ready, b * 4 + (k + 1))
                    fn(ebuf[:, k % 2, :], ebuf[:, k % 2, :], ACT.Exp).then_inc(exp_ready, 1)
            with act.Fori(0, NB // 2) as b2:
                for v in range(2):
                    b = b2 * 2 + v
                    for o in range(2):
                        act.wait_ge(z1_ps, b * 2 + (o + 1))
                        fn(z1T[:, o, ds(b * BLK, BLK)], ps[:, 2 + 2 * v + o, :], ACT.Relu,
                           bias=bcol[:, o:o + 1]).then_inc(z1_sb, 1)
            for b in range(NB):
                act.wait_ge(z2_ps, b + 1)
                fn(z2T[:, b * BLK:(b + 1) * BLK], ps[:, 6 + b % 2, :], ACT.Relu, bias=bcol[:, 2:3]).then_inc(z2_sb, 1)
            for b in range(NB):
                for o in range(2):
                    act.wait_ge(z3_ps, b * 2 + o + 1)
                    fn(z3T[:, o, b * BLK:(b + 1) * BLK], ps[:, 2 + 2 * (b % 2) + o, :], ACT.Relu,
                       bias=bcol[:, 3 + o:4 + o]).then_inc(z3_sb, 1)
            act.wait_ge(var_ready, NT)
            fn(rstd[:, :], var[:, :, 1], ACT.Ln, bias=cst[:, 0:1]).then_inc(ln_ready, 1)
            act.wait_ge(ln_ready, 1)
            fn(rstd[:, :], rstd[:, :], ACT.Exp, scale=-0.5).then_inc(rstd_ready, 1)
            with act.Fori(0, NT // 2) as t2:
                for u in range(2):
                    t = t2 * 2 + u
                    act.wait_ge(x1T_ps, t + 1)
                    nc.scalar.copy(x1T[u], ps[:, 2 + u, :]).then_inc(x1T_sb, 1)
                    nc.scalar.copy(xs[:, ds(t, 1), :], y[u]).then_inc(x1_kept, 1)
                    for w, dst in enumerate((q_dram, k_dram)):
                        act.wait_ge(qk_sb, t * 2 + (w + 3))
                        act.dma_start(dst[ds(t * P, P), :], qk_out[w]).then_inc(qk_dma[w], 16)
            act.wait_ge(beta_ready, 1)
            fn(e1, e1, ACT.Exp, scale=glob[:, 3:4], bias=cst[:, 1:2]).then_inc(e1_ready, 1)
            with act.Fori(0, (CHUNKS) // 2) as c_:
                c = c_ * 2
                for u in range(2):
                    act.wait_ge(oh_used, c + (u + 3))
                    nc.scalar.copy(ObT[:, ds((c + u) * CH, CH), :].rearrange("p t e -> p (t e)"),
                                   ps[:, 2 + 2 * u:4 + 2 * u, :].rearrange("p b n -> p (b n)")).then_inc(obT_sb, 1)
            act.wait_ge(lse_arg, 1)
            fn(base, base, ACT.Ln).then_inc(lse_ready, 1)
            act.wait_ge(m_ready, 1)
            fn(dterm, Z, ACT.Exp, scale=-1.0, bias=cst[:, 2:3]).then_inc(tabs_ready, 1)
            fn(base, Z, ACT.Exp, scale=-1.0).then_inc(tabs_ready, 1)
            act.wait_ge(p_arg, 1)
            fn(m_e, m_e, ACT.Exp).then_inc(p_exp, 1)
            act.wait_ge(c_ps, 1)
            nc.scalar.copy(c_row, ps[0:NT, 0, 0:P]).then_inc(c_row_ready, 1)
            with act.Fori(0, NB) as b:
                for t in range(TI):
                    act.wait_ge(o_var, b * 4 + (t + 1))
                    fn(rstd[:, t:t + 1], var[:, t, 1:2], ACT.Ln, bias=cst[:, 0:1]).then_inc(o_ln, 1)
                    act.wait_ge(o_ln, b * 4 + (t + 1))
                    fn(rstd[:, t:t + 1], rstd[:, t:t + 1], ACT.Exp, scale=-0.5).then_inc(o_rstd, 1)
                for t in range(TI):
                    act.wait_ge(o_norm, b * 4 + (t + 1))
                    act.dma_start(a["out"][ds((b * 4 + t) * P, P), :], o_buf[t]).then_inc(out_dma[t], 16)

        @block.vector
        def _(dve):
            v = nc.vector
            own = [0]

            def own_step(ins):
                own[0] += 1
                ins.then_inc(dve_own, 1)
                dve.wait_ge(dve_own, own[0])

            dve.wait_ge(pairs_in, 16)
            dve.wait_ge(consts, 13)
            pv = pairs[:, :].rearrange("p (t c) -> p t c", c=2)
            v.tensor_copy(sub_i[:, :], pv[:, :, 0]).then_inc(dve_own, 1)
            v.tensor_copy(obj_i[:, :], pv[:, :, 1]).then_inc(dve_own, 1)
            v.tensor_copy(trash_f, eid[:, :]).then_inc(dve_own, 1)
            v.tensor_copy(sub_f, pv[:, :, 0]).then_inc(dve_own, 1)
            own[0] = 4
            own_step(v.tensor_copy(obj_f, pv[:, :, 1]))
            v.tensor_scalar(ok_f, trash_f, float(EDGES), None, ALU.is_lt).then_inc(dve_own, 1)
            own[0] += 1
            own_step(v.tensor_scalar(ft_f, obj_f, float(N), None, ALU.mult))
            own_step(v.tensor_tensor(ft_f, ft_f, sub_f, ALU.add))
            own_step(v.tensor_scalar(fn_f, sub_f, float(N), None, ALU.mult))
            v.tensor_tensor(fn_f, fn_f, obj_f, ALU.add).then_inc(fn_ready, 1)
            dve.wait_ge(fn_ready, 1)
            own_step(v.tensor_copy(fn_i[:, :], fn_f))
            own_step(v.tensor_scalar(trash_f, trash_f, float(TRASH), None, ALU.add))
            dve.wait_ge(wh_in, 16 * 6)
            for k in range(KT):
                for w in range(2):
                    own_step(v.tensor_tensor(wa_tmp, W_in[:, k, :], a_in[w], ALU.mult))
                    v.tensor_reduce(Wa[:, k, w * H:(w + 1) * H], wa_tmp.rearrange("p (h d) -> p h d", h=H),
                                    AX.X, ALU.add).then_inc(wa_ready, 1)
                    dve.wait_ge(wa_ready, 2 * k + w + 1)
            dve.wait_ge(f_in, 16)
            for t in range(ET):
                own_step(v.scalar_tensor_tensor(out=junk0, in0=pair_rows[:, t * P:(t + 1) * P],
                                                scalar=fn_f[:, t:t + 1], in1=tri, op0=ALU.is_equal, op1=ALU.mult,
                                                accum_out=live[:, t:t + 1]))
            own_step(v.tensor_scalar(live, live, 0.5, None, ALU.is_lt))
            own_step(v.tensor_tensor(ok_f, ok_f, live, ALU.mult))
            own_step(v.tensor_tensor(live, fn_f, trash_f, ALU.subtract))
            own_step(v.tensor_tensor(live, live, ok_f, ALU.mult))
            own_step(v.tensor_tensor(live, live, trash_f, ALU.add))
            v.tensor_copy(tidx[:, :], live).then_inc(idx_ready, 1)
            dve.wait_ge(wt_sb, 2 + 13)
            with dve.Fori(0, (NT) // 2) as i_:
                i = i_ * 2
                for u in range(2):
                    dve.wait_ge(wh_ps, i + (u + 3))
                    v.tensor_copy(U[:, ds(i + u, 1), :, :].rearrange("p o h d -> p (o h) d"),
                                  ps[:, 4 + u, :].rearrange("p (h d) -> p h d", h=H)).then_inc(wh_sb, 1)
            dve.wait_ge(rows_sb, 8)
            own_step(v.tensor_reduce(d_lim[:, 0:1], d_row, AX.X, ALU.max))
            own_step(v.tensor_reduce(d_lim[:, 1:2], d_row, AX.X, ALU.min))
            own_step(v.tensor_tensor(d_lim[:, 2:3], d_lim[:, 0:1], d_lim[:, 1:2], ALU.subtract))
            v.tensor_scalar(d_diag[:, :], ident[0:H, 0:H], d_lim[:, 0:1], None, ALU.mult).then_inc(d_ready, 1)
            own_step(v.tensor_scalar(s_row, s_row, d_lim[:, 0:1], 0.0, ALU.add, ALU.max))
            v.tensor_scalar(s_row, s_row, d_lim[:, 2:3], None, ALU.min).then_inc(r_arg, 1)
            dve.wait_ge(d_ps, 1)
            v.tensor_tensor(e_col[:, :, H:2 * H], e_col[:, :, H:2 * H],
                            ps[:, 4, 0:H].unsqueeze(1).broadcast_to([P, NT, H]), ALU.subtract).then_inc(shift_ready, 1)
            with dve.Fori(0, (NT) // 2) as i_:
                i = i_ * 2
                for u in range(2):
                    dve.wait_ge(adj_cast, i + (u + 1))
                    dve.wait_ge(adj_dg, i + (u + 1))
                    v.scalar_tensor_tensor(out=junk0, in0=adj_b[u].rearrange("p (j n) -> p j n", n=P)[:, ds(i + u, 1), :]
                                           .rearrange("p o n -> p (o n)"), scalar=1.0, in1=identb[:, :], op0=ALU.mult,
                                           op1=ALU.mult, accum_out=adj_diag[:, ds(i + u, 1)]).then_inc(adj_dg, 1)
                    for half in range(2):
                        dve.wait_ge(adj_ps, (i + u) * 2 + (half + 1))
                        v.tensor_copy(adjT[:, half * 8:half * 8 + 8, ds((i + u) * P, P)],
                                      psb[:, 6 + half, :].rearrange("p (j n) -> p j n", n=P)).then_inc(adj_sb, 1)
            dve.wait_ge(ed_ready, 2)
            for j in range(NT):
                v.tensor_tensor(U[:, j, :, :], U[:, j, :, :],
                                ED[:, j, :].unsqueeze(2).broadcast_to([P, H, DH]), ALU.mult).then_inc(u_ready, 1)
            dve.wait_ge(bqk_in, 32)
            dve.wait_ge(bank_set, 1)

            with dve.Fori(0, H // 2) as hp:
                with dve.Fori(0, NB) as b:
                    m = hp * NB + b
                    for u in range(2):
                        g = m * 2 + u
                        dve.wait_ge(r_in[u], m * 16 + 16)
                        for j in range(NT):
                            if j == NP_BUF + 1:
                                dve.wait_ge(P_free, g * NT + NP_BUF)
                                v.reciprocal(rden[:, :], ps[DH:P, 1 - u, :]).then_inc(rden_ready, 1)
                                dve.wait_ge(rden_ready, g + 1)
                                v.tensor_tensor(enc_all[DH * (1 - u):DH * (2 - u), ds((m + u) * BLK, BLK)],
                                                ps[0:DH, 1 - u, :], rden[:, :], ALU.mult).then_inc(att_ev, 1)
                            dve.wait_ge(P_free, g * NT + (j + 1))
                            v.scalar_tensor_tensor(out=Pw[j % NP_BUF], in0=r_b[u], scalar=q_col[:, j, ds(hp * 2 + u, 1)],
                                                   in1=adjT[:, j, ds(b * BLK, BLK)], op0=ALU.max,
                                                   op1=ALU.mult).then_inc(P_ready, 1)
            dve.wait_ge(P_free, NB * H * NT + NP_BUF)
            v.reciprocal(rden[:, :], ps[DH:P, 1, :]).then_inc(rden_ready, 1)
            dve.wait_ge(rden_ready, NB * H + 1)
            v.tensor_tensor(enc_all[DH:P, NB * KT * BLK:NB * KT * BLK + BLK], ps[0:DH, 1, :], rden[:, :],
                            ALU.mult).then_inc(att_ev, 1)
            dve.wait_ge(att_ev, NB * H + 2)
            with dve.Fori(0, NB) as b:
                for k in range(KT):
                    dve.wait_ge(enc_ready, b * 4 + (k + 1))
                    v.tensor_scalar(ebuf[:, k % 2, :], encT[:, k, ds(b * BLK, BLK)], 0.0, None, ALU.min).then_inc(min_ready, 1)
                    if k % 2:
                        for s in (k - 1, k):
                            dve.wait_ge(exp_ready, b * 4 + (s + 1))
                            v.scalar_tensor_tensor(out=encT[:, s, ds(b * BLK, BLK)], in0=ebuf[:, s % 2, :], scalar=-1.0,
                                                   in1=encT[:, s, ds(b * BLK, BLK)], op0=ALU.add,
                                                   op1=ALU.max).then_inc(enc_ready, 1)
            dve.wait_ge(b4_in_s, 16)
            dve.wait_ge(x_res_in, 16)
            v.tensor_tensor(xs, xs, b4_row[:, :].unsqueeze(1).broadcast_to([P, NT, F]), ALU.add).then_inc(b4_added, 1)
            dve.wait_ge(b4_added, 1)
            for t in range(NT):
                dve.wait_ge(z4_ps, t + 1)
                v.tensor_tensor(xs[:, t, :], ps[:, 6 + t % 2, :], xs[:, t, :], ALU.add).then_inc(y_ready, 1)
                dve.wait_ge(y_ready, t + 1)
                v.bn_stats(stats[:, t, :], xs[:, t, :]).then_inc(st_ready, 1)
            for t in range(NT):
                dve.wait_ge(st_ready, t + 1)
                v.bn_aggr(var[:, t, :], stats[:, t, :]).then_inc(var_ready, 1)
            dve.wait_ge(rstd_ready, 1)
            with dve.Fori(0, NT // 2) as t2:
                for u in range(2):
                    t = t2 * 2 + u
                    dve.wait_ge(x1_kept, t + 1)
                    v.tensor_scalar(y[u], xs[:, ds(t, 1), :].rearrange("p o n -> p (o n)"), var[:, ds(t, 1), 0:1].rearrange("p o n -> p (o n)"),
                                    rstd[:, ds(t, 1)], ALU.subtract, ALU.mult).then_inc(x1_ready, 1)
                    for w in range(2):
                        dve.wait_ge(qk_ps, t * 2 + (w + 1))
                        dve.wait_ge(qk_dma[w], t * 16 + 16)
                        v.tensor_tensor(qk_out[w], ps[:, 4 + w, :], bqk[:, w, :], ALU.add).then_inc(qk_sb, 1)

            dve.wait_ge(t_in, 16 * ET)
            dve.wait_ge(aj_in, 16 * ET)
            dve.wait_ge(x1_kept, NT + 2)
            own_step(v.tensor_tensor(live, t_got[:, :], eid[:, :], ALU.is_equal))
            own_step(v.tensor_tensor(live, live, ok_f, ALU.mult))
            own_step(v.tensor_tensor(ok_f, sub_f, obj_f, ALU.not_equal))
            own_step(v.tensor_tensor(live, live, ok_f, ALU.mult))
            own_step(v.tensor_scalar(ok_f, adj_got, 1.0, None, ALU.is_equal))
            own_step(v.tensor_tensor(live, live, ok_f, ALU.mult))
            own_step(v.tensor_tensor(ft_f, ft_f, trash_f, ALU.subtract))
            own_step(v.tensor_tensor(ft_f, ft_f, live, ALU.mult))
            own_step(v.tensor_tensor(ft_f, ft_f, trash_f, ALU.add))
            v.tensor_copy(didx[:, :], ft_f).then_inc(didx_ready, 1)
            own_step(v.tensor_scalar(t_got[:, :], sub_i[:, :], 7, None, ALU.logical_shift_right))
            own_step(v.tensor_copy(a_f, t_got[:, :]))
            own_step(v.scalar_tensor_tensor(out=b_f, in0=a_f, scalar=-float(P), in1=sub_f, op0=ALU.mult, op1=ALU.add))
            own_step(v.tensor_tensor(Oa, biota[:, 0:NT].unsqueeze(1).broadcast_to([P, ET, NT]),
                                     a_f.unsqueeze(2).broadcast_to([P, ET, NT]), ALU.is_equal))
            with dve.Fori(0, (ET) // RING) as t8_:
                t8 = t8_ * RING
                for u in range(RING):
                    dve.wait_ge(k_in[u], t8 * 2 + 16)
                    dve.wait_ge(q_in[u], t8 * 2 + 16)
                    v.tensor_tensor(prod[u % 2], k_rows[u], q_rows[u], ALU.mult).then_inc(prod_ready, 1)
                    dve.wait_ge(prod_ready, t8 + (u + 1))
                    v.tensor_reduce(att[:, ds(t8 + u, 1), :].rearrange("p o h -> p (o h)"),
                                    prod[u % 2].rearrange("p (h d) -> p h d", h=H), AX.X, ALU.add).then_inc(rows_used, 1)
            dve.wait_ge(rows_used, ET)
            own_step(v.scalar_tensor_tensor(out=att, in0=att, scalar=1.0 / float(DH) ** 0.5,
                                            in1=live.unsqueeze(2).broadcast_to([P, ET, H]), op0=ALU.mult, op1=ALU.mult))
            v.tensor_reduce(glob[:, 0:1], att_f, AX.X, ALU.max).then_inc(gm_ready, 1)
            own_step(v.tensor_scalar(e1, att_f, 0.0, None, ALU.max))
            dve.wait_ge(gm_ps, 1)
            own_step(v.tensor_reduce(glob[0:1, 2:3], ps[0:1, 2, 0:P], AX.X, ALU.max))
            v.tensor_scalar(glob[0:1, 1:2], glob[0:1, 2:3], 1.0, None, ALU.max).then_inc(g1_ready, 1)
            dve.wait_ge(g_all, 1)
            own_step(v.tensor_scalar(glob[:, 4:5], ps[:, 3, 0:1], 1.0 / SPAN, None, ALU.mult))
            v.reciprocal(glob[:, 3:4], glob[:, 4:5]).then_inc(beta_ready, 1)
            dve.wait_ge(e1_ready, 1)
            e1v = e1.rearrange("p (t h) -> p t h", h=H)

            def one_hot(c, u, vals, nh):
                v.tensor_tensor(Ob[u], biota[:, :].unsqueeze(1).broadcast_to([P, CH, P]),
                                b_f[:, ds(c * CH, CH)].unsqueeze(2).broadcast_to([P, CH, P]),
                                ALU.is_equal).then_inc(oh_ready, 1)
                weighted(c, u, vals, nh).then_inc(oh_ready, 1)

            def weighted(c, u, vals, nh):
                return v.tensor_tensor(Wc[u][:, 0:CH * NT * nh].rearrange("p (t k h) -> p t k h", t=CH, k=NT),
                                       vals[:, ds(c * CH, CH), :].unsqueeze(2).broadcast_to([P, CH, NT, nh]),
                                       Oa[:, ds(c * CH, CH), :].unsqueeze(3).broadcast_to([P, CH, NT, nh]), ALU.mult)

            with dve.Fori(0, (CHUNKS) // 2) as c_:
                c = c_ * 2
                for u in range(2):
                    dve.wait_ge(oh_used, c + (u + 1))
                    one_hot(c + u, u, e1v, H)
            dve.wait_ge(oh_used, 2 + CHUNKS)
            v.tensor_scalar(base, ps[:, 0, 0:P], float(2.718281828459045 ** LOW), None, ALU.add).then_inc(lse_arg, 1)
            dve.wait_ge(lse_ready, 1)
            own_step(v.tensor_scalar(Z, base, -LOW, glob[:, 4:5], ALU.add, ALU.mult))
            own_step(v.tensor_copy(m_b, Z))
            v.tensor_copy(Z, m_b).then_inc(m_ready, 1)
            with dve.Fori(0, (CHUNKS) // 2) as c_:
                c = c_ * 2
                for u in range(2):
                    dve.wait_ge(mg_ps, c + (u + 1))
                    m_prod = Wc[u][:, 0:CH * P]
                    v.tensor_tensor(m_prod.rearrange("p (t k h) -> p t k h", t=CH, k=NT),
                                    ps[:, 2 + 2 * u:4 + 2 * u, :].rearrange("p b n -> p (b n)").rearrange(
                                        "p (t k h) -> p t k h", t=CH, k=NT),
                                    Oa[:, ds((c + u) * CH, CH), :].unsqueeze(3).broadcast_to([P, CH, NT, H]),
                                    ALU.mult).then_inc(mg_sb, 1)
                    dve.wait_ge(mg_sb, c + (u + 3))
                    v.tensor_reduce(m_e.rearrange("p (t h) -> p t h", h=H)[:, ds((c + u) * CH, CH), :],
                                    m_prod.rearrange("p (t k h) -> p t h k", t=CH, k=NT), AX.X, ALU.add).then_inc(dve_loop, 1)
            dve.wait_ge(dve_loop, CHUNKS)
            v.tensor_tensor(m_e, att_f, m_e, ALU.subtract).then_inc(p_arg, 1)
            dve.wait_ge(p_exp, 1)
            own_step(v.tensor_tensor(p9[:, :, 0:H], m_e.rearrange("p (t h) -> p t h", h=H),
                                     live.unsqueeze(2).broadcast_to([P, ET, H]), ALU.mult))
            own_step(v.tensor_copy(p9[:, :, H], live))
            with dve.Fori(0, (CHUNKS) // 2) as c_:
                c = c_ * 2
                for u in range(2):
                    dve.wait_ge(oh_used, CHUNKS + (c + u) + 1)
                    one_hot(c + u, u, p9, 9)
            dve.wait_ge(oh_used, 2 + 2 * CHUNKS)
            dve.wait_ge(tabs_ready, 2)
            own_step(v.tensor_copy(seg, ps[:, 1, 0:144].rearrange("p (t h) -> p t h", h=9)))
            own_step(v.tensor_tensor(n_col, adj_sum[:, :], adj_diag[:, :], ALU.subtract))
            own_step(v.tensor_tensor(n_col, n_col, seg[:, :, H], ALU.subtract))
            b3, d3, z3 = (w.rearrange("p (t h) -> p t h", h=H) for w in (base, dterm, Z))
            own_step(v.tensor_tensor(z3, b3, n_col.unsqueeze(2).broadcast_to([P, NT, H]), ALU.mult))
            own_step(v.tensor_tensor(z3, z3, seg[:, :, 0:H], ALU.add))
            own_step(v.tensor_tensor(z3, z3, d3, ALU.add))
            own_step(v.reciprocal(Z, Z))
            own_step(v.tensor_scalar(T9[:, :, 0:H], z3, 1.0 / H, None, ALU.mult))
            own_step(v.tensor_tensor(b3, b3, T9[:, :, 0:H], ALU.mult))
            own_step(v.tensor_tensor(d3, d3, T9[:, :, 0:H], ALU.mult))
            v.tensor_reduce(c_col, b3, AX.X, ALU.add).then_inc(c_ready, 1)
            own_step(v.tensor_reduce(cd_col, d3, AX.X, ALU.add))
            dve.wait_ge(c_ready, 1)
            own_step(v.tensor_scalar(T9[:, :, H], c_col, -1.0, None, ALU.mult))
            own_step(v.tensor_tensor(n_col, c_col, adj_diag[:, :], ALU.mult))
            own_step(v.tensor_tensor(cd_col, cd_col, n_col, ALU.subtract))
            own_step(v.tensor_scalar(dcoef, cd_col, 1.0, None, ALU.add))
            own_step(v.tensor_copy(Tb[0], T9f))
            own_step(v.tensor_tensor(T_tmp, T9f, Tb[0], ALU.subtract))
            own_step(v.tensor_copy(Tb[1], T_tmp))
            own_step(v.tensor_tensor(T_tmp, T_tmp, Tb[1], ALU.subtract))
            v.tensor_copy(Tb[2], T_tmp).then_inc(t9_ready, 1)
            with dve.Fori(0, (CHUNKS) // 2) as c_:
                c = c_ * 2
                for u in range(2):
                    weighted(c + u, u, p9, 9).then_inc(w_ready, 1)
                    dve.wait_ge(w_ready, c + (u + 1))
                    dve.wait_ge(g9_ps, c + (u + 1))
                    for k in range(CH):
                        last = v.tensor_tensor_reduce(Wc[u][:, k * 144:(k + 1) * 144], ps[:, 2 + 3 * u + k // 3, (k % 3) * 144:(k % 3 + 1) * 144],
                                                      Wc[u][:, k * 144:(k + 1) * 144], 1.0, 0.0, ALU.mult, ALU.add,
                                                      v_part[:, k:k + 1])
                        last.then_inc(v_sum, 1)
                    dve.wait_ge(v_sum, (c + u) * CH + CH)
                    v.tensor_copy(v_e[:, ds((c + u) * CH, CH)], v_part).then_inc(v_ready, 1)
            dve.wait_ge(c_in, 16)
            with dve.Fori(0, (NB) // 2) as b_:
                b = b_ * 2
                for w in range(2):
                    with dve.Fori(0, NT // 4) as jq:
                        for u in range(4):
                            n = (b + w) * NT + jq * 4 + u
                            dve.wait_ge(A_free, n + 1)
                            v.tensor_tensor(A[u], adjT[:, ds(jq * 4 + u, 1), ds((b + w) * BLK, BLK)].rearrange("p o n -> p (o n)"),
                                            c_b[:, ds((b + w) * BLK, BLK)], ALU.mult).then_inc(A_tmp, 1)
                            dve.wait_ge(A_tmp, n + 1)
                            dve.wait_ge(d_slot[u], (b + w) * 64 + jq * 16 + 16)
                            v.tensor_tensor(A[u], A[u], d_in[u], ALU.add).then_inc(A_ready, 1)
                    dve.wait_ge(A_free, (b + w) * NT + (NT + 4))
                    for t in range(TI):
                        dve.wait_ge(out_dma[t], (b + w) * 16 + 16)
                        v.scalar_tensor_tensor(out=o_buf[t], in0=xs[:, ds((b + w) * 4 + t, 1), :].rearrange("p o n -> p (o n)"),
                                               scalar=dcoef[:, ds((b + w) * 4 + t, 1)], in1=ps[:, 4 * w + t, :],
                                               op0=ALU.mult, op1=ALU.add).then_inc(o_ev, 1)
                        dve.wait_ge(o_ev, (b + w) * 4 + (t + 9))
                        v.bn_stats(stats[:, t, :], o_buf[t]).then_inc(o_st, 1)
                    dve.wait_ge(o_st, (b + w) * 4 + 4)
                    v.memset(carrier[:, :], 0.0)
                    for t in range(TI):
                        v.bn_aggr(var[:, t, :], stats[:, t, :]).then_inc(o_var, 1)
                    for t in range(TI):
                        dve.wait_ge(o_rstd, (b + w) * 4 + (t + 1))
                        v.tensor_scalar(o_buf[t], o_buf[t], var[:, t, 0:1], rstd[:, t:t + 1], ALU.subtract,
                                        ALU.mult).then_inc(o_norm, 1)


_INS = {"x": "x", "adj": "adj", "W": "L0_gnn_W", "a1": "L0_gnn_a1", "a2": "L0_gnn_a2",
        "W1": "L0_gnn_W1", "b1": "L0_gnn_b1", "W2": "L0_gnn_W2", "b2": "L0_gnn_b2", "W3": "L0_gnn_W3",
        "b3": "L0_gnn_b3", "W4": "L0_gnn_W4", "b4": "L0_gnn_b4", "pairs": "L1_gnn_rel_pair_index",
        "Wq": "L1_gnn_Wq", "bq": "L1_gnn_bq", "Wk": "L1_gnn_Wk", "bk": "L1_gnn_bk"}


def kernel(**inputs):
    import numpy as _np
    import concourse.bacc as _bacc
    from concourse import mybir as _mybir
    from concourse.bass_utils import run_bass_kernel_spmd as _run

    nc = _bacc.Bacc("TRN2", target_bir_lowering=False, num_devices=1)
    arrays, args = {}, {}
    for short, name in _INS.items():
        arr = _np.ascontiguousarray(inputs[name])
        arrays[f"in_{short}"] = arr
        args[short] = nc.dram_tensor(f"in_{short}", arr.shape, _mybir.dt.from_np(arr.dtype), kind="ExternalInput").ap()
    args["out"] = nc.dram_tensor("out_0", (N, F), F32, kind="ExternalOutput").ap()
    build(nc, args)
    r = _run(nc, [arrays], core_ids=[0])
    return r.results[0]["out_0"]
```

```python
import concourse.bass as bass
from concourse import mybir
from contextlib import ExitStack

F32 = mybir.dt.float32
BF16 = mybir.dt.bfloat16
I32 = mybir.dt.int32
ALU = mybir.AluOpType
ACT = mybir.ActivationFunctionType
AX = mybir.AxisListType

P = 128
N, F, H, DH = 2048, 512, 8, 64
NT = N // P
KT = F // P
BLK = 512
NB = N // BLK
TI = BLK // P
E1, E2, E3 = 256, 128, 256
EDGES = 10000
ET = 80
EP = EDGES // ET
TRASH = N * N
CH = 8
SPAN = 78.0
LOW = -44.0
EPS = 1e-5
DIAG = 1e-7
NP_BUF = 4
EARLY = 4
RING = 4


def build(nc, a):
    ds = bass.ds
    with ExitStack() as ctx:
        def sb(name, shape, dt=F32):
            return ctx.enter_context(nc.sbuf_tensor(name, shape, dt))

        def sem(name):
            return ctx.enter_context(nc.semaphore(name))

        def dram(name, shape, dt=F32):
            return nc.dram_tensor(name, shape, dt).ap()

        r_dram = dram("r_dram", (NB * H, BLK))
        f_dram = dram("f_dram", (ET, P))
        q_dram = dram("q_dram", (N, F))
        k_dram = dram("k_dram", (N, F))
        c_dram = dram("c_dram", (NT, P))
        t_dram = dram("t_dram", (N * N + P * ET, 1), I32)
        d_dram = dram("d_dram", (N * N + P * ET, 1))

        adjT = sb("adjT", [P, NT, N], BF16)
        U = sb("U", [P, NT, H, DH])
        xs = U[:, :, :, :].rearrange("p j h d -> p j (h d)")
        WT = sb("WT", [P, 52, P])
        arena = sb("arena", [P, 15872])
        ED = sb("ED", [P, NT, H])
        q_col = sb("q_col", [P, NT, H])
        bqk = sb("bqk", [P, 2, F])
        b4_row = sb("b4_row", [P, F])
        tri = sb("tri", [P, P])[:, :]
        junk0 = sb("junk0", [P, P])[:, :]
        e_col = sb("e_col", [P, NT, 2 * H])
        Wa = sb("Wa", [P, KT, 2 * H])
        bcol = sb("bcol", [P, 5])
        zero = sb("zero", [P, 144])
        ident = sb("ident", [P, P])
        identb = sb("identb", [P, P], BF16)
        biota = sb("biota", [P, P])
        ones = sb("ones", [8, P])
        cst = sb("cst", [P, 4])
        adj_sum = sb("adj_sum", [P, NT])
        adj_diag = sb("adj_diag", [P, NT])
        pairs = sb("pairs", [P, 2 * ET], I32)
        eid = sb("eid", [P, ET], I32)
        sub_i = sb("sub_i", [P, ET], I32)
        obj_i = sb("obj_i", [P, ET], I32)
        fn_i = sb("fn_i", [P, ET], I32)
        tidx = sb("tidx", [P, ET], I32)
        didx = sb("didx", [P, ET], I32)
        t_got = sb("t_got", [P, ET], I32)
        ef = sb("ef", [P, 8, ET])
        sub_f, obj_f, fn_f, ft_f, trash_f, ok_f, live, adj_got = (ef[:, k, :] for k in range(8))
        stats = sb("stats", [P, NT, 6])
        var = sb("var", [P, NT, 2])
        rstd = sb("rstd", [P, NT])
        carrier = sb("carrier", [P, 1])
        unread = sb("unread", [P, 1])

        adj_raw = [arena[:, w:w + 2048] for w in (0, 2048, 6144)]

        def raw_buf(i):
            return i % 2 if i < NT // 2 else (i - NT // 2) % 3
        adj_b = [arena[:, 4096 + 1024 * u:5120 + 1024 * u].bitcast(BF16) for u in range(2)]
        x_in = [arena[:, 6144 + 512 * u:6656 + 512 * u] for u in range(2)]
        xT = [arena[:, 7168 + 512 * u:7680 + 512 * u] for u in range(2)]
        W_in = arena[:, 8704:10752].rearrange("p (k n) -> p k n", k=KT)
        a_in = [arena[:, 10752 + 512 * u:11264 + 512 * u] for u in range(2)]
        wa_tmp = arena[:, 11776:12288]
        s_row = arena[0:H, 8704:10752]
        d_row = arena[0:H, 10752:12800]
        d_lim = sb("d_lim", [H, 4])
        d_diag = sb("d_diag", [H, H])
        f_row = arena[0:ET, 12800:12928]
        pair_rows = adjT[:, 0:10, :].rearrange("p a n -> p (a n)").bitcast(F32)
        raw = U[:, :, :, :].rearrange("p j h d -> p (j h d)")
        w_raw = raw[:, 0:2560]
        W1r = w_raw[:, 0:1024].rearrange("p (o n) -> p o n", o=2)
        W2r = w_raw[:, 1024:1280]
        W3r = w_raw[:, 1280:1536].rearrange("p (o n) -> p o n", o=2)
        W4r = w_raw[:, 1536:2560].rearrange("p (o n) -> p o n", o=4)
        Wqr = arena[:, 12800:14848].rearrange("p (o n) -> p o n", o=4)
        Wkr = WT[:, 36:52, :].rearrange("p t n -> p (t n)").rearrange("p (o n) -> p o n", o=4)
        chunks = ([(W1r[:, o, k * P:(k + 1) * P]) for k in range(4) for o in range(2)]
                  + [W2r[:, k * P:(k + 1) * P] for k in range(2)]
                  + [W3r[:, o, :] for o in range(2)]
                  + [W4r[:, o, k * P:(k + 1) * P] for k in range(2) for o in range(4)]
                  + [Wqr[:, o, k * P:(k + 1) * P] for k in range(4) for o in range(4)]
                  + [Wkr[:, o, k * P:(k + 1) * P] for k in range(4) for o in range(4)])
        W1T = [WT[:, 2 * k:2 * k + 2, :].rearrange("p o n -> p (o n)") for k in range(4)]
        W2T = [WT[:, 8 + k, :] for k in range(2)]
        W3T = WT[:, 10:12, :].rearrange("p o n -> p (o n)")
        W4T = [WT[:, 12 + 4 * k:16 + 4 * k, :].rearrange("p o n -> p (o n)") for k in range(2)]
        WqT = [WT[:, 20 + 4 * k:24 + 4 * k, :].rearrange("p o n -> p (o n)") for k in range(4)]
        WkT = [WT[:, 36 + 4 * k:40 + 4 * k, :].rearrange("p o n -> p (o n)") for k in range(4)]

        enc_all = arena[:, 0:8704]
        encT = enc_all[:, 512:8704].rearrange("p (k n) -> p k n", k=KT)
        Us = [arena[:, 8704 + 2048 * u:10752 + 2048 * u].rearrange("p (j n) -> p j n", j=NT) for u in range(2)]
        Pw = [arena[:, 12800 + 512 * u:13312 + 512 * u] for u in range(NP_BUF)]
        r_b = [arena[:, 14848 + 512 * u:15360 + 512 * u] for u in range(2)]
        den = sb("den", [P, BLK])
        ebuf = arena[:, 14848:15872].rearrange("p (t n) -> p t n", t=2)
        z1T = arena[:, 8704:12800].rearrange("p (o n) -> p o n", o=2)
        z2T = arena[:, 12800:14848]
        z3T = arena[:, 8704:12800].rearrange("p (o n) -> p o n", o=2)
        y = [arena[:, 512 * u:512 * u + 512] for u in range(2)]
        x1T = [arena[:, 1024 + 512 * u:1536 + 512 * u] for u in range(2)]
        qk_out = [arena[:, 2048 + 512 * u:2560 + 512 * u] for u in range(2)]

        k_rows = [arena[:, 512 * u:512 * u + 512] for u in range(RING)]
        q_rows = [arena[:, 2048 + 512 * u:2560 + 512 * u] for u in range(RING)]
        o = 8704
        att = arena[:, o:o + 640].rearrange("p (t h) -> p t h", h=H)
        att_f = arena[:, o:o + 640]
        e1 = arena[:, o + 640:o + 1280]
        m_e = arena[:, o + 1280:o + 1920]
        p9 = arena[:, o + 1920:o + 2640].rearrange("p (t h) -> p t h", h=9)
        Oa = arena[:, o + 2640:o + 3920].rearrange("p (t k) -> p t k", k=NT)
        a_f = arena[:, o + 3920:o + 4000]
        b_f = arena[:, o + 4000:o + 4080]
        v_e = arena[:, o + 4080:o + 4160]
        v_part = arena[:, o + 4160:o + 4168]
        prod = [arena[:, o + 4176 + 512 * u:o + 4688 + 512 * u] for u in range(2)]
        norms = arena[:, o + 5200:o + 5456].rearrange("p (w n) -> p w n", w=2)
        Ob = [arena[:, 4096 + 1024 * u:5120 + 1024 * u].rearrange("p (t b) -> p t b", t=CH) for u in range(2)]
        Ob_early = [arena[:, 1024 * u:1024 * u + 1024].rearrange("p (t b) -> p t b", t=CH) for u in range(EARLY)]
        Wc = [arena[:, 6144 + 1152 * u:7296 + 1152 * u] for u in range(2)]
        ObT = WT[:, 0:40, :].rearrange("p t n -> p (t n)").bitcast(BF16).rearrange("p (t e) -> p t e", t=ET)
        tab = WT[:, 40:52, :].rearrange("p t n -> p (t n)")
        m_b = tab[:, 0:64].bitcast(BF16)
        base = tab[:, 64:192]
        dterm = tab[:, 192:320]
        seg = tab[:, 320:464].rearrange("p (t h) -> p t h", h=9)
        Z = tab[:, 464:592]
        T9 = tab[:, 592:736].rearrange("p (t h) -> p t h", h=9)
        T9f = tab[:, 592:736]
        Tb = [tab[:, 736 + 72 * u:808 + 72 * u].bitcast(BF16) for u in range(3)]
        c_col = tab[:, 952:968]
        cd_col = tab[:, 968:984]
        n_col = tab[:, 984:1000]
        dcoef = tab[:, 1000:1016]
        c_row = tab[0:NT, 1016:1144]
        glob = tab[:, 1144:1156]
        T_tmp = tab[:, 1156:1300]
        A = [arena[:, 512 * u:512 * u + 512] for u in range(4)]
        o_buf = [arena[:, 2048 + 512 * u:2560 + 512 * u] for u in range(TI)]
        c_b = arena[:, 4096:6144]
        d_in = [arena[:, 6400 + 512 * u:6912 + 512 * u] for u in range(4)]

        ps = ctx.enter_context(nc.psum_tensor("ps", [P, 8, 512], F32))
        psb = ps[:, :, :].rearrange("p b n -> p (b n)").bitcast(BF16).rearrange("p (b n) -> p b n", b=8)

        consts = sem("consts")
        pairs_in = sem("pairs_in")
        w_in = sem("w_in")
        wqk_in = sem("wqk_in")
        wqk_ps = sem("wqk_ps")
        wqk_sb = sem("wqk_sb")
        wh_in = sem("wh_in")
        small_in = sem("small_in")
        b4_in_s = sem("b4_in_s")
        bqk_in = sem("bqk_in")
        x_res_in = sem("x_res_in")
        dve_own = sem("dve_own")
        fn_ready = sem("fn_ready")
        fn_ps = sem("fn_ps")
        f_row_ready = sem("f_row_ready")
        f_out = sem("f_out")
        f_in = [sem(f"f_in{q}") for q in range(4)]
        idx_ready = sem("idx_ready")
        wa_ready = sem("wa_ready")
        wt_ps = sem("wt_ps")
        wt_sb = sem("wt_sb")
        x_in_s = [sem(f"x_in_s{u}") for u in range(2)]
        xT_ps = sem("xT_ps")
        xT_sb = sem("xT_sb")
        wh_ps = sem("wh_ps")
        wh_sb = sem("wh_sb")
        e_sb = sem("e_sb")
        rows_ps = sem("rows_ps")
        rows_sb = sem("rows_sb")
        d_ready = sem("d_ready")
        d_ps = sem("d_ps")
        shift_ready = sem("shift_ready")
        r_arg = sem("r_arg")
        r_ready = sem("r_ready")
        ed_ready = sem("ed_ready")
        u_ready = sem("u_ready")
        adj_in = [sem(f"adj_in{u}") for u in range(3)]
        adj_cast = sem("adj_cast")
        m_e_ready = sem("m_e_ready")
        adj_dg = sem("adj_dg")
        adj_ps = sem("adj_ps")
        adj_sb0 = sem("adj_sb0")
        adj_sb1 = sem("adj_sb1")
        r_out = sem("r_out")
        r_in = [sem(f"r_in{u}") for u in range(2)]
        P_ready = sem("P_ready")
        P_free = sem("P_free")
        us_ready = sem("us_ready")
        bank_set = sem("bank_set")
        den_ready = sem("den_ready")
        rden_ready = sem("rden_ready")
        att_ev = sem("att_ev")
        b4_added = sem("b4_added")
        min_ready = sem("min_ready")
        exp_ready = sem("exp_ready")
        enc_ready = sem("enc_ready")
        z1_ps, z1_sb = sem("z1_ps"), sem("z1_sb")
        z2_ps, z2_sb = sem("z2_ps"), sem("z2_sb")
        z3_ps, z3_sb = sem("z3_ps"), sem("z3_sb")
        z4_ps = sem("z4_ps")
        y_ready = sem("y_ready")
        st_ready = sem("st_ready")
        var_ready = sem("var_ready")
        ln_ready = sem("ln_ready")
        rstd_ready = sem("rstd_ready")
        x1_ready = sem("x1_ready")
        x1_kept = sem("x1_kept")
        x1T_ps, x1T_sb = sem("x1T_ps"), sem("x1T_sb")
        qk_ps = sem("qk_ps")
        qk_sb = sem("qk_sb")
        qk_dma = [sem(f"qk_dma{w}") for w in range(2)]
        t_out = sem("t_out")
        t_in = sem("t_in")
        aj_in = sem("aj_in")
        zeroed = sem("zeroed")
        k_in = [sem(f"k_in{u}") for u in range(RING)]
        q_in = [sem(f"q_in{u}") for u in range(RING)]
        prod_ready = sem("prod_ready")
        rows_used = sem("rows_used")
        didx_ready = sem("didx_ready")
        sq_done, norm_done = sem("sq_done"), sem("norm_done")
        gm_ready, gm_ps, g1_ready, g_all = sem("gm_ready"), sem("gm_ps"), sem("g1_ready"), sem("g_all")
        sq_ready, bound_ready = sem("sq_ready"), sem("bound_ready")
        scaled, e1_arg = sem("scaled"), sem("e1_arg")
        beta_ready, e1_ready = sem("beta_ready"), sem("e1_ready")
        oh_ready = sem("oh_ready")
        oh_used = sem("oh_used")
        obT_sb = sem("obT_sb")
        table_in = sem("table_in")
        lse_arg, lse_ready = sem("lse_arg"), sem("lse_ready")
        m_ready = sem("m_ready")
        tabs_ready = sem("tabs_ready")
        mg_ps, mg_sb = sem("mg_ps"), sem("mg_sb")
        p_arg, p_exp = sem("p_arg"), sem("p_exp")
        c_ready, c_ps, c_row_ready = sem("c_ready"), sem("c_ps"), sem("c_row_ready")
        c_out, c_in = sem("c_out"), sem("c_in")
        t9_ready = sem("t9_ready")
        w_ready = sem("w_ready")
        g9_ps = sem("g9_ps")
        v_sum = sem("v_sum")
        v_ready = sem("v_ready")
        d_out = sem("d_out")
        d_slot = [sem(f"d_slot{u}") for u in range(4)]
        A_tmp = sem("A_tmp")
        A_ready = sem("A_ready")
        o_ps = sem("o_ps")
        A_free = sem("A_free")
        o_ev = sem("o_ev")
        o_st, o_var, o_ln, o_rstd, o_norm = sem("o_st"), sem("o_var"), sem("o_ln"), sem("o_rstd"), sem("o_norm")
        out_dma = [sem(f"out_dma{t}") for t in range(TI)]

        credits = ([(s, 2) for s in (wt_sb, xT_sb, wh_ps, wh_sb, e_sb, enc_ready, oh_used, obT_sb,
                                     mg_sb, v_ready)]
                   + [(adj_sb0, 2), (adj_sb1, 1), (adj_dg, 1), (att_ev, 1), (z1_sb, 4), (qk_sb, 2), (x1T_sb, 2),
                      (x1_kept, 2), (P_free, NP_BUF), (A_ready, 4), (A_free, 4), (o_ev, 8)]
                   + [(s, 16) for s in qk_dma + out_dma])
        CHUNKS = ET // CH
        WB = 5

        block = ctx.enter_context(nc.Block())

        @block.sync
        def _(sp):
            sp.wait_ge(consts, 1)
            sp.dma_start(pairs[0:EP, :], a["pairs"].rearrange("(p t) c -> p (t c)", t=ET)).then_inc(pairs_in, 16)
            for k in range(KT):
                sp.dma_start(W_in[:, k, :].rearrange("p (h d) -> p h d", h=H),
                             a["W"][:, k * P:(k + 1) * P, :].rearrange("h p d -> p h d")).then_inc(wh_in, 16)
            for u, name in enumerate(("a1", "a2")):
                sp.dma_start(a_in[u], a[name].rearrange("h d -> (h d)").partition_broadcast(P)).then_inc(wh_in, 16)
            for u in range(2):
                sp.dma_start(x_in[u], a["x"][u * P:(u + 1) * P, :]).then_inc(x_in_s[u], 16)
            sp.dma_start(W1r, a["W1"].rearrange("(o p) n -> p o n", p=P)).then_inc(w_in, 16)
            sp.dma_start(W2r, a["W2"]).then_inc(w_in, 16)
            sp.dma_start(W3r, a["W3"].rearrange("(o p) n -> p o n", p=P)).then_inc(w_in, 16)
            sp.dma_start(W4r, a["W4"].rearrange("(o p) n -> p o n", p=P)).then_inc(w_in, 16)
            for c, name, n in ((0, "b1", 2), (2, "b2", 1), (3, "b3", 2)):
                for o in range(n):
                    sp.dma_start(bcol[:, c + o:c + o + 1],
                                 a[name][o * P:(o + 1) * P].unsqueeze(1)).then_inc(small_in, 16)
            sp.dma_start(b4_row[:, :], a["b4"].partition_broadcast(P)).then_inc(b4_in_s, 16)
            for w, name in enumerate(("bq", "bk")):
                sp.dma_start(bqk[:, w, :], a[name].partition_broadcast(P)).then_inc(bqk_in, 16)
            for u in range(2):
                sp.dma_start(adj_raw[u], a["adj"][u * P:(u + 1) * P, :]).then_inc(adj_in[u], 16)
            sp.wait_ge(f_row_ready, 1)
            sp.dma_start(f_dram, f_row).then_inc(f_out, 16)
            sp.wait_ge(f_out, 16)
            def load_x(i, u):
                sp.wait_ge(xT_ps, i + (u - 1))
                sp.dma_start(x_in[u], a["x"][ds((i + u) * P, P), :]).then_inc(x_in_s[u], 16)

            def load_adj(i, u):
                sp.wait_ge(adj_cast, i + (u - 1))
                sp.dma_start(adj_raw[u], a["adj"][ds((i + u) * P, P), :]).then_inc(adj_in[u], 16)

            for q in range(4):
                part = slice(q * ET // 4 * P, (q + 1) * ET // 4 * P)
                sp.dma_start(pair_rows[:, part], f_dram.rearrange("t e -> (t e)")[part].partition_broadcast(P)
                             ).then_inc(f_in[q], 16)
                for u in range(2):
                    load_x(2 * q + 2, u)
            sp.dma_start(Wqr, a["Wq"].rearrange("(o p) n -> p o n", p=P)).then_inc(wqk_in, 16)
            sp.dma_start(Wkr, a["Wk"].rearrange("(o p) n -> p o n", p=P)).then_inc(wqk_in, 16)
            with sp.Fori(1, NT // 4) as i_:
                for u in range(2):
                    load_x(i_ * 2 + NT // 2, u)
                    load_adj(i_ * 2, u)
            for i in range(NT // 2, NT):
                if i == NT // 2 + 2:
                    sp.wait_ge(wh_ps, 2 + NT)
                else:
                    sp.wait_ge(adj_cast, i - 1 if i < NT // 2 + 2 else i - 2)
                sp.dma_start(adj_raw[raw_buf(i)], a["adj"][i * P:(i + 1) * P, :]).then_inc(adj_in[raw_buf(i)], 16)
            sp.wait_ge(r_ready, 1)
            r_view = r_dram.rearrange("(g b u) n -> g u b n", b=NB, u=2)
            for h in range(H):
                sp.dma_start(r_view[h // 2, h % 2].unsqueeze(0),
                             s_row[h:h + 1, :].rearrange("p (b n) -> p b n", b=NB)).then_inc(r_out, 16)
            sp.wait_ge(r_out, 16 * H)
            for u in range(2):
                sp.dma_start(r_b[u], r_dram[u, :].partition_broadcast(P)).then_inc(r_in[u], 16)
            for k in range(4):
                sp.dma_start(d_dram[(60 + k) * P * BLK:(61 + k) * P * BLK, :].rearrange("(p m n) o -> p m (n o)", m=4, n=P),
                             zero[:, 0:P].unsqueeze(1).broadcast_to([P, 4, P])).then_inc(zeroed, 16)
            with sp.Fori(0, (NB * H - 2) // 2) as g_:
                g = g_ * 2
                for u in range(2):
                    sp.wait_ge(P_ready, (g + (u + 1)) * NT)
                    sp.dma_start(r_b[u], r_dram[ds(g + (u + 2), 1), :].rearrange("o n -> (o n)").partition_broadcast(P)
                                 ).then_inc(r_in[u], 16)
                for k in range(4):
                    sp.dma_start(d_dram[ds((g * 2 + k) * (P * BLK), P * BLK), :].rearrange("(p m n) o -> p m (n o)", m=4, n=P),
                                 zero[:, 0:P].unsqueeze(1).broadcast_to([P, 4, P])).then_inc(zeroed, 16)
            sp.wait_ge(us_ready, 2 * H)
            sp.dma_start(xs, a["x"].rearrange("(t p) n -> p t n", p=P)).then_inc(x_res_in, 16)
            with sp.Fori(0, NT) as t:
                for w, dst in enumerate((q_dram, k_dram)):
                    sp.wait_ge(qk_sb, t * 2 + (w + 3))
                    sp.dma_start(dst[ds(t * P, P), :], qk_out[w]).then_inc(qk_dma[w], 16)
            sp.wait_ge(c_row_ready, 1)
            sp.dma_start(c_dram, c_row).then_inc(c_out, 16)
            sp.wait_ge(c_out, 16)
            sp.dma_start(c_b, c_dram.rearrange("t p -> (t p)").partition_broadcast(P)).then_inc(c_in, 16)
            sp.wait_ge(d_out, 16 * ET)
            dj = d_dram[0:N * N, :].rearrange("(j i) o -> j (i o)", i=N)
            with sp.Fori(0, NB) as b:
                with sp.Fori(0, NT // 4) as jq:
                    for u in range(4):
                        sp.wait_ge(A_ready, b * NT + jq * 4 + (u + 1))
                        sp.dma_start(d_in[u], dj[ds((jq * 4 + u) * P, P), ds(b * BLK, BLK)]).then_inc(d_slot[u], 16)
            for w in range(2):
                sp.wait_ge(qk_dma[w], 16 * (NT + 1))
            for t in range(TI):
                sp.wait_ge(out_dma[t], 16 * (NB + 1))

        @block.gpsimd
        def _(pool):
            nc.gpsimd.memset(pairs[:, :], 0).then_inc(consts, 1)
            nc.gpsimd.memset(zero[:, :], 0.0).then_inc(consts, 1)
            nc.gpsimd.memset(ones[:, :], 1.0).then_inc(consts, 1)
            nc.gpsimd.memset(cst[:, 0:1], EPS).then_inc(consts, 1)
            nc.gpsimd.memset(cst[:, 1:2], LOW).then_inc(consts, 1)
            nc.gpsimd.memset(cst[:, 2:3], DIAG).then_inc(consts, 1)
            nc.gpsimd.memset(ident[:, :], 0.0).then_inc(consts, 1)
            nc.gpsimd.memset(tri, 1.0).then_inc(consts, 1)
            pool.wait_ge(consts, 8)
            nc.gpsimd.affine_select(ident[:, :], ident[:, :], [[-1, P]], ALU.not_equal, 1.0,
                                    base=0, channel_multiplier=1).then_inc(consts, 1)
            nc.gpsimd.affine_select(tri, tri, [[-1, P]], ALU.is_gt, 0.0,
                                    base=0, channel_multiplier=1).then_inc(consts, 1)
            nc.gpsimd.iota(biota[:, :], [[1, P]], 0, 0, allow_small_or_imprecise_dtypes=True).then_inc(consts, 1)
            nc.gpsimd.iota(eid[:, :], [[1, ET]], 0, ET).then_inc(consts, 1)
            pool.wait_ge(consts, 12)
            nc.gpsimd.tensor_copy(identb[:, :], ident[:, :]).then_inc(consts, 1)
            for s, n in credits:
                pool.sem_inc(s, n)
            pool.wait_ge(idx_ready, 1)
            pool.wait_ge(consts, 13)
            for t in range(ET):
                if t:
                    pool.wait_ge(t_out, 16 * t)
                nc.gpsimd.indirect_dma_start(
                    out=t_dram, out_offset=bass.IndirectOffsetOnAxis(ap=tidx[:, t:t + 1], axis=0),
                    in_=eid[:, t:t + 1], in_offset=None).then_inc(t_out, 16)
            pool.wait_ge(t_out, 16 * ET)
            adj_flat = a["adj"].rearrange("i (j o) -> (i j) o", o=1)
            for t in range(ET):
                nc.gpsimd.indirect_dma_start(
                    out=t_got[:, t:t + 1], out_offset=None, in_=t_dram,
                    in_offset=bass.IndirectOffsetOnAxis(ap=tidx[:, t:t + 1], axis=0)).then_inc(t_in, 16)
                nc.gpsimd.indirect_dma_start(
                    out=adj_got[:, t:t + 1], out_offset=None, in_=adj_flat,
                    in_offset=bass.IndirectOffsetOnAxis(ap=fn_i[:, t:t + 1], axis=0)).then_inc(aj_in, 16)
            for w in range(2):
                pool.wait_ge(qk_dma[w], 16 * (NT + 1))
            pool.wait_ge(x1_kept, NT + 2)
            pool.wait_ge(sq_done, 2 * NT)
            for t in range(ET):
                if t >= RING:
                    pool.wait_ge(rows_used, t - RING + 1)
                nc.gpsimd.indirect_dma_start(
                    out=k_rows[t % RING], out_offset=None, in_=k_dram,
                    in_offset=bass.IndirectOffsetOnAxis(ap=obj_i[:, t:t + 1], axis=0)).then_inc(k_in[t % RING], 16)
                nc.gpsimd.indirect_dma_start(
                    out=q_rows[t % RING], out_offset=None, in_=q_dram,
                    in_offset=bass.IndirectOffsetOnAxis(ap=sub_i[:, t:t + 1], axis=0)).then_inc(q_in[t % RING], 16)
            pool.wait_ge(didx_ready, 1)
            pool.wait_ge(zeroed, 16 * 64)
            for t in range(ET):
                if t % CH == 0:
                    pool.wait_ge(v_ready, 2 + t // CH + 1)
                nc.gpsimd.indirect_dma_start(
                    out=d_dram, out_offset=bass.IndirectOffsetOnAxis(ap=didx[:, t:t + 1], axis=0),
                    in_=v_e[:, t:t + 1], in_offset=None).then_inc(d_out, 16)

        @block.tensor
        def _(pe):
            mm, tr = nc.tensor.matmul, nc.tensor.transpose
            pe.wait_ge(consts, 13)
            pe.wait_ge(fn_ready, 1)
            tr(ps[0:ET, 7, 0:P], fn_f, ident[:, :]).then_inc(fn_ps, 1)
            pe.wait_ge(w_in, 16 * 4)
            for g in range(WB):
                pe.wait_ge(wt_sb, g + 1)
                for k in range(4):
                    last = tr(ps[:, g % 2, k * P:(k + 1) * P], chunks[4 * g + k], ident[:, :])
                last.then_inc(wt_ps, 1)
            pe.wait_ge(wa_ready, 2 * KT)
            pe.wait_ge(wh_in, 16 * 6)
            pe.wait_ge(f_row_ready, 1)

            def x_transposed(i):
                for u in range(2):
                    pe.wait_ge(x_in_s[u], i * 8 + 16)
                    pe.wait_ge(xT_sb, i + (u + 1))
                    for k in range(KT):
                        last = tr(ps[:, 2 + u, k * P:(k + 1) * P], x_in[u][:, k * P:(k + 1) * P], ident[:, :])
                    last.then_inc(xT_ps, 1)

            def x_products(i):
                for u in range(2):
                    pe.wait_ge(xT_sb, i + (u + 3))
                    pe.wait_ge(wh_sb, i + (u + 1))
                    pe.wait_ge(e_sb, i + (u + 1))
                    for k in range(KT):
                        mm(ps[:, 4 + u, :], xT[u][:, k * P:(k + 1) * P], W_in[:, k, :], start=(k == 0), stop=(k == KT - 1))
                    for k in range(KT):
                        last = mm(ps[:, 6 + u, 0:2 * H], xT[u][:, k * P:(k + 1) * P], Wa[:, k, :],
                                  start=(k == 0), stop=(k == KT - 1))
                    last.then_inc(wh_ps, 1)

            def adj_transposed(i, u):
                pe.wait_ge(adj_cast, i + (u + 1))
                for half in range(2):
                    if half == 0:
                        pe.wait_ge(adj_sb0, i + (u + 2))
                    else:
                        pe.wait_ge(adj_sb1, i + (u + 1))
                    for k in range(8):
                        j = half * 8 + k
                        last = tr(psb[:, half, k * P:(k + 1) * P], adj_b[u][:, j * P:(j + 1) * P], identb[:, :])
                    last.then_inc(adj_ps, 1)

            with pe.Fori(0, NT // 4) as i_:
                x_transposed(i_ * 2)
                x_products(i_ * 2)
            pe.wait_ge(wt_sb, 2 + WB)
            with pe.Fori(0, NT // 4) as i_:
                x_transposed(i_ * 2 + NT // 2)
                adj_transposed(i_ * 2, 0)
                x_products(i_ * 2 + NT // 2)
                adj_transposed(i_ * 2, 1)
            pe.wait_ge(e_sb, 2 + NT)
            pe.wait_ge(wh_sb, 2 + NT)
            for g in range(4):
                if g >= 2:
                    pe.wait_ge(rows_sb, 2 * (g - 1))
                for w in range(2):
                    for k in range(4):
                        last = tr(ps[0:H, 2 + 2 * (g % 2) + w, k * P:(k + 1) * P],
                                  e_col[:, 4 * g + k, w * H:(w + 1) * H], ident[:, :])
                last.then_inc(rows_ps, 1)
            adj_transposed(NT // 2, 0)
            pe.wait_ge(d_ready, 1)
            mm(ps[:, 6, 0:H], ones[:, :], d_diag[:, :], start=True, stop=True).then_inc(d_ps, 1)
            pe.wait_ge(rows_sb, 8)
            pe.wait_ge(wqk_in, 32)
            for first in (4 * WB + 16, 4 * WB):
                for k in range(16):
                    last = tr(ps[:, 2 + k // 4, (k % 4) * P:(k % 4 + 1) * P], chunks[first + k], ident[:, :])
                last.then_inc(wqk_ps, 1)
                for i in range(*((NT // 2 + 1, 3 * NT // 4 + 1) if first > 4 * WB else (3 * NT // 4 + 1, NT))):
                    adj_transposed(i - i % 2, i % 2)
                pe.wait_ge(wqk_sb, 4 if first > 4 * WB else 8)
            for k in range(8):
                last = mm(ps[:, 2 + k // 4, (k % 4) * P:(k % 4 + 1) * P], ones[:, :], ones[:, :], start=True, stop=True)
            last.then_inc(bank_set, 1)
            with pe.Fori(0, H // 2) as hp:
                with pe.Fori(0, NB // 2) as b2:
                    for v in range(2):
                        m = hp * NB + b2 * 2 + v
                        pe.wait_ge(att_ev, m * 2 + 1)
                        for u in range(2):
                            pe.wait_ge(us_ready, hp * 4 + (2 * u + 2))
                            for j in range(NT):
                                pe.wait_ge(P_ready, m * (2 * NT) + (u * NT + j + 1))
                                mm(ps[:, 2 * v + u, :], Us[u][:, j, :], Pw[j % NP_BUF], start=(j == 0),
                                   stop=(j == NT - 1)).then_inc(P_free, 1)
            with pe.Fori(0, NB // 2) as b2:
                for v in range(2):
                    b = b2 * 2 + v
                    pe.wait_ge(enc_ready, b * 4 + 6)
                    for o in range(2):
                        pe.wait_ge(z1_sb, b * 2 + (o + 1))
                        for k in range(KT):
                            last = mm(ps[:, 4 + 2 * v + o, :], W1T[k][:, o * P:(o + 1) * P],
                                      encT[:, k, ds(b * BLK, BLK)], start=(k == 0), stop=(k == KT - 1))
                        last.then_inc(z1_ps, 1)
            for b in range(NB):
                pe.wait_ge(z1_sb, 4 + 2 * b + 2)
                for k in range(2):
                    last = mm(ps[:, b % 2, :], W2T[k], z1T[:, k, b * BLK:(b + 1) * BLK], start=(k == 0), stop=(k == 1))
                last.then_inc(z2_ps, 1)
                if b >= 1:
                    pe.wait_ge(z2_sb, b)
            pe.wait_ge(z1_sb, 4 + 2 * NB)
            for b in range(NB):
                pe.wait_ge(z2_sb, b + 1)
                if b == 0:
                    pe.wait_ge(z2_sb, NB)
                if b >= 2:
                    pe.wait_ge(z3_sb, 2 * (b - 1))
                for o in range(2):
                    mm(ps[:, 2 + 2 * (b % 2) + o, :], W3T[:, o * P:(o + 1) * P], z2T[:, b * BLK:(b + 1) * BLK],
                       start=True, stop=True).then_inc(z3_ps, 1)
            for t in range(NT):
                if t % TI == 0:
                    pe.wait_ge(z3_sb, 2 * (t // TI) + 2)
                if t >= 2:
                    pe.wait_ge(y_ready, t - 1)
                for k in range(2):
                    last = mm(ps[:, 6 + t % 2, :], z3T[:, k, t * P:(t + 1) * P], W4T[k], start=(k == 0), stop=(k == 1))
                last.then_inc(z4_ps, 1)
            pe.wait_ge(y_ready, NT)
            pe.wait_ge(z3_sb, 8)
            def x1_transposed(t, u):
                pe.wait_ge(x1_ready, t + 1)
                pe.wait_ge(x1T_sb, t + 1)
                for k in range(KT):
                    last = tr(ps[:, 2 + u, k * P:(k + 1) * P], y[u][:, k * P:(k + 1) * P], ident[:, :])
                last.then_inc(x1T_ps, 1)

            def q_and_k(t, u, more=True):
                pe.wait_ge(x1T_sb, t + 3)
                for w, wT in enumerate((WqT, WkT)):
                    pe.wait_ge(qk_sb, t * 2 + (w + 1))
                    for k in range(KT):
                        last = mm(ps[:, 4 + w, :], x1T[u][:, k * P:(k + 1) * P], wT[k],
                                  start=(k == 0), stop=(k == KT - 1))
                    last.then_inc(qk_ps, 1)
                    if w == 0 and more:
                        x1_transposed(t + 1, 1 - u)

            x1_transposed(0, 0)
            with pe.Fori(0, NT // 2 - 1) as t2:
                for u in range(2):
                    q_and_k(t2 * 2 + u, u)
            q_and_k(NT - 2, 0)
            q_and_k(NT - 1, 1, more=False)
            pe.wait_ge(gm_ready, 2)
            for w in range(2):
                last = tr(ps[0:1, 2, w * P:(w + 1) * P], glob[:, w:w + 1], ident[:, :])
            last.then_inc(gm_ps, 1)
            pe.wait_ge(g1_ready, 1)
            mm(ps[:, 3, 0:1], ones[0:1, :], glob[0:1, 2:3], start=True, stop=True).then_inc(g_all, 1)
            pe.wait_ge(beta_ready, 1)
            mm(ps[:, 0, 0:P], zero[:, 0:P], zero[:, 0:P], start=True, stop=False, skip_group_check=True)
            with pe.Fori(0, CHUNKS) as c:
                pe.wait_ge(oh_ready, c * 2 + 2)
                pe.wait_ge(obT_sb, c + 2)
                for k in range(CH):
                    mm(ps[:, 0, 0:P], Ob[0][:, k, :], Wc[0][:, k * P:(k + 1) * P], start=False, stop=False,
                       skip_group_check=True)
                    last = tr(ps[:, 2 + k // 4, (k % 4) * P:(k % 4 + 1) * P], Ob[0][:, k, :], ident[:, :])
                last.then_inc(oh_used, 1)
            pe.wait_ge(m_ready, 1)
            pe.wait_ge(obT_sb, 2 + CHUNKS)
            with pe.Fori(0, CHUNKS // 2) as c_:
                c = c_ * 2
                for u in range(2):
                    pe.wait_ge(mg_sb, c + (u + 1))
                    for k in range(CH):
                        last = mm(ps[:, 2 + 2 * u + k // 4, (k % 4) * P:(k % 4 + 1) * P],
                                  ObT[:, ds((c + u) * CH + k, 1), :].rearrange("p o e -> p (o e)"), m_b,
                                  start=(k % 4 == 0), stop=True, skip_group_check=True)
                    last.then_inc(mg_ps, 1)
            mm(ps[:, 1, 0:144], zero[:, 0:P], zero[:, 0:144], start=True, stop=False, skip_group_check=True)
            def pair_sums(one_hots, u):
                for k in range(CH):
                    last = mm(ps[:, 1, 0:144], one_hots[:, k, :], Wc[u][:, k * 144:(k + 1) * 144], start=False,
                              stop=False, skip_group_check=True)
                last.then_inc(oh_used, 1)

            for c in range(EARLY):
                pe.wait_ge(oh_ready, 2 * CHUNKS + EARLY + c + 1)
                pair_sums(Ob_early[c], c % 2)
            with pe.Fori(EARLY // 2, CHUNKS // 2) as c_:
                c = c_ * 2
                for u in range(2):
                    pe.wait_ge(oh_ready, 2 * CHUNKS + (c + u) * 2 + 2)
                    pair_sums(Ob[u], u)
            pe.wait_ge(c_ready, 1)
            tr(ps[0:NT, 0, 0:P], c_col, ident[:, :]).then_inc(c_ps, 1)
            pe.wait_ge(t9_ready, 1)
            pe.wait_ge(mg_sb, 2 + CHUNKS)
            with pe.Fori(0, CHUNKS // 2) as c_:
                c = c_ * 2
                for u in range(2):
                    pe.wait_ge(v_ready, c + (u + 1))
                    for k in range(CH):
                        for part in range(3):
                            last = mm(ps[:, 2 + 3 * u + k // 3, (k % 3) * 144:(k % 3 + 1) * 144],
                                      ObT[:, ds((c + u) * CH + k, 1), :].rearrange("p o e -> p (o e)"), Tb[part],
                                      start=(k % 3 == 0 and part == 0), stop=(part == 2), skip_group_check=True)
                    last.then_inc(g9_ps, 1)
            pe.wait_ge(x1_kept, NT + 2)
            pe.wait_ge(v_ready, 2 + CHUNKS)
            pe.wait_ge(c_row_ready, 1)
            for b in range(NB):
                pe.wait_ge(o_ev, b * 4 + 4)
                last_block = b == NB - 1

                def product(j, u, first=False):
                    pe.wait_ge(A_ready, j + (b * NT + 5))
                    for t in range(TI):
                        last = mm(ps[:, 4 * (b % 2) + t, :], A[u][:, t * P:(t + 1) * P],
                                  xs[:, ds(j, 1), :].rearrange("p o n -> p (o n)"), start=first,
                                  stop=False, skip_group_check=True)
                    last.then_inc(A_free, 1)

                for u in range(4):
                    product(u, u, first=(u == 0))
                with pe.Fori(1, NT // 4 - last_block) as jq:
                    for u in range(4):
                        product(jq * 4 + u, u)
            pe.wait_ge(A_ready, NB * NT + 4)
            for t in range(TI):
                for u in range(4):
                    last = mm(ps[:, 4 * ((NB - 1) % 2) + t, :], A[u][:, t * P:(t + 1) * P], xs[:, NT - 4 + u, :],
                              start=False, stop=(u == 3), skip_group_check=True)
                last.then_inc(o_ps, 1)

        @block.scalar
        def _(act):
            fn = nc.scalar.activation
            act.wait_ge(fn_ps, 1)
            nc.scalar.copy(f_row, ps[0:ET, 7, 0:P]).then_inc(f_row_ready, 1)
            for g in range(WB):
                act.wait_ge(wt_ps, g + 1)
                nc.scalar.copy(WT[:, 4 * g:4 * g + 4, :].rearrange("p t n -> p (t n)"), ps[:, g % 2, :]).then_inc(wt_sb, 1)

            def x_copies(i):
                for u in range(2):
                    act.wait_ge(xT_ps, i + (u + 1))
                    act.wait_ge(wh_ps, i + (u + 1))
                    nc.scalar.copy(xT[u], ps[:, 2 + u, :]).then_inc(xT_sb, 1)

            def wh_copies(i):
                for u in range(2):
                    act.wait_ge(wh_ps, i + (u + 3))
                    nc.scalar.copy(U[:, ds(i + u, 1), :, :].rearrange("p o h d -> p (o h d)"),
                                   ps[:, 4 + u, :]).then_inc(wh_sb, 1)
                    nc.scalar.copy(e_col[:, ds(i + u, 1), :], ps[:, 6 + u, 0:2 * H]).then_inc(e_sb, 1)

            def adj_cast_and_sum(i, u):
                act.wait_ge(adj_in[u], i * 8 + 16)
                act.wait_ge(adj_sb0, i + (u + 1))
                fn(adj_b[u], adj_raw[u], ACT.Copy, accum_out=adj_sum[:, ds(i + u, 1)]).then_inc(adj_cast, 1)

            def adj_half(i, u):
                act.wait_ge(adj_ps, (i + u) * 2 + 2)
                nc.scalar.copy(adjT[:, 8:16, ds((i + u) * P, P)],
                               psb[:, 1, :].rearrange("p (j n) -> p j n", n=P)).then_inc(adj_sb1, 1)

            def adj_late(i):
                turns = sum(raw_buf(k) == raw_buf(i) for k in range(i + 1))
                act.wait_ge(adj_in[raw_buf(i)], 16 * turns)
                act.wait_ge(adj_sb0, i + 1)
                fn(adj_b[i % 2], adj_raw[raw_buf(i)], ACT.Copy, accum_out=adj_sum[:, i:i + 1]).then_inc(adj_cast, 1)
                if i > NT // 2:
                    adj_half(i - 1, 0)

            with act.Fori(0, NT // 4) as i_:
                x_copies(i_ * 2)
                wh_copies(i_ * 2)
            act.wait_ge(idx_ready, 1)
            adj_cast_and_sum(0, 0)
            with act.Fori(0, NT // 4) as i_:
                x_copies(i_ * 2 + NT // 2)
                adj_cast_and_sum(i_ * 2, 1)
                adj_half(i_ * 2, 0)
                adj_cast_and_sum(i_ * 2 + 2, 0)
                wh_copies(i_ * 2 + NT // 2)
                adj_half(i_ * 2, 1)
            for g in range(4):
                act.wait_ge(rows_ps, g + 1)
                nc.scalar.copy(s_row[:, g * BLK:(g + 1) * BLK], ps[0:H, 2 + 2 * (g % 2), :]).then_inc(rows_sb, 1)
                nc.scalar.copy(d_row[:, g * BLK:(g + 1) * BLK], ps[0:H, 3 + 2 * (g % 2), :]).then_inc(rows_sb, 1)
            act.wait_ge(shift_ready, 1)
            fn(ED[:, :, :], e_col[:, :, H:2 * H], ACT.Exp).then_inc(ed_ready, 1)
            fn(q_col[:, :, :], e_col[:, :, H:2 * H], ACT.Exp, scale=-0.8).then_inc(ed_ready, 1)
            for step, tile in enumerate((36, 20)):
                act.wait_ge(wqk_ps, step + 1)
                for g in range(4):
                    nc.scalar.copy(WT[:, tile + 4 * g:tile + 4 * g + 4, :].rearrange("p t n -> p (t n)"),
                                   ps[:, 2 + g, :]).then_inc(wqk_sb, 1)
                if step == 0:
                    act.wait_ge(r_arg, 1)
                    fn(s_row, s_row, ACT.Exp, scale=0.8).then_inc(r_ready, 1)
                for i in range((2 + step) * NT // 4 + 1, min((3 + step) * NT // 4 + 1, NT)):
                    adj_late(i)
            adj_half(NT - 1, 0)
            act.wait_ge(u_ready, NT)
            act.wait_ge(r_out, 16 * H)

            def sources(hp, u):
                h = hp * 2 + u
                nc.scalar.copy(Us[u][:, :, u * DH:u * DH + DH], U[:, :, ds(h, 1), :].rearrange("p j o d -> p (j o) d")).then_inc(us_ready, 1)
                nc.scalar.copy(Us[u][:, :, (1 - u) * DH:(2 - u) * DH], ED[:, :, ds(h, 1)].broadcast_to([P, NT, DH])).then_inc(us_ready, 1)

            def denominators(m, v):
                act.wait_ge(P_free, m * (2 * NT) + NP_BUF)
                act.wait_ge(att_ev, m * 2 + 1)
                nc.scalar.copy(den[0:DH, :], ps[DH:P, 2 * (1 - v), :]).then_inc(den_ready, 1)
                nc.scalar.copy(den[DH:P, :], ps[0:DH, 2 * (1 - v) + 1, :]).then_inc(den_ready, 1)

            def pair_denominators(hp):
                with act.Fori(0, NB // 2) as b2:
                    for v in range(2):
                        denominators(hp * NB + b2 * 2 + v, v)

            sources(0, 0)
            sources(0, 1)
            act.wait_ge(bank_set, 1)
            with act.Fori(0, H // 2 - 1) as hp:
                pair_denominators(hp)
                for u in range(2):
                    act.wait_ge(P_free, hp * (NB * 2 * NT) + ((NB * 2 - 1 + u) * NT + NP_BUF))
                    sources(hp + 1, u)
            pair_denominators(H // 2 - 1)

            def elu_exp(b):
                for k in range(KT):
                    act.wait_ge(min_ready, b * 4 + (k + 1))
                    fn(ebuf[:, k % 2, :], ebuf[:, k % 2, :], ACT.Exp).then_inc(exp_ready, 1)

            elu_exp(0)
            denominators(H // 2 * NB, 0)
            with act.Fori(1, NB) as b:
                elu_exp(b)
            act.wait_ge(small_in, 16 * 5)
            with act.Fori(0, NB // 2) as b2:
                for v in range(2):
                    b = b2 * 2 + v
                    for o in range(2):
                        act.wait_ge(z1_ps, b * 2 + (o + 1))
                        fn(z1T[:, o, ds(b * BLK, BLK)], ps[:, 4 + 2 * v + o, :], ACT.Relu,
                           bias=bcol[:, o:o + 1]).then_inc(z1_sb, 1)
            for b in range(NB):
                act.wait_ge(z2_ps, b + 1)
                fn(z2T[:, b * BLK:(b + 1) * BLK], ps[:, b % 2, :], ACT.Relu, bias=bcol[:, 2:3]).then_inc(z2_sb, 1)
            for b in range(NB):
                for o in range(2):
                    act.wait_ge(z3_ps, b * 2 + o + 1)
                    fn(z3T[:, o, b * BLK:(b + 1) * BLK], ps[:, 2 + 2 * (b % 2) + o, :], ACT.Relu,
                       bias=bcol[:, 3 + o:4 + o]).then_inc(z3_sb, 1)
            act.wait_ge(var_ready, NT)
            fn(rstd[:, :], var[:, :, 1], ACT.Ln, bias=cst[:, 0:1]).then_inc(ln_ready, 1)
            act.wait_ge(ln_ready, 1)
            fn(rstd[:, :], rstd[:, :], ACT.Exp, scale=-0.5).then_inc(rstd_ready, 1)
            with act.Fori(0, NT // 2) as t2:
                for u in range(2):
                    t = t2 * 2 + u
                    act.wait_ge(x1T_ps, t + 1)
                    nc.scalar.copy(x1T[u], ps[:, 2 + u, :]).then_inc(x1T_sb, 1)
                    nc.scalar.copy(xs[:, ds(t, 1), :], y[u]).then_inc(x1_kept, 1)
            act.wait_ge(sq_ready, 1)
            fn(glob[0:1, 2:3], glob[0:1, 2:3], ACT.Ln).then_inc(g1_ready, 1)
            act.wait_ge(g_all, 1)
            fn(glob[:, 5:6], ps[:, 3, 0:1], ACT.Exp, scale=0.5).then_inc(bound_ready, 1)
            act.wait_ge(beta_ready, 1)
            def guard_exp(c):
                act.wait_ge(e1_arg, c + 1)
                fn(e1[:, ds(c * (CH * H), CH * H)], e1[:, ds(c * (CH * H), CH * H)], ACT.Exp, scale=glob[:, 3:4],
                   bias=cst[:, 1:2]).then_inc(e1_ready, 1)

            def one_hots_kept(c):
                act.wait_ge(oh_used, c + 3)
                nc.scalar.copy(ObT[:, ds(c * CH, CH), :].rearrange("p t e -> p (t e)"),
                               ps[:, 2:4, :].rearrange("p b n -> p (b n)")).then_inc(obT_sb, 1)
            with act.Fori(0, CHUNKS - 1) as c:
                guard_exp(c)
                one_hots_kept(c)
            guard_exp(CHUNKS - 1)
            fn(unread[:, :], cst[:, 2:3], ACT.Ln).then_inc(table_in, 1)
            one_hots_kept(CHUNKS - 1)
            act.wait_ge(lse_arg, 1)
            fn(base, base, ACT.Ln).then_inc(lse_ready, 1)
            act.wait_ge(table_in, 1)
            fn(unread[:, :], cst[:, 2:3], ACT.Exp).then_inc(table_in, 1)
            act.wait_ge(m_ready, 1)
            fn(dterm, Z, ACT.Exp, scale=-1.0, bias=cst[:, 2:3]).then_inc(tabs_ready, 1)
            fn(base, Z, ACT.Exp, scale=-1.0).then_inc(tabs_ready, 1)
            act.wait_ge(p_arg, 1)
            fn(m_e, m_e, ACT.Exp).then_inc(p_exp, 1)
            act.wait_ge(c_ps, 1)
            nc.scalar.copy(c_row, ps[0:NT, 0, 0:P]).then_inc(c_row_ready, 1)
            def out_rstd(done, steps, part):
                act.wait_ge(o_var, done)
                fn(rstd[:, part], var[:, part, 1], ACT.Ln, bias=cst[:, 0:1]).then_inc(o_ln, 1)
                act.wait_ge(o_ln, steps)
                fn(rstd[:, part], rstd[:, part], ACT.Exp, scale=-0.5).then_inc(o_rstd, 1)

            def store(b, t):
                act.wait_ge(o_norm, b * 4 + (t + 1))
                act.dma_start(a["out"][ds((b * 4 + t) * P, P), :], o_buf[t]).then_inc(out_dma[t], 16)

            with act.Fori(0, NB - 1) as b:
                out_rstd(b * TI + TI, b + 1, slice(0, TI))
                for t in range(TI):
                    store(b, t)
            for t in range(TI):
                out_rstd((NB - 1) * TI + t + 1, NB + t, slice(t, t + 1))
                if t:
                    store(NB - 1, t - 1)
            store(NB - 1, TI - 1)

        @block.vector
        def _(dve):
            v = nc.vector
            own = [0]

            def own_step(ins):
                own[0] += 1
                ins.then_inc(dve_own, 1)
                dve.wait_ge(dve_own, own[0])

            dve.wait_ge(pairs_in, 16)
            dve.wait_ge(consts, 13)
            pv = pairs[:, :].rearrange("p (t c) -> p t c", c=2)
            v.tensor_copy(sub_i[:, :], pv[:, :, 0]).then_inc(dve_own, 1)
            v.tensor_copy(obj_i[:, :], pv[:, :, 1]).then_inc(dve_own, 1)
            v.tensor_copy(trash_f, eid[:, :]).then_inc(dve_own, 1)
            v.tensor_copy(sub_f, pv[:, :, 0]).then_inc(dve_own, 1)
            own[0] = 4
            own_step(v.tensor_copy(obj_f, pv[:, :, 1]))
            v.tensor_scalar(ok_f, trash_f, float(EDGES), None, ALU.is_lt).then_inc(dve_own, 1)
            own[0] += 1
            own_step(v.tensor_scalar(ft_f, obj_f, float(N), None, ALU.mult))
            own_step(v.tensor_tensor(ft_f, ft_f, sub_f, ALU.add))
            own_step(v.tensor_scalar(fn_f, sub_f, float(N), None, ALU.mult))
            v.tensor_tensor(fn_f, fn_f, obj_f, ALU.add).then_inc(fn_ready, 1)
            dve.wait_ge(fn_ready, 1)
            own_step(v.tensor_copy(fn_i[:, :], fn_f))
            own_step(v.tensor_scalar(trash_f, trash_f, float(TRASH), None, ALU.add))
            dve.wait_ge(wh_in, 16 * 6)
            for k in range(KT):
                for w in range(2):
                    own_step(v.tensor_tensor(wa_tmp, W_in[:, k, :], a_in[w], ALU.mult))
                    v.tensor_reduce(Wa[:, k, w * H:(w + 1) * H], wa_tmp.rearrange("p (h d) -> p h d", h=H),
                                    AX.X, ALU.add).then_inc(wa_ready, 1)
                    dve.wait_ge(wa_ready, 2 * k + w + 1)
            for t in range(ET):
                if t % (ET // 4) == 0:
                    dve.wait_ge(f_in[t // (ET // 4)], 16)
                own_step(v.scalar_tensor_tensor(out=junk0, in0=pair_rows[:, t * P:(t + 1) * P],
                                                scalar=fn_f[:, t:t + 1], in1=tri, op0=ALU.is_equal, op1=ALU.mult,
                                                accum_out=live[:, t:t + 1]))
            own_step(v.tensor_scalar(live, live, 0.5, None, ALU.is_lt))
            own_step(v.tensor_tensor(ok_f, ok_f, live, ALU.mult))
            own_step(v.tensor_tensor(live, fn_f, trash_f, ALU.subtract))
            own_step(v.tensor_tensor(live, live, ok_f, ALU.mult))
            own_step(v.tensor_tensor(live, live, trash_f, ALU.add))
            v.tensor_copy(tidx[:, :], live).then_inc(idx_ready, 1)
            def adj_copies(i, u):
                dve.wait_ge(adj_cast, i + (u + 1))
                dve.wait_ge(adj_dg, i + (u + 1))
                v.scalar_tensor_tensor(out=junk0, in0=adj_b[u].rearrange("p (j n) -> p j n", n=P)[:, ds(i + u, 1), :]
                                       .rearrange("p o n -> p (o n)"), scalar=1.0, in1=identb[:, :], op0=ALU.mult,
                                       op1=ALU.mult, accum_out=adj_diag[:, ds(i + u, 1)]).then_inc(adj_dg, 1)
                dve.wait_ge(adj_ps, (i + u) * 2 + 1)
                v.tensor_copy(adjT[:, 0:8, ds((i + u) * P, P)],
                              psb[:, 0, :].rearrange("p (j n) -> p j n", n=P)).then_inc(adj_sb0, 1)

            with dve.Fori(0, NT // 4) as i_:
                for u in range(2):
                    adj_copies(i_ * 2, u)
            dve.wait_ge(rows_sb, 8)
            own_step(v.tensor_reduce(d_lim[:, 0:1], d_row, AX.X, ALU.max))
            own_step(v.tensor_reduce(d_lim[:, 1:2], d_row, AX.X, ALU.min))
            own_step(v.tensor_tensor(d_lim[:, 2:3], d_lim[:, 0:1], d_lim[:, 1:2], ALU.subtract))
            v.tensor_scalar(d_diag[:, :], ident[0:H, 0:H], d_lim[:, 0:1], None, ALU.mult).then_inc(d_ready, 1)
            dve.wait_ge(d_ps, 1)
            v.tensor_tensor(e_col[:, :, H:2 * H], e_col[:, :, H:2 * H],
                            ps[:, 6, 0:H].unsqueeze(1).broadcast_to([P, NT, H]), ALU.subtract).then_inc(shift_ready, 1)
            own_step(v.tensor_scalar(s_row, s_row, d_lim[:, 0:1], 0.0, ALU.add, ALU.max))
            v.tensor_scalar(s_row, s_row, d_lim[:, 2:3], None, ALU.min).then_inc(r_arg, 1)
            dve.wait_ge(ed_ready, 2)
            with dve.Fori(NT // 4, NT // 2) as i_:
                for u in range(2):
                    adj_copies(i_ * 2, u)
                    for k in range(2):
                        j = i_ * 4 + (2 * u + k - NT)
                        v.tensor_tensor(U[:, ds(j, 1), :, :].rearrange("p o h d -> p (o h) d"),
                                        U[:, ds(j, 1), :, :].rearrange("p o h d -> p (o h) d"),
                                        ED[:, ds(j, 1), :].rearrange("p o h -> p (o h)").unsqueeze(2).broadcast_to([P, H, DH]),
                                        ALU.mult).then_inc(u_ready, 1)
            dve.wait_ge(bqk_in, 32)
            dve.wait_ge(bank_set, 1)

            def divide(m, w, step):
                if step == 0:
                    dve.wait_ge(den_ready, m * 2 + 2)
                if step < 4:
                    part = slice(step * P, (step + 1) * P)
                    v.reciprocal(den[:, part], den[:, part]).then_inc(rden_ready, 1)
                else:
                    u = step - 4
                    rows = slice(u * DH, (u + 1) * DH)
                    dve.wait_ge(rden_ready, m * 4 + 4)
                    v.tensor_tensor(enc_all[rows, ds(m * BLK, BLK)], ps[rows, 2 * (1 - w) + u, :], den[rows, :],
                                     ALU.mult).then_inc(att_ev, 1)

            at_slot = {7: 0, 11: 1, 15: 2, 19: 3, 23: 4, 27: 5}
            with dve.Fori(0, H // 2) as hp:
                with dve.Fori(0, NB // 2) as b2:
                    for w in range(2):
                        b = b2 * 2 + w
                        m = hp * NB + b
                        for u in range(2):
                            dve.wait_ge(r_in[u], m * 16 + 16)
                            for j in range(NT):
                                if u * NT + j in at_slot:
                                    divide(m, w, at_slot[u * NT + j])
                                dve.wait_ge(P_free, m * (2 * NT) + (u * NT + j + 1))
                                v.scalar_tensor_tensor(out=Pw[j % NP_BUF], in0=r_b[u],
                                                        scalar=q_col[:, j, ds(hp * 2 + u, 1)],
                                                        in1=adjT[:, j, ds(b * BLK, BLK)], op0=ALU.max,
                                                        op1=ALU.mult).then_inc(P_ready, 1)
            def elu(b):
                for k in range(KT):
                    dve.wait_ge(enc_ready, b * 4 + (k + 1))
                    v.tensor_scalar(ebuf[:, k % 2, :], encT[:, k, ds(b * BLK, BLK)], 0.0, None, ALU.min).then_inc(min_ready, 1)
                    if k % 2:
                        for kk in (k - 1, k):
                            dve.wait_ge(exp_ready, b * 4 + (kk + 1))
                            v.scalar_tensor_tensor(out=encT[:, kk, ds(b * BLK, BLK)], in0=ebuf[:, kk % 2, :], scalar=-1.0,
                                                   in1=encT[:, kk, ds(b * BLK, BLK)], op0=ALU.add,
                                                   op1=ALU.max).then_inc(enc_ready, 1)

            dve.wait_ge(att_ev, 2 * (H // 2 * NB) + 1)
            dve.wait_ge(P_ready, NB * H * NT)
            with dve.Fori(0, NB - 1) as b:
                elu(b)
            for step in range(6):
                divide(H // 2 * NB, 0, step)
            dve.wait_ge(att_ev, NB * H + 3)
            elu(NB - 1)
            dve.wait_ge(b4_in_s, 16)
            dve.wait_ge(x_res_in, 16)
            v.tensor_tensor(xs, xs, b4_row[:, :].unsqueeze(1).broadcast_to([P, NT, F]), ALU.add).then_inc(b4_added, 1)
            dve.wait_ge(b4_added, 1)
            for t in range(NT):
                dve.wait_ge(z4_ps, t + 1)
                v.tensor_tensor(xs[:, t, :], ps[:, 6 + t % 2, :], xs[:, t, :], ALU.add).then_inc(y_ready, 1)
                dve.wait_ge(y_ready, t + 1)
                v.bn_stats(stats[:, t, :], xs[:, t, :]).then_inc(st_ready, 1)
            for t in range(NT):
                dve.wait_ge(st_ready, t + 1)
                v.bn_aggr(var[:, t, :], stats[:, t, :]).then_inc(var_ready, 1)
            dve.wait_ge(rstd_ready, 1)
            def normalised(t, u):
                dve.wait_ge(x1_kept, t + 1)
                v.tensor_scalar(y[u], xs[:, ds(t, 1), :].rearrange("p o n -> p (o n)"),
                                var[:, ds(t, 1), 0:1].rearrange("p o n -> p (o n)"),
                                rstd[:, ds(t, 1)], ALU.subtract, ALU.mult).then_inc(x1_ready, 1)

            def q_and_k_biased(t):
                for w in range(2):
                    dve.wait_ge(qk_ps, t * 2 + (w + 1))
                    dve.wait_ge(qk_dma[w], t * 16 + 16)
                    v.tensor_tensor(qk_out[w], ps[:, 4 + w, :], bqk[:, w, :], ALU.add).then_inc(qk_sb, 1)
                    dve.wait_ge(qk_sb, t * 2 + (w + 3))
                    v.tensor_tensor(prod[w], qk_out[w], qk_out[w], ALU.mult).then_inc(sq_done, 1)
                    dve.wait_ge(sq_done, t * 2 + (w + 1))
                    v.tensor_reduce(norms[:, w, ds(t * H, H)], prod[w].rearrange("p (h d) -> p h d", h=H), AX.X,
                                    ALU.add).then_inc(norm_done, 1)

            for u in range(2):
                normalised(u, u)
            with dve.Fori(0, NT // 2 - 1) as t2:
                for u in range(2):
                    q_and_k_biased(t2 * 2 + u)
                    normalised(t2 * 2 + (u + 2), u)
            for t in (NT - 2, NT - 1):
                q_and_k_biased(t)

            dve.wait_ge(norm_done, 2 * NT)
            for w in range(2):
                v.tensor_reduce(glob[:, w:w + 1], norms[:, w, :], AX.X, ALU.max).then_inc(gm_ready, 1)
            dve.wait_ge(gm_ps, 1)
            for w in range(2):
                own_step(v.tensor_reduce(glob[0:1, 3 + w:4 + w], ps[0:1, 2, w * P:(w + 1) * P], AX.X, ALU.max))
            own_step(v.tensor_scalar(glob[0:1, 3:5], glob[0:1, 3:5], 1.0 / 8.0, 1e9, ALU.mult, ALU.min))
            own_step(v.tensor_tensor(glob[0:1, 2:3], glob[0:1, 3:4], glob[0:1, 4:5], ALU.mult))
            v.tensor_scalar(glob[0:1, 2:3], glob[0:1, 2:3], 1.0, None, ALU.max).then_inc(sq_ready, 1)
            dve.wait_ge(bound_ready, 1)
            own_step(v.tensor_scalar(glob[:, 4:5], glob[:, 5:6], 1.0 / SPAN, None, ALU.mult))
            v.reciprocal(glob[:, 3:4], glob[:, 4:5]).then_inc(beta_ready, 1)
            dve.wait_ge(t_in, 16 * ET)
            dve.wait_ge(aj_in, 16 * ET)
            dve.wait_ge(x1_kept, NT + 2)
            own_step(v.tensor_tensor(live, t_got[:, :], eid[:, :], ALU.is_equal))
            own_step(v.tensor_tensor(live, live, ok_f, ALU.mult))
            own_step(v.tensor_tensor(ok_f, sub_f, obj_f, ALU.not_equal))
            own_step(v.tensor_tensor(live, live, ok_f, ALU.mult))
            own_step(v.tensor_scalar(ok_f, adj_got, 1.0, None, ALU.is_equal))
            own_step(v.tensor_tensor(live, live, ok_f, ALU.mult))
            own_step(v.tensor_tensor(ft_f, ft_f, trash_f, ALU.subtract))
            own_step(v.tensor_tensor(ft_f, ft_f, live, ALU.mult))
            own_step(v.tensor_tensor(ft_f, ft_f, trash_f, ALU.add))
            v.tensor_copy(didx[:, :], ft_f).then_inc(didx_ready, 1)
            own_step(v.tensor_scalar(t_got[:, :], sub_i[:, :], 7, None, ALU.logical_shift_right))
            own_step(v.tensor_copy(a_f, t_got[:, :]))
            own_step(v.scalar_tensor_tensor(out=b_f, in0=a_f, scalar=-float(P), in1=sub_f, op0=ALU.mult, op1=ALU.add))
            own_step(v.tensor_tensor(Oa, biota[:, 0:NT].unsqueeze(1).broadcast_to([P, ET, NT]),
                                     a_f.unsqueeze(2).broadcast_to([P, ET, NT]), ALU.is_equal))
            e1v = e1.rearrange("p (t h) -> p t h", h=H)

            def one_hot(c, u, vals, nh):
                one_hot_b(c, u)
                weighted(c, u, vals, nh).then_inc(oh_ready, 1)

            def one_hot_b(c, u):
                one_hot_into(Ob[u], c)

            def one_hot_into(place, c):
                v.tensor_tensor(place, biota[:, :].unsqueeze(1).broadcast_to([P, CH, P]),
                                b_f[:, ds(c * CH, CH)].unsqueeze(2).broadcast_to([P, CH, P]),
                                ALU.is_equal).then_inc(oh_ready, 1)

            def weighted(c, u, vals, nh):
                return v.tensor_tensor(Wc[u][:, 0:CH * NT * nh].rearrange("p (t k h) -> p t k h", t=CH, k=NT),
                                       vals[:, ds(c * CH, CH), :].unsqueeze(2).broadcast_to([P, CH, NT, nh]),
                                       Oa[:, ds(c * CH, CH), :].unsqueeze(3).broadcast_to([P, CH, NT, nh]), ALU.mult)

            def scores(c, before):
                for k in range(CH):
                    u = k % RING
                    dve.wait_ge(k_in[u], c * (16 * CH // RING) + 16 * (k // RING + 1))
                    dve.wait_ge(q_in[u], c * (16 * CH // RING) + 16 * (k // RING + 1))
                    v.tensor_tensor(prod[k % 2], k_rows[u], q_rows[u], ALU.mult).then_inc(prod_ready, 1)
                    dve.wait_ge(prod_ready, c * CH + (k + 1))
                    v.tensor_reduce(att[:, ds(c * CH + k, 1), :].rearrange("p o h -> p (o h)"),
                                    prod[k % 2].rearrange("p (h d) -> p h d", h=H), AX.X, ALU.add).then_inc(rows_used, 1)
                    if before and k == 2:
                        dve.wait_ge(oh_used, c + 1)
                        one_hot_b(c - 1, 0)
                    if before and k == 4:
                        dve.wait_ge(e1_ready, c)
                        weighted(c - 1, 0, e1v, H).then_inc(oh_ready, 1)
                dve.wait_ge(rows_used, c * CH + CH)
                v.scalar_tensor_tensor(out=att[:, ds(c * CH, CH), :], in0=att[:, ds(c * CH, CH), :],
                                       scalar=1.0 / float(DH) ** 0.5,
                                       in1=live[:, ds(c * CH, CH)].unsqueeze(2).broadcast_to([P, CH, H]), op0=ALU.mult,
                                       op1=ALU.mult).then_inc(scaled, 1)
                dve.wait_ge(scaled, c + 1)
                v.tensor_scalar(e1[:, ds(c * (CH * H), CH * H)], att_f[:, ds(c * (CH * H), CH * H)], 0.0, None,
                                ALU.max).then_inc(e1_arg, 1)

            scores(0, False)
            with dve.Fori(1, CHUNKS) as c:
                scores(c, True)
            dve.wait_ge(oh_used, CHUNKS + 1)
            one_hot_b(CHUNKS - 1, 0)
            dve.wait_ge(e1_ready, CHUNKS)
            weighted(CHUNKS - 1, 0, e1v, H).then_inc(oh_ready, 1)
            for c in range(EARLY):
                one_hot_into(Ob_early[c], c)
            dve.wait_ge(oh_used, 2 + CHUNKS)
            v.tensor_scalar(base, ps[:, 0, 0:P], float(2.718281828459045 ** LOW), None, ALU.add).then_inc(lse_arg, 1)
            dve.wait_ge(lse_ready, 1)
            own_step(v.tensor_scalar(Z, base, -LOW, glob[:, 4:5], ALU.add, ALU.mult))
            own_step(v.tensor_copy(m_b, Z))
            v.tensor_copy(Z, m_b).then_inc(m_ready, 1)
            with dve.Fori(0, CHUNKS // 2) as c_:
                c = c_ * 2
                for u in range(2):
                    dve.wait_ge(mg_ps, c + (u + 1))
                    m_prod = Wc[u][:, 0:CH * P]
                    v.tensor_tensor(m_prod.rearrange("p (t k h) -> p t k h", t=CH, k=NT),
                                    ps[:, 2 + 2 * u:4 + 2 * u, :].rearrange("p b n -> p (b n)").rearrange(
                                        "p (t k h) -> p t k h", t=CH, k=NT),
                                    Oa[:, ds((c + u) * CH, CH), :].unsqueeze(3).broadcast_to([P, CH, NT, H]),
                                    ALU.mult).then_inc(mg_sb, 1)
                    dve.wait_ge(mg_sb, c + (u + 3))
                    v.tensor_reduce(m_e.rearrange("p (t h) -> p t h", h=H)[:, ds((c + u) * CH, CH), :],
                                    m_prod.rearrange("p (t k h) -> p t h k", t=CH, k=NT), AX.X, ALU.add).then_inc(m_e_ready, 1)
            dve.wait_ge(m_e_ready, CHUNKS)
            v.tensor_tensor(m_e, att_f, m_e, ALU.subtract).then_inc(p_arg, 1)
            dve.wait_ge(p_exp, 1)
            own_step(v.tensor_tensor(p9[:, :, 0:H], m_e.rearrange("p (t h) -> p t h", h=H),
                                     live.unsqueeze(2).broadcast_to([P, ET, H]), ALU.mult))
            own_step(v.tensor_copy(p9[:, :, H], live))
            for c in range(EARLY):
                dve.wait_ge(oh_used, CHUNKS + c + 1)
                weighted(c, c % 2, p9, 9).then_inc(oh_ready, 1)
            with dve.Fori(EARLY // 2, CHUNKS // 2) as c_:
                c = c_ * 2
                for u in range(2):
                    dve.wait_ge(oh_used, CHUNKS + (c + u) + 1)
                    one_hot(c + u, u, p9, 9)
            dve.wait_ge(oh_used, 2 + 2 * CHUNKS)
            dve.wait_ge(tabs_ready, 2)
            own_step(v.tensor_copy(seg, ps[:, 1, 0:144].rearrange("p (t h) -> p t h", h=9)))
            own_step(v.tensor_tensor(n_col, adj_sum[:, :], adj_diag[:, :], ALU.subtract))
            own_step(v.tensor_tensor(n_col, n_col, seg[:, :, H], ALU.subtract))
            b3, d3, z3 = (w.rearrange("p (t h) -> p t h", h=H) for w in (base, dterm, Z))
            own_step(v.tensor_tensor(z3, b3, n_col.unsqueeze(2).broadcast_to([P, NT, H]), ALU.mult))
            own_step(v.tensor_tensor(z3, z3, seg[:, :, 0:H], ALU.add))
            own_step(v.tensor_tensor(z3, z3, d3, ALU.add))
            own_step(v.reciprocal(Z, Z))
            own_step(v.tensor_scalar(T9[:, :, 0:H], z3, 1.0 / H, None, ALU.mult))
            own_step(v.tensor_tensor(b3, b3, T9[:, :, 0:H], ALU.mult))
            own_step(v.tensor_tensor(d3, d3, T9[:, :, 0:H], ALU.mult))
            v.tensor_reduce(c_col, b3, AX.X, ALU.add).then_inc(c_ready, 1)
            own_step(v.tensor_reduce(cd_col, d3, AX.X, ALU.add))
            dve.wait_ge(c_ready, 1)
            own_step(v.tensor_scalar(T9[:, :, H], c_col, -1.0, None, ALU.mult))
            own_step(v.tensor_tensor(n_col, c_col, adj_diag[:, :], ALU.mult))
            own_step(v.tensor_tensor(cd_col, cd_col, n_col, ALU.subtract))
            own_step(v.tensor_scalar(dcoef, cd_col, 1.0, None, ALU.add))
            own_step(v.tensor_copy(Tb[0], T9f))
            own_step(v.tensor_tensor(T_tmp, T9f, Tb[0], ALU.subtract))
            own_step(v.tensor_copy(Tb[1], T_tmp))
            own_step(v.tensor_tensor(T_tmp, T_tmp, Tb[1], ALU.subtract))
            v.tensor_copy(Tb[2], T_tmp).then_inc(t9_ready, 1)
            with dve.Fori(0, CHUNKS // 2) as c_:
                c = c_ * 2
                for u in range(2):
                    weighted(c + u, u, p9, 9).then_inc(w_ready, 1)
                    dve.wait_ge(w_ready, c + (u + 1))
                    dve.wait_ge(g9_ps, c + (u + 1))
                    for k in range(CH):
                        last = v.tensor_tensor_reduce(Wc[u][:, k * 144:(k + 1) * 144], ps[:, 2 + 3 * u + k // 3, (k % 3) * 144:(k % 3 + 1) * 144],
                                                      Wc[u][:, k * 144:(k + 1) * 144], 1.0, 0.0, ALU.mult, ALU.add,
                                                      v_part[:, k:k + 1])
                        last.then_inc(v_sum, 1)
                    dve.wait_ge(v_sum, (c + u) * CH + CH)
                    v.tensor_copy(v_e[:, ds((c + u) * CH, CH)], v_part).then_inc(v_ready, 1)
            dve.wait_ge(c_in, 16)
            def aggregator(b, jq):
                for u in range(4):
                    n = b * NT + jq * 4 + u
                    dve.wait_ge(A_free, n + 1)
                    v.tensor_tensor(A[u], adjT[:, ds(jq * 4 + u, 1), ds(b * BLK, BLK)].rearrange("p o n -> p (o n)"),
                                    c_b[:, ds(b * BLK, BLK)], ALU.mult).then_inc(A_tmp, 1)
                    dve.wait_ge(A_tmp, n + 1)
                    dve.wait_ge(d_slot[u], b * 64 + jq * 16 + 16)
                    v.tensor_tensor(A[u], A[u], d_in[u], ALU.add).then_inc(A_ready, 1)

            def output_tile(b, t):
                dve.wait_ge(out_dma[t], b * 16 + 16)
                v.scalar_tensor_tensor(out=o_buf[t], in0=xs[:, b * 4 + t, :], scalar=dcoef[:, b * 4 + t:b * 4 + t + 1],
                                       in1=ps[:, 4 * (b % 2) + t, :], op0=ALU.mult, op1=ALU.add).then_inc(o_ev, 1)
                dve.wait_ge(o_ev, b * 4 + (t + 9))
                v.bn_stats(stats[:, t, :], o_buf[t]).then_inc(o_st, 1)

            def normalise(t):
                v.tensor_scalar(o_buf[t], o_buf[t], var[:, t, 0:1], rstd[:, t:t + 1], ALU.subtract,
                                ALU.mult).then_inc(o_norm, 1)

            def finish(b):
                dve.wait_ge(A_free, b * NT + (NT + 4))
                for t in range(TI):
                    output_tile(b, t)
                dve.wait_ge(o_st, b * 4 + 4)
                v.memset(carrier[:, :], 0.0)
                for t in range(TI):
                    v.bn_aggr(var[:, t, :], stats[:, t, :]).then_inc(o_var, 1)
                for t in range(TI):
                    dve.wait_ge(o_rstd, b + 1)
                    normalise(t)

            aggregator(0, 0)
            for b in range(NB - 1):
                with dve.Fori(1, NT // 4) as jq:
                    aggregator(b, jq)
                aggregator(b + 1, 0)
                finish(b)
            with dve.Fori(1, NT // 4) as jq:
                aggregator(NB - 1, jq)
            for t in range(TI):
                dve.wait_ge(o_ps, t + 1)
                output_tile(NB - 1, t)
                dve.wait_ge(o_st, (NB - 1) * TI + t + 1)
                v.bn_aggr(var[:, t, :], stats[:, t, :]).then_inc(o_var, 1)
                if t:
                    dve.wait_ge(o_rstd, NB - 1 + t)
                    normalise(t - 1)
            dve.wait_ge(o_rstd, NB - 1 + TI)
            normalise(TI - 1)


_INS = {"x": "x", "adj": "adj", "W": "L0_gnn_W", "a1": "L0_gnn_a1", "a2": "L0_gnn_a2",
        "W1": "L0_gnn_W1", "b1": "L0_gnn_b1", "W2": "L0_gnn_W2", "b2": "L0_gnn_b2", "W3": "L0_gnn_W3",
        "b3": "L0_gnn_b3", "W4": "L0_gnn_W4", "b4": "L0_gnn_b4", "pairs": "L1_gnn_rel_pair_index",
        "Wq": "L1_gnn_Wq", "bq": "L1_gnn_bq", "Wk": "L1_gnn_Wk", "bk": "L1_gnn_bk"}


def kernel(**inputs):
    import numpy as _np
    import concourse.bacc as _bacc
    from concourse import mybir as _mybir
    from concourse.bass_utils import run_bass_kernel_spmd as _run

    nc = _bacc.Bacc("TRN2", target_bir_lowering=False, num_devices=1)
    arrays, args = {}, {}
    for short, name in _INS.items():
        arr = _np.ascontiguousarray(inputs[name])
        arrays[f"in_{short}"] = arr
        args[short] = nc.dram_tensor(f"in_{short}", arr.shape, _mybir.dt.from_np(arr.dtype), kind="ExternalInput").ap()
    args["out"] = nc.dram_tensor("out_0", (N, F), F32, kind="ExternalOutput").ap()
    build(nc, args)
    r = _run(nc, [arrays], core_ids=[0])
    return r.results[0]["out_0"]
```
